# Optimizing a Trainium2 kernel written in Bass

```python
import numpy as np
import jax
import jax.numpy as jnp

def _softmax(x, axis=-1):
    return jax.nn.softmax(x, axis=axis)

def _gelu(x):
    return jax.nn.gelu(x, approximate=True)

def _silu(x):
    return jax.nn.silu(x)

def _sigmoid(x):
    return jax.nn.sigmoid(x)

def _layernorm(x, axis=-1, eps=1e-05):
    m = jnp.mean(x, axis=axis, keepdims=True)
    v = jnp.var(x, axis=axis, keepdims=True)
    return (x - m) / jnp.sqrt(v + eps)

def _scatter_add(tgt, idx, src, axis=0):
    return tgt.at[idx].add(src)

def _segment_sum(src, seg, n):
    return jax.ops.segment_sum(src, seg, n)
kernel_name = 'mk_pixart_seq_d1_seqx_r4_af85eb'

def setup_inputs(seed: int=0):
    np.random.seed(seed)
    _w = jnp.asarray

    def _rec_inputs():
        import jax
        import jax.numpy as jnp
        _rk = jax.random.key(seed)
        x = 7.22e-05 + 1 * jax.random.normal(jax.random.fold_in(_rk, 1), (4, 512, 256), jnp.float32)
        _lenS = 512 - jax.random.randint(jax.random.fold_in(_rk, 7), (4,), 0, max(1, 512 // 4) + 1, jnp.int32)
        _lenS2 = 1601 - jax.random.randint(jax.random.fold_in(_rk, 8), (4,), 0, max(1, 1601 // 4) + 1, jnp.int32)
        cond_1024 = 0.000887014 + 1.03683 * jax.random.normal(jax.random.fold_in(_rk, 11), (4, 256), jnp.float32)
        _ctx_1024P = jax.random.normal(jax.random.fold_in(_rk, 12), (4, 16, 256), jnp.float32)
        _ctx_1024c = jax.random.dirichlet(jax.random.fold_in(_rk, 512), 0.3 * jnp.ones((16,), jnp.float32), (4, 1601))
        _ctx_1024t = jnp.einsum('bsk,bkd->bsd', _ctx_1024c, _ctx_1024P)
        _ctx_1024t = _ctx_1024t * jax.lax.rsqrt(jnp.mean(jnp.square(_ctx_1024t)) + 1e-12) * 0.953939
        ctx_1024 = 0.00086875 + 0.999764 * (_ctx_1024t + 0.3 * jax.random.normal(jax.random.fold_in(_rk, 612), (4, 1601, 256), jnp.float32))
        return (x, cond_1024, ctx_1024)
    x, cond_1024, ctx_1024 = _rec_inputs()

    def _L0_xcond_setup():
        import jax, jax.numpy as jnp
        import numpy as np
        C = 256
        H = 16
        D = C // H
        WIN = 128
        SHIFT = 64
        TOPK = 16
        HID = 1024
        EPS = 1e-06

        def _ln(x):
            x32 = x.astype(jnp.float32)
            m = x32.mean(-1, keepdims=True)
            v = jnp.mean((x32 - m) ** 2, axis=-1, keepdims=True)
            return ((x32 - m) * jax.lax.rsqrt(v + EPS)).astype(x.dtype)

        def _self_attn(h, w_qkv, b_qkv, w_so, b_so):
            B, L, _ = h.shape
            qkv = h @ w_qkv + b_qkv
            qkv = jnp.roll(qkv, -SHIFT, axis=1)
            nw = L // WIN
            qkv = qkv.reshape(B, nw, WIN, 3, H, D)
            q, k, v = (qkv[:, :, :, 0], qkv[:, :, :, 1], qkv[:, :, :, 2])
            scores = jnp.einsum('bnqhd,bnkhd->bnhqk', q, k) / jnp.sqrt(jnp.float32(D)).astype(h.dtype)
            attn = jax.nn.softmax(scores, axis=-1)
            o = jnp.einsum('bnhqk,bnkhd->bnqhd', attn, v).reshape(B, L, C)
            o = jnp.roll(o, SHIFT, axis=1)
            return o @ w_so + b_so

        def _topk_cross_attn(h, ctx, w_q, b_q, w_kv, b_kv, w_co, b_co):
            B, L, _ = h.shape
            Lc = ctx.shape[1]
            q = (h @ w_q + b_q).reshape(B, L, H, D)
            kv = (ctx @ w_kv + b_kv).reshape(B, Lc, 2, H, D)
            k, v = (kv[:, :, 0], kv[:, :, 1])
            scores = jnp.einsum('bqhd,bkhd->bhqk', q, k) / jnp.sqrt(jnp.float32(D)).astype(h.dtype)
            top_s, top_i = jax.lax.top_k(scores, TOPK)
            attn = jax.nn.softmax(top_s, axis=-1)
            v_bh = jnp.transpose(v, (0, 2, 1, 3))
            vg = jnp.take_along_axis(v_bh[:, :, None, :, :], top_i[..., None], axis=3)
            o = jnp.einsum('bhqk,bhqkd->bqhd', attn, vg).reshape(B, L, C)
            return o @ w_co + b_co

        def _swiglu(h, w_m1, b_m1, w_m2, b_m2):
            u = h @ w_m1 + b_m1
            a, b = (u[..., :HID], u[..., HID:])
            return jax.nn.silu(a) * b @ w_m2 + b_m2
        key = jax.random.key(seed)
        ks = jax.random.split(key, 24)
        s = 0.02
        inp = {'x': jax.random.normal(ks[0], (2, 1024, C), jnp.float32), 'mod': jax.random.normal(ks[1], (2, C), jnp.float32), 'context': jax.random.normal(ks[2], (2, 256, C), jnp.float32), 'w_ada': jax.random.normal(ks[3], (C, 9 * C), jnp.float32) * s, 'b_ada': jnp.zeros((9 * C,), jnp.float32), 'w_qkv': jax.random.normal(ks[4], (C, 3 * C), jnp.float32) * s, 'b_qkv': jnp.zeros((3 * C,), jnp.float32), 'w_so': jax.random.normal(ks[5], (C, C), jnp.float32) * s, 'b_so': jnp.zeros((C,), jnp.float32), 'w_q': jax.random.normal(ks[6], (C, C), jnp.float32) * s, 'b_q': jnp.zeros((C,), jnp.float32), 'w_kv': jax.random.normal(ks[7], (C, 2 * C), jnp.float32) * s, 'b_kv': jnp.zeros((2 * C,), jnp.float32), 'w_co': jax.random.normal(ks[8], (C, C), jnp.float32) * s, 'b_co': jnp.zeros((C,), jnp.float32), 'w_m1': jax.random.normal(ks[9], (C, 2 * HID), jnp.float32) * s, 'b_m1': jnp.zeros((2 * HID,), jnp.float32), 'w_m2': jax.random.normal(ks[10], (HID, C), jnp.float32) * s, 'b_m2': jnp.zeros((C,), jnp.float32)}
        return inp
    _L0_xcond_all = _L0_xcond_setup()
    _L0_xcond_in = {k: v for k, v in _L0_xcond_all.items() if k in ('w_ada', 'b_ada', 'w_qkv', 'b_qkv', 'w_so', 'b_so', 'w_q', 'b_q', 'w_kv', 'b_kv', 'w_co', 'b_co', 'w_m1', 'b_m1', 'w_m2', 'b_m2')}
    del _L0_xcond_all
    return {'x': x, 'cond_1024': cond_1024, 'ctx_1024': ctx_1024, 'L0_xcond_w_ada': _L0_xcond_in['w_ada'], 'L0_xcond_b_ada': _L0_xcond_in['b_ada'], 'L0_xcond_w_qkv': _L0_xcond_in['w_qkv'], 'L0_xcond_b_qkv': _L0_xcond_in['b_qkv'], 'L0_xcond_w_so': _L0_xcond_in['w_so'], 'L0_xcond_b_so': _L0_xcond_in['b_so'], 'L0_xcond_w_q': _L0_xcond_in['w_q'], 'L0_xcond_b_q': _L0_xcond_in['b_q'], 'L0_xcond_w_kv': _L0_xcond_in['w_kv'], 'L0_xcond_b_kv': _L0_xcond_in['b_kv'], 'L0_xcond_w_co': _L0_xcond_in['w_co'], 'L0_xcond_b_co': _L0_xcond_in['b_co'], 'L0_xcond_w_m1': _L0_xcond_in['w_m1'], 'L0_xcond_b_m1': _L0_xcond_in['b_m1'], 'L0_xcond_w_m2': _L0_xcond_in['w_m2'], 'L0_xcond_b_m2': _L0_xcond_in['b_m2']}

def reference(x, cond_1024, ctx_1024, L0_xcond_w_ada, L0_xcond_b_ada, L0_xcond_w_qkv, L0_xcond_b_qkv, L0_xcond_w_so, L0_xcond_b_so, L0_xcond_w_q, L0_xcond_b_q, L0_xcond_w_kv, L0_xcond_b_kv, L0_xcond_w_co, L0_xcond_b_co, L0_xcond_w_m1, L0_xcond_b_m1, L0_xcond_w_m2, L0_xcond_b_m2):
    import jax
    import jax.numpy as jnp

    def _L0_xcond_ref(x, mod, context, w_ada, b_ada, w_qkv, b_qkv, w_so, b_so, w_q, b_q, w_kv, b_kv, w_co, b_co, w_m1, b_m1, w_m2, b_m2):
        import jax, jax.numpy as jnp
        import numpy as np
        C = 256
        H = 16
        D = C // H
        WIN = 128
        SHIFT = 64
        TOPK = 16
        HID = 1024
        EPS = 1e-06

        def _ln(x):
            x32 = x.astype(jnp.float32)
            m = x32.mean(-1, keepdims=True)
            v = jnp.mean((x32 - m) ** 2, axis=-1, keepdims=True)
            return ((x32 - m) * jax.lax.rsqrt(v + EPS)).astype(x.dtype)

        def _self_attn(h, w_qkv, b_qkv, w_so, b_so):
            B, L, _ = h.shape
            qkv = h @ w_qkv + b_qkv
            qkv = jnp.roll(qkv, -SHIFT, axis=1)
            nw = L // WIN
            qkv = qkv.reshape(B, nw, WIN, 3, H, D)
            q, k, v = (qkv[:, :, :, 0], qkv[:, :, :, 1], qkv[:, :, :, 2])
            scores = jnp.einsum('bnqhd,bnkhd->bnhqk', q, k) / jnp.sqrt(jnp.float32(D)).astype(h.dtype)
            attn = jax.nn.softmax(scores, axis=-1)
            o = jnp.einsum('bnhqk,bnkhd->bnqhd', attn, v).reshape(B, L, C)
            o = jnp.roll(o, SHIFT, axis=1)
            return o @ w_so + b_so

        def _topk_cross_attn(h, ctx, w_q, b_q, w_kv, b_kv, w_co, b_co):
            B, L, _ = h.shape
            Lc = ctx.shape[1]
            q = (h @ w_q + b_q).reshape(B, L, H, D)
            kv = (ctx @ w_kv + b_kv).reshape(B, Lc, 2, H, D)
            k, v = (kv[:, :, 0], kv[:, :, 1])
            scores = jnp.einsum('bqhd,bkhd->bhqk', q, k) / jnp.sqrt(jnp.float32(D)).astype(h.dtype)
            top_s, top_i = jax.lax.top_k(scores, TOPK)
            attn = jax.nn.softmax(top_s, axis=-1)
            v_bh = jnp.transpose(v, (0, 2, 1, 3))
            vg = jnp.take_along_axis(v_bh[:, :, None, :, :], top_i[..., None], axis=3)
            o = jnp.einsum('bhqk,bhqkd->bqhd', attn, vg).reshape(B, L, C)
            return o @ w_co + b_co

        def _swiglu(h, w_m1, b_m1, w_m2, b_m2):
            u = h @ w_m1 + b_m1
            a, b = (u[..., :HID], u[..., HID:])
            return jax.nn.silu(a) * b @ w_m2 + b_m2
        m = jax.nn.silu(mod) @ w_ada + b_ada
        sh_msa, sc_msa, g_msa, sh_mca, sc_mca, g_mca, sh_mlp, sc_mlp, g_mlp = [m[:, i * C:(i + 1) * C][:, None, :] for i in range(9)]
        h = _ln(x) * (1 + sc_msa) + sh_msa
        h = _self_attn(h, w_qkv, b_qkv, w_so, b_so)
        x = x + h * g_msa
        h = _ln(x) * (1 + sc_mca) + sh_mca
        h = _topk_cross_attn(h, context, w_q, b_q, w_kv, b_kv, w_co, b_co)
        x = x + h * g_mca
        h = _ln(x) * (1 + sc_mlp) + sh_mlp
        h = _swiglu(h, w_m1, b_m1, w_m2, b_m2)
        x = x + h * g_mlp
        return x
    x = _L0_xcond_ref(x, cond_1024, ctx_1024, L0_xcond_w_ada, L0_xcond_b_ada, L0_xcond_w_qkv, L0_xcond_b_qkv, L0_xcond_w_so, L0_xcond_b_so, L0_xcond_w_q, L0_xcond_b_q, L0_xcond_w_kv, L0_xcond_b_kv, L0_xcond_w_co, L0_xcond_b_co, L0_xcond_w_m1, L0_xcond_b_m1, L0_xcond_w_m2, L0_xcond_b_m2)
    return x

_drawn_inputs = setup_inputs


def setup_inputs(seed=0):
    import zlib

    import numpy as np

    out = dict(_drawn_inputs(seed))
    spreads = {'L0_xcond_b_ada': (0.0, 0.366),
     'L0_xcond_b_qkv': (0.0, 0.8),
     'L0_xcond_b_so': (0.0, 0.372),
     'L0_xcond_b_q': (0.0, 0.8),
     'L0_xcond_b_kv': (0.0, 0.8),
     'L0_xcond_b_co': (0.0, 0.393),
     'L0_xcond_b_m1': (0.0, 0.8),
     'L0_xcond_b_m2': (0.0, 1.378)}
    factors = {'ctx_1024': 3.062,
     'L0_xcond_w_qkv': 8.0,
     'L0_xcond_w_so': 6.019,
     'L0_xcond_w_q': 3.225,
     'L0_xcond_w_m1': 6.091,
     'L0_xcond_w_m2': 6.1}
    for name, (base, spread) in spreads.items():
        noise = np.random.default_rng([zlib.crc32(name.encode()), seed]).standard_normal(out[name].shape)
        drawn = base * np.exp(spread * noise) if base else spread * noise
        out[name] = jnp.asarray(drawn.astype(out[name].dtype))
    for name, factor in factors.items():
        out[name] = (out[name] * factor).astype(out[name].dtype)
    return out
```

```python
from contextlib import ExitStack

import concourse.bass as bass
from concourse import mybir

F32 = mybir.dt.float32
BF16 = mybir.dt.bfloat16
ALU = mybir.AluOpType
ACT = mybir.ActivationFunctionType
AX_X = mybir.AxisListType.X

P = 128
HEADS = 16
HD = 16
TOPK = 16
SHIFT = 64
COMBO = 6
PARTS = 3
KROWS = COMBO * HD
BROWS = KROWS + PARTS
LOWEST = -3.4028234663852886e38
BIG = 2.0 ** 100
EPS = 1e-6


def build(nc, x, cond, ctx, w_ada, b_ada, w_qkv, b_qkv, w_so, b_so, w_q, b_q, w_kv, b_kv,
          w_co, b_co, w_m1, b_m1, w_m2, b_m2, out):
    B, L, C = x.shape
    LC = ctx.shape[1]
    HID = w_m2.shape[0]
    KC = C // P
    NT = L // P
    NK = -(-LC // P)
    KLAST = LC - (NK - 1) * P
    U = B * HEADS
    PAIRS = U // 2
    NMOD = w_ada.shape[1] // P
    QSCALE = float(HD) ** -0.5
    HC = HID // P

    with ExitStack() as top:
        used = {}

        def unique(name):
            used[name] = used.get(name, 0) + 1
            return name if used[name] == 1 else f"{name}_{used[name]}"

        def sbuf(stack, name, shape, dt=F32):
            return stack.enter_context(nc.sbuf_tensor(unique(name), shape, dt))

        def psum(stack, name, shape, dt=F32):
            return stack.enter_context(nc.psum_tensor(unique(name), shape, dt))

        fresh = []

        def sem(stack, name):
            fresh.append(stack.enter_context(nc.semaphore(unique(name))))
            return fresh[-1]

        def set_to_one(eng):
            for s in fresh:
                eng.sem_inc(s, 1)
            fresh.clear()

        def at(count):
            return count + 1

        s_held = top.enter_context(nc.semaphore("s_held"))

        qs_d = nc.dram_tensor("qs_d", [PARTS, U * HD, L], BF16)
        ks_d = nc.dram_tensor("ks_d", [PARTS, U * HD, L], BF16)
        vs_d = nc.dram_tensor("vs_d", [U, P, NT * HD], F32)
        qc_d = nc.dram_tensor("qc_d", [PARTS, U * HD, L], BF16)
        kc_d = nc.dram_tensor("kc_d", [PARTS, U * HD, LC], BF16)
        vc_d = nc.dram_tensor("vc_d", [U, P, NK * HD], F32)
        os_d = nc.dram_tensor("os_d", [U * HD, L], F32)
        oc_d = nc.dram_tensor("oc_d", [U * HD, L], F32)

        xs = sbuf(top, "xs", [P, B, NT, C])
        ident = sbuf(top, "ident", [P, P])
        identb = sbuf(top, "identb", [P, P], BF16)
        negbig = sbuf(top, "negbig", [P, P], BF16)
        ones = sbuf(top, "ones", [P, P])
        modT = sbuf(top, "modT", [P, NMOD, B])
        gate = sbuf(top, "gate", [P, 3, B, C])
        mhalf = sbuf(top, "mhalf", [P, NT])

        with ExitStack() as s:
            wa = sbuf(s, "wa", [P, KC, NMOD * P])
            bac = sbuf(s, "bac", [P, NMOD])
            bar = sbuf(s, "bar", [1, NMOD * P])
            condT = sbuf(s, "condT", [P, KC, B])
            e = sbuf(s, "e", [P, KC, B])
            d = sbuf(s, "d", [P, KC, B])
            rd = sbuf(s, "rd", [P, KC, B])
            sl = sbuf(s, "sl", [P, KC, B])
            slb = sbuf(s, "slb", [P, KC, B, P])
            psM = psum(s, "psM", [P, 512 // B, B])
            psG = [psum(s, f"psG{k}", [P, 512]) for k in range(2)]
            s_x, s_w, s_e, s_d, s_slb = (sem(s, n) for n in ("s_x", "s_w", "s_e", "s_d", "s_slb"))
            s_one, s_id, s_m, s_mc, s_g, s_gc = (sem(s, n) for n in
                                                 ("s_one", "s_id", "s_m", "s_mc", "s_g", "s_gc"))
            block = s.enter_context(nc.Block())

            @block.sync
            def _(sp):
                set_to_one(sp)
                for k in range(KC):
                    sp.dma_start(condT[:, k, :], cond[:, k * P:(k + 1) * P].rearrange("b p -> p b"),
                                 allow_slow_non_contiguous=True).then_inc(s_w, 16)
                sp.dma_start(bac[:, :], b_ada.rearrange("(n p) -> p n", p=P),
                             allow_slow_non_contiguous=True).then_inc(s_w, 16)
                sp.dma_start(bar[:, :], b_ada.rearrange("(o n) -> o n", o=1)).then_inc(s_w, 16)
                sp.dma_start(wa[:, :, :], w_ada.rearrange("(k p) n -> p k n", p=P)).then_inc(s_w, 16)
                for b in range(B):
                    sp.dma_start(xs[:, b, 0:NT - 1, :],
                                 x[b, SHIFT:L - SHIFT, :].rearrange("(t p) c -> p t c", p=P)).then_inc(s_x, 16)
                    sp.dma_start(xs[0:SHIFT, b, NT - 1, :], x[b, L - SHIFT:L, :]).then_inc(s_x, 16)
                    sp.dma_start(xs[SHIFT:P, b, NT - 1, :], x[b, 0:SHIFT, :]).then_inc(s_x, 16)
                sp.wait_ge(s_x, at(48 * B))

            @block.gpsimd
            def _(pool):
                nc.gpsimd.memset(ident[:, :], 0.0).then_inc(s_id, 1)
                nc.gpsimd.memset(mhalf[:, :], -0.5)
                pool.wait_ge(s_id, at(1))
                nc.gpsimd.affine_select(out=ident[:, :], in_=ident[:, :], compare_op=ALU.not_equal,
                                        fill=1.0, base=0, pattern=[[-1, P]],
                                        channel_multiplier=1).then_inc(s_id, 1)
                pool.wait_ge(s_id, at(2))
                nc.gpsimd.tensor_copy(identb[:, :], ident[:, :]).then_inc(s_id, 1)
                nc.gpsimd.tensor_scalar(negbig[:, :], ident[:, :], -BIG, None, ALU.mult).then_inc(s_id, 1)

            @block.scalar
            def _(act):
                act.wait_ge(s_w, at(16 * (KC + 3)))
                nc.scalar.activation(e[:, :, :], condT[:, :, :], ACT.Exp, scale=-1.0).then_inc(s_e, 1)

            @block.vector
            def _(dve):
                nc.vector.memset(ones[:, :], 1.0).then_inc(s_one, 1)
                dve.wait_ge(s_e, at(1))
                nc.vector.tensor_scalar(d[:, :, :], e[:, :, :], 1.0, None, ALU.add).then_inc(s_d, 1)
                dve.wait_ge(s_d, at(1))
                nc.vector.reciprocal(rd[:, :, :], d[:, :, :]).then_inc(s_d, 1)
                dve.wait_ge(s_d, at(2))
                nc.vector.tensor_tensor(sl[:, :, :], condT[:, :, :], rd[:, :, :], ALU.mult).then_inc(s_d, 1)
                dve.wait_ge(s_d, at(3))
                dve.wait_ge(s_one, at(1))
                for k in range(KC):
                    for b in range(B):
                        nc.vector.tensor_scalar(slb[:, k, b, :], ones[:, :], sl[:, k, b:b + 1], None,
                                                ALU.mult).then_inc(s_slb, 1)
                dve.wait_ge(s_m, at(1))
                for b in range(B):
                    nc.vector.tensor_tensor(modT[:, :, b], psM[:, 0:NMOD, b], bac[:, :], ALU.add).then_inc(s_mc, 1)
                dve.wait_ge(s_mc, at(B))
                for part in (1, 4, 7):
                    m = modT[:, part * KC:(part + 1) * KC, :]
                    nc.vector.tensor_scalar(m, m, 1.0, None, ALU.add).then_inc(s_mc, 1)
                for n in range(3 * B):
                    dve.wait_ge(s_g, at(n + 1))
                    nc.vector.tensor_copy(gate[:, n // B, n % B, :], psG[n % 2][:, 0:C]).then_inc(s_gc, 1)

            @block.tensor
            def _(pe):
                pe.wait_ge(s_d, at(3))
                for n in range(NMOD):
                    for k in range(KC):
                        mm = nc.tensor.matmul(psM[:, n, :], wa[:, k, n * P:(n + 1) * P], sl[:, k, :],
                                              start=(k == 0), stop=(k == KC - 1))
                mm.then_inc(s_m, 1)
                pe.wait_ge(s_slb, at(KC * B))
                for n in range(3 * B):
                    g, b = n // B, n % B
                    cols = slice((3 * g + 2) * C, (3 * g + 3) * C)
                    if n >= 2:
                        pe.wait_ge(s_gc, at(n - 1))
                    nc.tensor.matmul(psG[n % 2][:, 0:C], ones[0:1, :], bar[:, cols], start=True, stop=False)
                    for k in range(KC):
                        mm = nc.tensor.matmul(psG[n % 2][:, 0:C], slb[:, k, b, :], wa[:, k, cols],
                                              start=False, stop=(k == KC - 1))
                    mm.then_inc(s_g, 1)

        def norm_buffers(s):
            t = {}
            t["st"] = sbuf(s, "st", [P, NT, 6])
            t["mv"] = sbuf(s, "mv", [P, NT, 2])
            t["ve"] = sbuf(s, "ve", [P, NT])
            t["rs"] = sbuf(s, "rs", [P, NT])
            t["xn"] = sbuf(s, "xn", [P, NT, C])
            t["hT"] = sbuf(s, "hT", [P, KC, L])
            t["psX"] = [psum(s, f"psX{k}", [P, L]) for k in range(KC)]
            for n in ("stats", "aggr", "var", "rstd", "xnorm", "turned", "hready"):
                t[n] = sem(s, "s_" + n)
            return t

        def norm_vector(dve, t, b, added=None, adds=NT):
            for w in range(NT):
                if added is not None:
                    dve.wait_ge(added, at(adds * b + w + 1))
                    dve.sem_inc(s_held, 1)
                nc.vector.bn_stats(t["st"][:, w, :], xs[:, b, w, :]).then_inc(t["stats"], 1)
            for w in range(NT):
                dve.wait_ge(t["stats"], at(NT * b + w + 1))
                dve.sem_inc(s_held, 1)
                nc.vector.bn_aggr(t["mv"][:, w, :], t["st"][:, w, :]).then_inc(t["aggr"], 1)
            dve.wait_ge(t["rstd"], at(b + 1))
            dve.wait_ge(t["turned"], at(KC * NT * b))
            for w in range(NT):
                nc.vector.tensor_scalar(t["xn"][:, w, :], xs[:, b, w, :], t["mv"][:, w, 0:1],
                                        t["rs"][:, w:w + 1], ALU.subtract, ALU.mult).then_inc(t["xnorm"], 1)

        def norm_pool(pool, t, b):
            pool.wait_ge(t["aggr"], at(NT * (b + 1)))
            pool.wait_ge(t["xnorm"], at(NT * b))
            pool.sem_inc(s_held, 1)
            nc.gpsimd.tensor_scalar(t["ve"][:, :], t["mv"][:, :, 1], EPS, None, ALU.add).then_inc(t["var"], 1)
            pool.wait_ge(t["var"], at(b + 1))
            nc.gpsimd.tensor_tensor(t["rs"][:, :], t["ve"][:, :], mhalf[:, :], ALU.pow).then_inc(t["rstd"], 1)

        def norm_tensor(pe, t, b):
            pe.wait_ge(t["hready"], at(KC * b))
            for w in range(NT):
                pe.wait_ge(t["xnorm"], at(NT * b + w + 1))
                for k in range(KC):
                    nc.tensor.transpose(t["psX"][k][:, w * P:(w + 1) * P], t["xn"][:, w, k * P:(k + 1) * P],
                                        ident[:, :]).then_inc(t["turned"], 1)

        def norm_scalar(act, t, b, which, used, uses):
            act.wait_ge(t["turned"], at(KC * NT * (b + 1)))
            act.wait_ge(used, at(uses * b))
            for k in range(KC):
                nc.scalar.activation(t["hT"][:, k, :], t["psX"][k][:, :], ACT.Identity,
                                     bias=modT[:, (3 * which) * KC + k, bass.ds(b, 1)],
                                     scale=modT[:, (3 * which + 1) * KC + k, bass.ds(b, 1)]).then_inc(t["hready"], 1)

        def split_buffers(s):
            t = {"psP": [psum(s, f"psP{k}", [P, L]) for k in range(2)],
                 "T": [sbuf(s, f"T{k}", [P, L]) for k in range(2)],
                 "R": [sbuf(s, f"R{k}", [P, L]) for k in range(2)],
                 "Pt": [sbuf(s, f"Pt{k}", [P, PARTS, L], BF16) for k in range(2)]}
            for n in ("prod", "biased", "part1", "rest", "part2", "part3"):
                t[n] = sem(s, "s_" + n)
            t["parted"] = [sem(s, f"s_parted{k}") for k in range(2)]
            return t

        def split_tensor(pe, t, b, J, j, n, lhs, rhs):
            pe.wait_ge(t["biased"], at(J * b if j < 2 else J * b + j - 1))
            for k in range(KC):
                mm = nc.tensor.matmul(t["psP"][j % 2][:, 0:n], lhs(k), rhs(k), start=(k == 0), stop=(k == KC - 1))
            mm.then_inc(t["prod"], 1)

        def split_scalar(act, t, b, J, j, n, bias, scale):
            act.wait_ge(t["prod"], at(J * b + j + 1))
            act.wait_ge(t["rest"], at(J * b if j < 2 else J * b + j - 1))
            nc.scalar.activation(t["T"][j % 2][:, 0:n], t["psP"][j % 2][:, 0:n], ACT.Identity,
                                 bias=bias, scale=scale).then_inc(t["biased"], 1)

        def split_vector(dve, t, b, J, j, n):
            T, R, Pt = t["T"][j % 2], t["R"][j % 2], t["Pt"][j % 2]
            g = J * b + j
            dve.wait_ge(t["biased"], at(g + 1))
            dve.wait_ge(t["parted"][j % 2], at(16 * PARTS * (J // 2 * b + j // 2)))
            nc.vector.tensor_copy(Pt[:, 0, 0:n], T[:, 0:n]).then_inc(t["part1"], 1)
            dve.wait_ge(t["part1"], at(g + 1))
            dve.wait_ge(t["part3"], at(J * b if j < 2 else g - 1))
            nc.vector.tensor_tensor(R[:, 0:n], T[:, 0:n], Pt[:, 0, 0:n], ALU.subtract).then_inc(t["rest"], 1)
            dve.wait_ge(t["rest"], at(g + 1))
            nc.vector.tensor_copy(Pt[:, 1, 0:n], R[:, 0:n]).then_inc(t["part2"], 1)

        def split_pool(pool, t, b, J, j, n):
            R, Pt = t["R"][j % 2], t["Pt"][j % 2]
            pool.wait_ge(t["part2"], at(J * b + j + 1))
            nc.gpsimd.tensor_tensor(Pt[:, 2, 0:n], R[:, 0:n], Pt[:, 1, 0:n], ALU.subtract).then_inc(t["part3"], 1)

        def split_sync(sp, t, b, J, j, n, dram, chunk, c0):
            sp.wait_ge(t["part3"], at(J * b + j + 1))
            sp.sem_inc(s_held, 1)
            for a in range(PARTS):
                sp.dma_start(dram[a, bass.ds(b * C + chunk * P, P), c0:c0 + n],
                             t["Pt"][j % 2][:, a, 0:n]).then_inc(t["parted"][j % 2], 16)

        def add_buffers(s):
            t = {"psV": [psum(s, f"psV{k}", [P, 512]) for k in range(2)],
                 "tmp": [sbuf(s, f"tmp{k}", [P, C]) for k in range(2)]}
            for n in ("summed", "gated", "added"):
                t[n] = sem(s, "s_" + n)
            return t

        def add_tensor(pe, t, b, J, j, bias, lhs, rhs, chunks):
            pe.wait_ge(t["gated"], at(J * b if j < 2 else J * b + j - 1))
            ps = t["psV"][j % 2][:, 0:C]
            nc.tensor.matmul(ps, ones[0:1, :], bias, start=True, stop=False)
            for k in range(chunks):
                mm = nc.tensor.matmul(ps, lhs(k), rhs(k), start=False, stop=(k == chunks - 1))
            mm.then_inc(t["summed"], 1)

        def add_vector(dve, t, b, J, j, w, which):
            dve.wait_ge(t["summed"], at(J * b + j + 1))
            dve.wait_ge(t["added"], at(J * b if j < 2 else J * b + j - 1))
            nc.vector.tensor_tensor(t["tmp"][j % 2][:, :], t["psV"][j % 2][:, 0:C],
                                    gate[:, which, bass.ds(b, 1), :], ALU.mult).then_inc(t["gated"], 1)
            dve.wait_ge(t["gated"], at(J * b + j + 1))
            xt = xs[:, b, w, :]
            nc.vector.tensor_tensor(xt, xt, t["tmp"][j % 2][:, :], ALU.add).then_inc(t["added"], 1)

        def head_major(ap):
            return ap.rearrange("p (h d) -> p h d", d=HD)

        def column(v):
            return v.rearrange("(n p) -> p n", p=P)

        def row(v):
            return v.rearrange("(o n) -> o n", o=1)

        with ExitStack() as s:
            t = norm_buffers(s)
            f = split_buffers(s)
            wqkv = sbuf(s, "wqkv", [P, KC, 3 * C])
            bqk = sbuf(s, "bqk", [P, 2 * KC])
            bqks = sbuf(s, "bqks", [P, 2 * KC])
            bv = sbuf(s, "bv", [1, C])
            vh = sbuf(s, "vh", [P, HEADS, NT, HD])
            psV = [psum(s, f"psV{k}", [P, 512]) for k in range(2)]
            s_w, s_bs, s_v, s_vc, s_vd = (sem(s, n) for n in ("s_w", "s_bs", "s_v", "s_vc", "s_vd"))
            J = 2 * KC
            block = s.enter_context(nc.Block())

            @block.sync
            def _(sp):
                set_to_one(sp)
                sp.dma_start(wqkv[:, :, :], w_qkv.rearrange("(k p) n -> p k n", p=P)).then_inc(s_w, 16)
                sp.dma_start(bqk[:, :], column(b_qkv[0:2 * C]), allow_slow_non_contiguous=True).then_inc(s_w, 16)
                sp.dma_start(bv[:, :], row(b_qkv[2 * C:3 * C])).then_inc(s_w, 16)
                with sp.Fori(0, B) as b:
                    for j in range(J):
                        split_sync(sp, f, b, J, j, L, qs_d if j < KC else ks_d, j % KC, 0)
                    sp.wait_ge(s_vc, at(NT * (b + 1)))
                    sp.dma_start(vs_d[bass.ds(b * HEADS, HEADS), :, :].rearrange("h p n -> p h n"),
                                 vh[:, :, :, :].rearrange("p h w d -> p h (w d)")).then_inc(s_vd, 16)
                for k in range(2):
                    sp.wait_ge(f["parted"][k], at(16 * PARTS * B * J // 2))
                sp.wait_ge(s_vd, at(16 * B))

            @block.gpsimd
            def _(pool):
                with pool.Fori(0, B) as b:
                    norm_pool(pool, t, b)
                    for j in range(J):
                        split_pool(pool, f, b, J, j, L)

            @block.vector
            def _(dve):
                dve.wait_ge(s_w, at(48))
                nc.vector.tensor_scalar(bqks[:, 0:KC], bqk[:, 0:KC], QSCALE, None, ALU.mult).then_inc(s_bs, 1)
                nc.vector.tensor_copy(bqks[:, KC:2 * KC], bqk[:, KC:2 * KC]).then_inc(s_bs, 1)
                with dve.Fori(0, B) as b:
                    norm_vector(dve, t, b)
                    for j in range(J):
                        split_vector(dve, f, b, J, j, L)

            @block.scalar
            def _(act):
                act.wait_ge(s_bs, at(2))
                with act.Fori(0, B) as b:
                    norm_scalar(act, t, b, 0, s_v, NT)
                    for j in range(J):
                        split_scalar(act, f, b, J, j, L, bqks[:, j:j + 1], QSCALE if j < KC else 1.0)
                    act.wait_ge(s_vd, at(16 * b))
                    for w in range(NT):
                        act.wait_ge(s_v, at(NT * b + w + 1))
                        nc.scalar.copy(vh[:, :, w, :], head_major(psV[w % 2][:, 0:C])).then_inc(s_vc, 1)

            @block.tensor
            def _(pe):
                pe.wait_ge(s_w, at(48))
                with pe.Fori(0, B) as b:
                    norm_tensor(pe, t, b)
                    pe.wait_ge(t["hready"], at(KC * (b + 1)))
                    for j in range(J):
                        split_tensor(pe, f, b, J, j, L, lambda k: wqkv[:, k, j * P:(j + 1) * P],
                                     lambda k: t["hT"][:, k, :])
                    for w in range(NT):
                        pe.wait_ge(s_vc, at(NT * b if w < 2 else NT * b + w - 1))
                        nc.tensor.matmul(psV[w % 2][:, 0:C], ones[0:1, :], bv[:, :], start=True, stop=False)
                        for k in range(KC):
                            mm = nc.tensor.matmul(psV[w % 2][:, 0:C], t["hT"][:, k, w * P:(w + 1) * P],
                                                  wqkv[:, k, 2 * C:3 * C], start=False, stop=(k == KC - 1))
                        mm.then_inc(s_v, 1)

        with ExitStack() as s:
            f = split_buffers(s)
            wkv = sbuf(s, "wkv", [P, KC, 2 * C])
            bk = sbuf(s, "bk", [P, KC])
            bv = sbuf(s, "bv", [1, C])
            cs = sbuf(s, "cs", [P, NK, C])
            cT = sbuf(s, "cT", [P, KC, NK * P])
            vh = sbuf(s, "vh", [P, HEADS, NK, HD])
            psX = [psum(s, f"psX{k}", [P, 512]) for k in range(KC)]
            psV = [psum(s, f"psV{k}", [P, 512]) for k in range(2)]
            s_w, s_z, s_v, s_vc, s_vd = (sem(s, n) for n in ("s_w", "s_z", "s_v", "s_vc", "s_vd"))
            s_c, s_turned, s_ct = (sem(s, n) for n in ("s_c", "s_turned", "s_ct"))
            GT = 512 // P
            NG = -(-NK // GT)
            J = KC * NG
            gw = [min(GT * P, LC - g * GT * P) for g in range(NG)]
            rows = [min(P, LC - kt * P) for kt in range(NK)]
            block = s.enter_context(nc.Block())

            @block.sync
            def _(sp):
                set_to_one(sp)
                sp.dma_start(wkv[:, :, :], w_kv.rearrange("(k p) n -> p k n", p=P)).then_inc(s_w, 16)
                sp.dma_start(bk[:, :], column(b_kv[0:C]), allow_slow_non_contiguous=True).then_inc(s_w, 16)
                sp.dma_start(bv[:, :], row(b_kv[C:2 * C])).then_inc(s_w, 16)
                with sp.Fori(0, B) as b:
                    sp.wait_ge(s_turned, at(KC * NG * b))
                    cb = ctx[bass.ds(b, 1), :, :].rearrange("o r c -> (o r) c")
                    sp.dma_start(cs[:, 0:NK - 1, :],
                                 cb[0:(NK - 1) * P, :].rearrange("(t p) c -> p t c", p=P)).then_inc(s_c, 16)
                    sp.dma_start(cs[0:KLAST, NK - 1, :], cb[(NK - 1) * P:LC, :]).then_inc(s_c, 16)
                    for j in range(J):
                        split_sync(sp, f, b, J, j, gw[j // KC], kc_d, j % KC, (j // KC) * GT * P)
                    sp.wait_ge(s_vc, at(NK * (b + 1)))
                    sp.dma_start(vc_d[bass.ds(b * HEADS, HEADS), :, :].rearrange("h p n -> p h n"),
                                 vh[:, :, :, :].rearrange("p h w d -> p h (w d)")).then_inc(s_vd, 16)
                for k in range(2):
                    sp.wait_ge(f["parted"][k], at(16 * PARTS * B * J // 2))
                sp.wait_ge(s_vd, at(16 * B))

            @block.gpsimd
            def _(pool):
                nc.gpsimd.memset(vh[KLAST // 32 * 32:P, :, NK - 1, :], 0.0).then_inc(s_z, 1)
                pool.wait_ge(s_z, at(1))
                with pool.Fori(0, B) as b:
                    for j in range(J):
                        split_pool(pool, f, b, J, j, gw[j // KC])

            @block.vector
            def _(dve):
                with dve.Fori(0, B) as b:
                    dve.wait_ge(s_v, at(NK * b))
                    for g in range(NG):
                        for k in range(KC):
                            dve.wait_ge(s_turned, at(KC * NG * b + KC * g + k + 1))
                            nc.vector.tensor_copy(cT[:, k, g * GT * P:g * GT * P + gw[g]],
                                                  psX[k][:, 0:gw[g]]).then_inc(s_ct, 1)
                    for j in range(J):
                        split_vector(dve, f, b, J, j, gw[j // KC])

            @block.scalar
            def _(act):
                act.wait_ge(s_w, at(48))
                act.wait_ge(s_z, at(1))
                with act.Fori(0, B) as b:
                    for j in range(J):
                        split_scalar(act, f, b, J, j, gw[j // KC], bk[:, j % KC:j % KC + 1], 1.0)
                    act.wait_ge(s_vd, at(16 * b))
                    for kt in range(NK):
                        act.wait_ge(s_v, at(NK * b + kt + 1))
                        nc.scalar.copy(vh[0:rows[kt], :, kt, :],
                                       head_major(psV[kt % 2][0:rows[kt], 0:C])).then_inc(s_vc, 1)

            @block.tensor
            def _(pe):
                pe.wait_ge(s_w, at(48))
                with pe.Fori(0, B) as b:
                    pe.wait_ge(s_c, at(32 * (b + 1)))
                    for g in range(NG):
                        for k in range(KC):
                            pe.wait_ge(s_ct, at(J * b if g == 0 else J * b + KC * (g - 1) + k + 1))
                            for kt in range(g * GT, min(NK, (g + 1) * GT)):
                                r = rows[kt]
                                tr = nc.tensor.transpose(psX[k][:, (kt - g * GT) * P:(kt - g * GT) * P + r],
                                                         cs[0:r, kt, k * P:(k + 1) * P], ident[0:r, 0:r])
                            tr.then_inc(s_turned, 1)
                    for j in range(J):
                        g = j // KC
                        pe.wait_ge(s_ct, at(J * b + KC * (g + 1)))
                        split_tensor(pe, f, b, J, j, gw[g], lambda k: wkv[:, k, (j % KC) * P:(j % KC + 1) * P],
                                     lambda k: cT[:, k, g * GT * P:g * GT * P + gw[g]])
                    for kt in range(NK):
                        r = rows[kt]
                        pe.wait_ge(s_vc, at(NK * b if kt < 2 else NK * b + kt - 1))
                        nc.tensor.matmul(psV[kt % 2][0:r, 0:C], ones[0:1, 0:r], bv[:, :], start=True, stop=False)
                        for k in range(KC):
                            mm = nc.tensor.matmul(psV[kt % 2][0:r, 0:C], cT[:, k, kt * P:kt * P + r],
                                                  wkv[:, k, C:2 * C], start=False, stop=(k == KC - 1))
                        mm.then_inc(s_v, 1)

        def attention(topk, q_d, k_d, v_d, o_d):
            KW = LC if topk else L
            NB = NK if topk else NT
            rows = [min(P, KW - kt * P) for kt in range(NB)]
            LOADS = 2 * COMBO + 1
            KPART = [0, 1, 2, 0, 1, 0]
            QPART = [0, 0, 0, 1, 1, 2]
            NW = 3
            with ExitStack() as s:
                Q = [sbuf(s, f"Q{r}", [P, L], BF16) for r in range(2)]
                K = [sbuf(s, f"K{r}", [P, KW], BF16) for r in range(2)]
                V = [sbuf(s, f"V{r}", [P, NB, HD]) for r in range(2)]
                VO = [sbuf(s, f"VO{r}", [P, NB, 4 * HD]) for r in range(2)]
                W = sbuf(s, "W", [P, NW, L])
                OL = sbuf(s, "OL", [4 * HD, L])
                RL = sbuf(s, "RL", [2 * HD, L])
                OT = sbuf(s, "OT", [2 * HD, L])
                tops = [sbuf(s, f"tops{r}", [P, NT, TOPK]) for r in range(2)]
                nm = sbuf(s, "nm", [P, NT])
                r1 = sbuf(s, "r1", [P, NT])
                mp = [sbuf(s, f"mp{r}", [P, NT, PARTS], BF16) for r in range(2)]
                if topk:
                    S = [sbuf(s, f"S{w}", [P, KW]) for w in range(NT)]
                    M = [sbuf(s, f"M{w}", [P, KW]) for w in range(2)]
                    N = [[sbuf(s, f"N{r}_{w}", [P, KW], BF16) for w in range(NT)] for r in range(2)]
                    psS = psum(s, "psS", [P, 4 * 512])
                else:
                    psS2 = [psum(s, f"psS{r}", [P, 512]) for r in range(2)]
                psT = psum(s, "psT", [P, 1024], BF16)
                psB = [psum(s, f"psB{k}", [P, 512]) for k in range(2)]
                psO = psum(s, "psO", [P, 512])
                s_ld = [sem(s, f"s_ld{r}") for r in range(2)]
                (s_set, s_vo, s_sc, s_ev, s_pick, s_top, s_mark, s_chain, s_mp, s_mt, s_qb, s_b, s_e, s_pv,
                 s_oc, s_rl, s_o, s_od) = (sem(s, n) for n in (
                     "s_set", "s_vo", "s_sc", "s_ev", "s_pick", "s_top", "s_mark", "s_chain", "s_mp", "s_mt",
                     "s_qb", "s_b", "s_e", "s_pv", "s_oc", "s_rl", "s_o", "s_od"))
                block = s.enter_context(nc.Block())

                def quarter(w):
                    return range(w * NB // NT, (w + 1) * NB // NT)

                def load(sp, u, r):
                    for c in range(COMBO):
                        sp.dma_start(Q[r][c * HD:(c + 1) * HD, :],
                                     q_d[QPART[c], bass.ds(u * HD, HD), :]).then_inc(s_ld[r], 16)
                    for c in range(COMBO):
                        sp.dma_start(K[r][c * HD:(c + 1) * HD, :],
                                     k_d[KPART[c], bass.ds(u * HD, HD), :]).then_inc(s_ld[r], 16)
                    sp.dma_start(V[r][:, :, :], v_d[bass.ds(u, 1), :, :].rearrange("o p n -> p (o n)")
                                 .rearrange("p (t d) -> p t d", d=HD)).then_inc(s_ld[r], 16)

                @block.sync
                def _(sp):
                    set_to_one(sp)
                    def store(i):
                        sp.wait_ge(s_o, at(i + 1))
                        sp.dma_start(o_d[bass.ds(i * 2 * HD, 2 * HD), :], OT[:, :]).then_inc(s_od, 16)

                    load(sp, 0, 0)
                    load(sp, 1, 1)
                    with sp.Fori(0, PAIRS - 1) as i:
                        sp.wait_ge(s_pv, at(NB * (2 * i + 1)))
                        sp.sem_inc(s_held, 1)
                        load(sp, 2 * i + 2, 0)
                        sp.wait_ge(s_pv, at(NB * (2 * i + 2)))
                        sp.sem_inc(s_held, 1)
                        load(sp, 2 * i + 3, 1)
                        store(i)
                    store(PAIRS - 1)
                    sp.wait_ge(s_od, at(16 * PAIRS))

                @block.gpsimd
                def _(pool):
                    def values(i, r):
                        pool.wait_ge(s_ld[r], at(16 * LOADS * (i + 1)))
                        pool.sem_inc(s_held, 1)
                        nc.gpsimd.tensor_copy(VO[r][:, :, r * HD:(r + 1) * HD], V[r][:, :, :]).then_inc(s_vo, 1)

                    def front(u, r):
                        if topk:
                            for w in range(NT):
                                pool.wait_ge(s_mark, at(NT * u + w + 1))
                                pool.sem_inc(s_held, 1)
                                nc.gpsimd.tensor_scalar(N[r][w][:, :], M[w % 2][:, :], LOWEST, None,
                                                        ALU.is_gt).then_inc(s_pick, 1)
                        else:
                            pool.wait_ge(s_top, at(u + 1))
                        pool.wait_ge(s_mt, at(u))
                        chain = [(nm[:, :], tops[r][:, :, 0], -1.0), (mp[r][:, :, 0], nm[:, :], None),
                                 (r1[:, :], nm[:, :], mp[r][:, :, 0]), (mp[r][:, :, 1], r1[:, :], None),
                                 (mp[r][:, :, 2], r1[:, :], mp[r][:, :, 1])]
                        for n, (o, a, c) in enumerate(chain):
                            pool.wait_ge(s_chain, at(5 * u + n))
                            pool.sem_inc(s_held, 1)
                            if c is None:
                                ins = nc.gpsimd.tensor_copy(o, a)
                            elif n == 0:
                                ins = nc.gpsimd.tensor_scalar(o, a, c, None, ALU.mult)
                            else:
                                ins = nc.gpsimd.tensor_tensor(o, a, c, ALU.subtract)
                            ins.then_inc(s_chain, 1)

                    def finish(i):
                        pool.wait_ge(s_rl, at(i + 1))
                        pool.wait_ge(s_od, at(16 * i))
                        nc.gpsimd.tensor_tensor(OT[:, :], OL[0:2 * HD, :], RL[:, :], ALU.mult).then_inc(s_o, 1)

                    pool.wait_ge(s_set, at(6))
                    values(0, 0)
                    front(0, 0)
                    with pool.Fori(0, PAIRS - 1) as i:
                        values(i, 1)
                        front(2 * i + 1, 1)
                        values(i + 1, 0)
                        front(2 * i + 2, 0)
                        finish(i)
                    values(PAIRS - 1, 1)
                    front(2 * PAIRS - 1, 1)
                    finish(PAIRS - 1)

                @block.vector
                def _(dve):
                    for r in range(2):
                        nc.vector.memset(VO[r][:, :, :], 0.0).then_inc(s_set, 1)
                        nc.vector.memset(K[r][KROWS:P, :], 1.0).then_inc(s_set, 1)
                    dve.wait_ge(s_set, at(4))
                    for r in range(2):
                        nc.vector.memset(VO[r][:, :, (2 + r) * HD:(3 + r) * HD], 1.0).then_inc(s_set, 1)

                    def front(u, r):
                        if not topk:
                            dve.wait_ge(s_sc, at(u + 1))
                            nc.vector.tensor_reduce(tops[r][:, :, 0],
                                                    psS2[r][:, :].rearrange("p (w k) -> p w k", k=P),
                                                    AX_X, ALU.max).then_inc(s_top, 1)
                            return
                        for w in range(NT):
                            a, b = tops[r][:, w, 0:8], tops[r][:, w, 8:16]
                            n = NT * u + w
                            dve.wait_ge(s_ev, at(n + 1))
                            dve.sem_inc(s_held, 1)
                            nc.vector.max(a, S[w][:, :]).then_inc(s_top, 1)
                            dve.wait_ge(s_top, at(3 * n + 1))
                            dve.wait_ge(s_pick, at(NT * u if w < 2 else n - 1))
                            dve.sem_inc(s_held, 1)
                            nc.vector.match_replace(M[w % 2][:, :], a, S[w][:, :], LOWEST).then_inc(s_top, 1)
                            dve.wait_ge(s_top, at(3 * n + 2))
                            dve.sem_inc(s_held, 1)
                            nc.vector.max(b, M[w % 2][:, :]).then_inc(s_top, 1)
                            dve.wait_ge(s_top, at(3 * n + 3))
                            dve.sem_inc(s_held, 1)
                            nc.vector.match_replace(M[w % 2][:, :], b, M[w % 2][:, :], LOWEST).then_inc(s_mark, 1)

                    def finish(i):
                        dve.wait_ge(s_oc, at(i + 1))
                        dve.wait_ge(s_o, at(i))
                        nc.vector.reciprocal(RL[:, :], OL[2 * HD:4 * HD, :]).then_inc(s_rl, 1)

                    front(0, 0)
                    with dve.Fori(0, PAIRS - 1) as i:
                        front(2 * i + 1, 1)
                        dve.wait_ge(s_chain, at(5 * (2 * i + 1)))
                        front(2 * i + 2, 0)
                        finish(i)
                        dve.wait_ge(s_chain, at(5 * (2 * i + 2)))
                    front(2 * PAIRS - 1, 1)
                    finish(PAIRS - 1)

                @block.scalar
                def _(act):
                    def copy_scores(u, w):
                        if topk:
                            n = NT * u + w
                            act.wait_ge(s_sc, at(n + 1))
                            act.wait_ge(s_top, at(3 * (NT * (u - 1) + w) + 2))
                            nc.scalar.copy(S[w][:, :], psS[:, 0:KW]).then_inc(s_ev, 1)

                    def first_copies():
                        if topk:
                            for w in range(NT):
                                act.wait_ge(s_sc, at(w + 1))
                                nc.scalar.copy(S[w][:, :], psS[:, 0:KW]).then_inc(s_ev, 1)

                    def maxima(u, r):
                        act.wait_ge(s_mt, at(u + 1))
                        nc.scalar.copy(Q[r][KROWS:BROWS, :], psT[0:PARTS, 0:L]).then_inc(s_qb, 1)

                    def exps(u, tiles):
                        for kt in tiles:
                            act.wait_ge(s_pv, at(NB * u if kt < NW else NB * u + kt - NW + 1))
                            if topk:
                                act.wait_ge(s_b, at(NB * u + kt + 1))
                                nc.scalar.activation(W[0:rows[kt], kt % NW, :], psB[kt % 2][0:rows[kt], :],
                                                     ACT.Exp).then_inc(s_e, 1)
                            elif kt == 0:
                                act.wait_ge(s_b, at(u + 1))
                                nc.scalar.activation(W[:, 0, :], psB[0][:, :], ACT.Exp).then_inc(s_e, 1)

                    def step(u, r, nxt):
                        maxima(u, r)
                        for w in range(NT):
                            if nxt:
                                copy_scores(u + 1, w)
                            exps(u, quarter(w))

                    def finish(i):
                        act.wait_ge(s_pv, at(NB * (2 * i + 2)))
                        act.wait_ge(s_o, at(i))
                        nc.scalar.copy(OL[:, :], psO[0:4 * HD, :]).then_inc(s_oc, 1)

                    first_copies()
                    with act.Fori(0, PAIRS - 1) as i:
                        step(2 * i, 0, True)
                        step(2 * i + 1, 1, True)
                        finish(i)
                    step(2 * PAIRS - 2, 0, True)
                    step(2 * PAIRS - 1, 1, False)
                    finish(PAIRS - 1)

                @block.tensor
                def _(pe):
                    def scores(i, u, w, r):
                        if w == 0:
                            pe.wait_ge(s_ld[r], at(16 * LOADS * (i + 1)))
                        if topk:
                            pe.wait_ge(s_ev, at(NT * u + w))
                            for c in range(0, KW, 512):
                                n = min(512, KW - c)
                                mm = nc.tensor.matmul(psS[:, c:c + n], Q[r][0:KROWS, w * P:(w + 1) * P],
                                                      K[r][0:KROWS, c:c + n], start=True, stop=True)
                            mm.then_inc(s_sc, 1)
                        else:
                            mm = nc.tensor.matmul(psS2[r][:, w * P:(w + 1) * P], Q[r][0:KROWS, w * P:(w + 1) * P],
                                                  K[r][0:KROWS, w * P:(w + 1) * P], start=True, stop=True)
                            if w == NT - 1:
                                mm.then_inc(s_sc, 1)

                    def maxima(u, r):
                        pe.wait_ge(s_chain, at(5 * (u + 1)))
                        pe.wait_ge(s_qb, at(u))
                        for w in range(NT):
                            tr = nc.tensor.transpose(psT[0:PARTS, w * P:(w + 1) * P], mp[r][:, w, :], identb[:, :])
                        tr.then_inc(s_mt, 1)

                    def shifted(i, u, r, kt):
                        if kt == 0:
                            pe.wait_ge(s_qb, at(u + 1))
                            if topk:
                                pe.wait_ge(s_pick, at(NT * (u + 1)))
                        if not topk:
                            if kt == 0:
                                pe.wait_ge(s_e, at(u))
                            mm = nc.tensor.matmul(psB[0][:, kt * P:(kt + 1) * P], K[r][0:BROWS, kt * P:(kt + 1) * P],
                                                  Q[r][0:BROWS, kt * P:(kt + 1) * P], start=True, stop=True)
                            if kt == NB - 1:
                                mm.then_inc(s_b, 1)
                            return
                        m = rows[kt]
                        pe.wait_ge(s_e, at(NB * u if kt < 2 else NB * u + kt - 1))
                        nc.tensor.matmul(psB[kt % 2][0:m, :], K[r][0:BROWS, kt * P:kt * P + m], Q[r][0:BROWS, :],
                                         start=True, stop=True)
                        for w in range(NT):
                            mm = nc.tensor.matmul(psB[kt % 2][0:m, w * P:(w + 1) * P], N[r][w][:, kt * P:kt * P + m],
                                                  negbig[:, :], start=False, stop=True,
                                                  skip_group_check=True)
                        mm.then_inc(s_b, 1)

                    def product(i, u, r, kt):
                        m = rows[kt]
                        if kt == 0:
                            pe.wait_ge(s_vo, at(u + 1))
                            if r == 0:
                                pe.wait_ge(s_oc, at(i))
                        if topk:
                            pe.wait_ge(s_e, at(NB * u + kt + 1))
                            nc.tensor.matmul(psO[0:4 * HD, :], VO[r][0:m, kt, :], W[0:m, kt % NW, :],
                                             start=(r == 0 and kt == 0), stop=(r == 1 and kt == NB - 1),
                                             skip_group_check=True).then_inc(s_pv, 1)
                        else:
                            if kt == 0:
                                pe.wait_ge(s_e, at(u + 1))
                            nc.tensor.matmul(psO[0:4 * HD, kt * P:(kt + 1) * P], VO[r][:, kt, :],
                                             W[:, 0, kt * P:(kt + 1) * P],
                                             start=(r == 0 and kt == 0), stop=(r == 1 and kt == NB - 1),
                                             skip_group_check=True).then_inc(s_pv, 1)

                    def step(i, u, r, nxt):
                        for w in range(NT):
                            if nxt is not None and topk:
                                scores(nxt, u + 1, w, 1 - r)
                            if w == 0:
                                maxima(u, r)
                            if not topk:
                                continue
                            for kt in quarter(w):
                                shifted(i, u, r, kt)
                                if kt >= 1:
                                    product(i, u, r, kt - 1)
                        if topk:
                            product(i, u, r, NB - 1)
                            return
                        if nxt is not None:
                            pe.wait_ge(s_top, at(u))
                            for w in range(NT):
                                scores(nxt, u + 1, w, 1 - r)
                        for kt in range(NB):
                            shifted(i, u, r, kt)
                        for kt in range(NB):
                            product(i, u, r, kt)

                    pe.wait_ge(s_set, at(6))
                    for w in range(NT):
                        scores(0, 0, w, 0)
                    with pe.Fori(0, PAIRS - 1) as i:
                        step(i, 2 * i, 0, i)
                        step(i, 2 * i + 1, 1, i + 1)
                    step(PAIRS - 1, 2 * PAIRS - 2, 0, PAIRS - 1)
                    step(PAIRS - 1, 2 * PAIRS - 1, 1, None)

        attention(False, qs_d, ks_d, vs_d, os_d)

        with ExitStack() as s:
            t = norm_buffers(s)
            f = split_buffers(s)
            a = add_buffers(s)
            wso = sbuf(s, "wso", [P, KC, C])
            bso = sbuf(s, "bso", [1, C])
            wq = sbuf(s, "wq", [P, KC, C])
            bq = sbuf(s, "bq", [P, KC])
            bqs = sbuf(s, "bqs", [P, KC])
            oT = sbuf(s, "oT", [P, KC, L])
            s_w, s_bs, s_oT = (sem(s, n) for n in ("s_w", "s_bs", "s_oT"))
            J = KC
            block = s.enter_context(nc.Block())

            @block.sync
            def _(sp):
                set_to_one(sp)
                sp.dma_start(wso[:, :, :], w_so.rearrange("(k p) n -> p k n", p=P)).then_inc(s_w, 16)
                sp.dma_start(bso[:, :], row(b_so)).then_inc(s_w, 16)
                sp.dma_start(wq[:, :, :], w_q.rearrange("(k p) n -> p k n", p=P)).then_inc(s_w, 16)
                sp.dma_start(bq[:, :], column(b_q), allow_slow_non_contiguous=True).then_inc(s_w, 16)
                with sp.Fori(0, B) as b:
                    sp.wait_ge(a["summed"], at(NT * b))
                    sp.dma_start(oT[:, :, :], os_d[bass.ds(b * C, C), :].rearrange("(k p) l -> p k l", p=P)
                                 ).then_inc(s_oT, 16)
                    for j in range(J):
                        split_sync(sp, f, b, J, j, L, qc_d, j, 0)
                for k in range(2):
                    sp.wait_ge(f["parted"][k], at(16 * PARTS * B * J // 2))

            @block.gpsimd
            def _(pool):
                with pool.Fori(0, B) as b:
                    norm_pool(pool, t, b)
                    for j in range(J):
                        split_pool(pool, f, b, J, j, L)

            @block.vector
            def _(dve):
                dve.wait_ge(s_w, at(64))
                nc.vector.tensor_scalar(bqs[:, :], bq[:, :], QSCALE, None, ALU.mult).then_inc(s_bs, 1)
                with dve.Fori(0, B) as b:
                    for w in range(NT):
                        add_vector(dve, a, b, NT, w, w, 0)
                    norm_vector(dve, t, b, a["added"])
                    for j in range(J):
                        split_vector(dve, f, b, J, j, L)

            @block.scalar
            def _(act):
                act.wait_ge(s_bs, at(1))
                with act.Fori(0, B) as b:
                    norm_scalar(act, t, b, 1, f["prod"], J)
                    for j in range(J):
                        split_scalar(act, f, b, J, j, L, bqs[:, j:j + 1], QSCALE)

            @block.tensor
            def _(pe):
                pe.wait_ge(s_w, at(64))
                with pe.Fori(0, B) as b:
                    pe.wait_ge(s_oT, at(16 * (b + 1)))
                    for w in range(NT):
                        add_tensor(pe, a, b, NT, w, bso[:, :], lambda k: oT[:, k, w * P:(w + 1) * P],
                                   lambda k: wso[:, k, :], KC)
                    norm_tensor(pe, t, b)
                    pe.wait_ge(t["hready"], at(KC * (b + 1)))
                    for j in range(J):
                        split_tensor(pe, f, b, J, j, L, lambda k: wq[:, k, j * P:(j + 1) * P],
                                     lambda k: t["hT"][:, k, :])

        attention(True, qc_d, kc_d, vc_d, oc_d)

        with ExitStack() as s:
            t = norm_buffers(s)
            a = add_buffers(s)
            wco = sbuf(s, "wco", [P, KC, C])
            bco = sbuf(s, "bco", [1, C])
            wm1 = sbuf(s, "wm1", [P, KC, 2 * HID])
            bm1 = sbuf(s, "bm1", [P, 2 * HC])
            nbm1 = sbuf(s, "nbm1", [P, HC])
            wm2 = sbuf(s, "wm2", [P, HC, C])
            bm2 = sbuf(s, "bm2", [1, C])
            oT = sbuf(s, "oT", [P, KC, L])
            E = [sbuf(s, f"E{k}", [P, L]) for k in range(2)]
            D = sbuf(s, "D", [P, L])
            R = sbuf(s, "R", [P, L])
            SA = sbuf(s, "SA", [P, L])
            uT = sbuf(s, "uT", [P, HC, L])
            psA = [psum(s, f"psA{k}", [P, L]) for k in range(2)]
            psU = [psum(s, f"psU{k}", [P, L]) for k in range(2)]
            s_w, s_bs, s_oT, s_u, s_ex, s_ch, s_gl, s_out = (
                sem(s, n) for n in ("s_w", "s_bs", "s_oT", "s_u", "s_ex", "s_ch", "s_gl", "s_out"))
            J = 2 * NT
            block = s.enter_context(nc.Block())

            @block.sync
            def _(sp):
                set_to_one(sp)
                sp.dma_start(wco[:, :, :], w_co.rearrange("(k p) n -> p k n", p=P)).then_inc(s_w, 16)
                sp.dma_start(bco[:, :], row(b_co)).then_inc(s_w, 16)
                sp.dma_start(bm2[:, :], row(b_m2)).then_inc(s_w, 16)
                sp.dma_start(bm1[:, :], column(b_m1), allow_slow_non_contiguous=True).then_inc(s_w, 16)
                sp.dma_start(wm1[:, :, :], w_m1.rearrange("(k p) n -> p k n", p=P)).then_inc(s_w, 16)
                sp.dma_start(wm2[:, :, :], w_m2.rearrange("(k p) n -> p k n", p=P)).then_inc(s_w, 16)
                with sp.Fori(0, B) as b:
                    sp.wait_ge(t["stats"], at(NT * b))
                    sp.dma_start(oT[:, :, :], oc_d[bass.ds(b * C, C), :].rearrange("(k p) l -> p k l", p=P)
                                 ).then_inc(s_oT, 16)
                    sp.wait_ge(a["added"], at(J * (b + 1)))
                    ob = out[bass.ds(b, 1), :, :].rearrange("o l c -> (o l) c")
                    sp.dma_start(ob[SHIFT:L - SHIFT, :].rearrange("(t p) c -> p t c", p=P),
                                 xs[:, bass.ds(b, 1), 0:NT - 1, :].rearrange("p o t c -> p (o t) c")).then_inc(s_out, 16)
                    sp.dma_start(ob[L - SHIFT:L, :],
                                 xs[0:SHIFT, bass.ds(b, 1), NT - 1, :].rearrange("p o c -> p (o c)")).then_inc(s_out, 16)
                    sp.dma_start(ob[0:SHIFT, :],
                                 xs[SHIFT:P, bass.ds(b, 1), NT - 1, :].rearrange("p o c -> p (o c)")).then_inc(s_out, 16)
                sp.wait_ge(s_out, at(48 * B))

            @block.gpsimd
            def _(pool):
                with pool.Fori(0, B) as b:
                    norm_pool(pool, t, b)

            @block.vector
            def _(dve):
                dve.wait_ge(s_w, at(96))
                nc.vector.tensor_scalar(nbm1[:, :], bm1[:, 0:HC], -1.0, None, ALU.mult).then_inc(s_bs, 1)
                with dve.Fori(0, B) as b:
                    for w in range(NT):
                        add_vector(dve, a, b, J, w, w, 1)
                    norm_vector(dve, t, b, a["added"], J)
                    dve.wait_ge(a["summed"], at(J * b))
                    for j in range(HC):
                        n = HC * b + j
                        dve.wait_ge(s_ex, at(n + 1))
                        nc.vector.tensor_scalar(D[:, :], E[j % 2][:, :], 1.0, None, ALU.add).then_inc(s_ch, 1)
                        dve.wait_ge(s_ch, at(3 * n + 1))
                        nc.vector.reciprocal(R[:, :], D[:, :]).then_inc(s_ch, 1)
                        dve.wait_ge(s_ch, at(3 * n + 2))
                        nc.vector.scalar_tensor_tensor(out=SA[:, :], in0=psA[j % 2][:, :], scalar=bm1[:, j:j + 1],
                                                       in1=R[:, :], op0=ALU.add, op1=ALU.mult).then_inc(s_ch, 1)
                        dve.wait_ge(s_ch, at(3 * n + 3))
                        nc.vector.scalar_tensor_tensor(out=uT[:, j, :], in0=psU[j % 2][:, :],
                                                       scalar=bm1[:, HC + j:HC + j + 1], in1=SA[:, :],
                                                       op0=ALU.add, op1=ALU.mult).then_inc(s_gl, 1)
                    for w in range(NT):
                        add_vector(dve, a, b, J, NT + w, w, 2)

            @block.scalar
            def _(act):
                act.wait_ge(s_bs, at(1))
                with act.Fori(0, B) as b:
                    norm_scalar(act, t, b, 2, s_u, HC)
                    for j in range(HC):
                        n = HC * b + j
                        act.wait_ge(s_u, at(n + 1))
                        act.wait_ge(s_ch, at(3 * HC * b if j < 2 else 3 * (n - 2) + 1))
                        nc.scalar.activation(E[j % 2][:, :], psA[j % 2][:, :], ACT.Exp, bias=nbm1[:, j:j + 1],
                                             scale=-1.0).then_inc(s_ex, 1)

            @block.tensor
            def _(pe):
                pe.wait_ge(s_w, at(96))
                with pe.Fori(0, B) as b:
                    pe.wait_ge(s_oT, at(16 * (b + 1)))
                    for w in range(NT):
                        add_tensor(pe, a, b, J, w, bco[:, :], lambda k: oT[:, k, w * P:(w + 1) * P],
                                   lambda k: wco[:, k, :], KC)
                    norm_tensor(pe, t, b)
                    pe.wait_ge(t["hready"], at(KC * (b + 1)))
                    for j in range(HC):
                        pe.wait_ge(s_gl, at(HC * b if j < 2 else HC * b + j - 1))
                        for ps, c in ((psA, j * P), (psU, HID + j * P)):
                            for k in range(KC):
                                mm = nc.tensor.matmul(ps[j % 2][:, :], wm1[:, k, c:c + P], t["hT"][:, k, :],
                                                      start=(k == 0), stop=(k == KC - 1))
                        mm.then_inc(s_u, 1)
                    pe.wait_ge(s_gl, at(HC * (b + 1)))
                    for w in range(NT):
                        add_tensor(pe, a, b, J, NT + w, bm2[:, :], lambda k: uT[:, k, w * P:(w + 1) * P],
                                   lambda k: wm2[:, k, :], HC)


_INS = ['x', 'cond_1024', 'ctx_1024', 'L0_xcond_w_ada', 'L0_xcond_b_ada', 'L0_xcond_w_qkv', 'L0_xcond_b_qkv',
        'L0_xcond_w_so', 'L0_xcond_b_so', 'L0_xcond_w_q', 'L0_xcond_b_q', 'L0_xcond_w_kv', 'L0_xcond_b_kv',
        'L0_xcond_w_co', 'L0_xcond_b_co', 'L0_xcond_w_m1', 'L0_xcond_b_m1', 'L0_xcond_w_m2', 'L0_xcond_b_m2']


def kernel(**inputs):
    import numpy as _np
    import concourse.bacc as _bacc
    from concourse import mybir as _mybir
    from concourse.bass_utils import run_bass_kernel_spmd as _run

    nc = _bacc.Bacc("TRN2", target_bir_lowering=False, num_devices=1)
    arrays, args = {}, []
    for name in _INS:
        a = _np.ascontiguousarray(inputs[name])
        arrays[f"in_{name}_dram"] = a
        args.append(nc.dram_tensor(f"in_{name}_dram", a.shape, _mybir.dt.from_np(a.dtype), kind="ExternalInput").ap())
    shape = inputs['x'].shape
    args.append(nc.dram_tensor("out_0_dram", shape, _mybir.dt.from_np(_np.dtype("float32")), kind="ExternalOutput").ap())
    build(nc, *args)
    r = _run(nc, [arrays], core_ids=[0])
    return r.results[0]["out_0_dram"]
```

```python
from contextlib import ExitStack

import concourse.bass as bass
from concourse import mybir

F32 = mybir.dt.float32
BF16 = mybir.dt.bfloat16
ALU = mybir.AluOpType
ACT = mybir.ActivationFunctionType
AX_X = mybir.AxisListType.X

P = 128
HEADS = 16
HD = 16
TOPK = 16
SHIFT = 64
COMBO = 6
PARTS = 3
KROWS = COMBO * HD
BROWS = KROWS + PARTS
LOWEST = -3.4028234663852886e38
BIG = 2.0 ** 100
EPS = 1e-6


def build(nc, x, cond, ctx, w_ada, b_ada, w_qkv, b_qkv, w_so, b_so, w_q, b_q, w_kv, b_kv,
          w_co, b_co, w_m1, b_m1, w_m2, b_m2, out):
    B, L, C = x.shape
    LC = ctx.shape[1]
    HID = w_m2.shape[0]
    KC = C // P
    NT = L // P
    NK = -(-LC // P)
    KLAST = LC - (NK - 1) * P
    U = B * HEADS
    PAIRS = U // 2
    NMOD = w_ada.shape[1] // P
    QSCALE = float(HD) ** -0.5
    HC = HID // P

    with ExitStack() as top:
        used = {}

        def unique(name):
            used[name] = used.get(name, 0) + 1
            return name if used[name] == 1 else f"{name}_{used[name]}"

        def sbuf(stack, name, shape, dt=F32):
            return stack.enter_context(nc.sbuf_tensor(unique(name), shape, dt))

        def psum(stack, name, shape, dt=F32):
            return stack.enter_context(nc.psum_tensor(unique(name), shape, dt))

        fresh = []

        def sem(stack, name):
            fresh.append(stack.enter_context(nc.semaphore(unique(name))))
            return fresh[-1]

        def set_to_one(eng):
            for s in fresh:
                eng.sem_inc(s, 1)
            fresh.clear()

        def at(count):
            return count + 1

        s_held = top.enter_context(nc.semaphore("s_held"))

        qs_d = nc.dram_tensor("qs_d", [PARTS, U * HD, L], BF16)
        ks_d = nc.dram_tensor("ks_d", [PARTS, U * HD, L], BF16)
        vs_d = nc.dram_tensor("vs_d", [U, P, NT * HD], F32)
        qc_d = nc.dram_tensor("qc_d", [PARTS, U * HD, L], BF16)
        kc_d = nc.dram_tensor("kc_d", [PARTS, U * HD, LC], BF16)
        vc_d = nc.dram_tensor("vc_d", [U, P, NK * HD], F32)
        os_d = nc.dram_tensor("os_d", [2, U * HD, L], F32)
        oc_d = nc.dram_tensor("oc_d", [2, U * HD, L], F32)

        xs = sbuf(top, "xs", [P, B, NT, C])
        ident = sbuf(top, "ident", [P, P])
        identb = sbuf(top, "identb", [P, P], BF16)
        negbig = sbuf(top, "negbig", [P, P], BF16)
        ones = sbuf(top, "ones", [P, P])
        modT = sbuf(top, "modT", [P, NMOD, B])
        gate = sbuf(top, "gate", [P, 3, B, C])
        mhalf = sbuf(top, "mhalf", [P, NT])

        with ExitStack() as s:
            wa = sbuf(s, "wa", [P, KC, NMOD * P])
            bac = sbuf(s, "bac", [P, NMOD])
            bar = sbuf(s, "bar", [1, NMOD * P])
            condT = sbuf(s, "condT", [P, KC, B])
            e = sbuf(s, "e", [P, KC, B])
            d = sbuf(s, "d", [P, KC, B])
            rd = sbuf(s, "rd", [P, KC, B])
            sl = sbuf(s, "sl", [P, KC, B])
            slb = sbuf(s, "slb", [P, KC, B, P])
            psM = psum(s, "psM", [P, 512 // B, B])
            psG = [psum(s, f"psG{k}", [P, 512]) for k in range(2)]
            s_x, s_w, s_e, s_d, s_slb = (sem(s, n) for n in ("s_x", "s_w", "s_e", "s_d", "s_slb"))
            s_one, s_id, s_m, s_mc, s_g, s_gc = (sem(s, n) for n in
                                                 ("s_one", "s_id", "s_m", "s_mc", "s_g", "s_gc"))
            block = s.enter_context(nc.Block())

            @block.sync
            def _(sp):
                set_to_one(sp)
                for k in range(KC):
                    sp.dma_start(condT[:, k, :], cond[:, k * P:(k + 1) * P].rearrange("b p -> p b"),
                                 allow_slow_non_contiguous=True).then_inc(s_w, 16)
                sp.dma_start(bac[:, :], b_ada.rearrange("(n p) -> p n", p=P),
                             allow_slow_non_contiguous=True).then_inc(s_w, 16)
                sp.dma_start(bar[:, :], b_ada.rearrange("(o n) -> o n", o=1)).then_inc(s_w, 16)
                sp.dma_start(wa[:, :, :], w_ada.rearrange("(k p) n -> p k n", p=P)).then_inc(s_w, 16)
                for b in range(B):
                    sp.dma_start(xs[:, b, 0:NT - 1, :],
                                 x[b, SHIFT:L - SHIFT, :].rearrange("(t p) c -> p t c", p=P)).then_inc(s_x, 16)
                    sp.dma_start(xs[0:SHIFT, b, NT - 1, :], x[b, L - SHIFT:L, :]).then_inc(s_x, 16)
                    sp.dma_start(xs[SHIFT:P, b, NT - 1, :], x[b, 0:SHIFT, :]).then_inc(s_x, 16)
                sp.wait_ge(s_x, at(48 * B))

            @block.gpsimd
            def _(pool):
                nc.gpsimd.memset(ident[:, :], 0.0).then_inc(s_id, 1)
                nc.gpsimd.memset(mhalf[:, :], -0.5)
                pool.wait_ge(s_id, at(1))
                nc.gpsimd.affine_select(out=ident[:, :], in_=ident[:, :], compare_op=ALU.not_equal,
                                        fill=1.0, base=0, pattern=[[-1, P]],
                                        channel_multiplier=1).then_inc(s_id, 1)
                pool.wait_ge(s_id, at(2))
                nc.gpsimd.tensor_copy(identb[:, :], ident[:, :]).then_inc(s_id, 1)
                nc.gpsimd.tensor_scalar(negbig[:, :], ident[:, :], -BIG, None, ALU.mult).then_inc(s_id, 1)

            @block.scalar
            def _(act):
                act.wait_ge(s_w, at(16 * (KC + 3)))
                nc.scalar.activation(e[:, :, :], condT[:, :, :], ACT.Exp, scale=-1.0).then_inc(s_e, 1)

            @block.vector
            def _(dve):
                nc.vector.memset(ones[:, :], 1.0).then_inc(s_one, 1)
                dve.wait_ge(s_e, at(1))
                nc.vector.tensor_scalar(d[:, :, :], e[:, :, :], 1.0, None, ALU.add).then_inc(s_d, 1)
                dve.wait_ge(s_d, at(1))
                nc.vector.reciprocal(rd[:, :, :], d[:, :, :]).then_inc(s_d, 1)
                dve.wait_ge(s_d, at(2))
                nc.vector.tensor_tensor(sl[:, :, :], condT[:, :, :], rd[:, :, :], ALU.mult).then_inc(s_d, 1)
                dve.wait_ge(s_d, at(3))
                dve.wait_ge(s_one, at(1))
                for k in range(KC):
                    for b in range(B):
                        nc.vector.tensor_scalar(slb[:, k, b, :], ones[:, :], sl[:, k, b:b + 1], None,
                                                ALU.mult).then_inc(s_slb, 1)
                dve.wait_ge(s_m, at(1))
                for b in range(B):
                    nc.vector.tensor_tensor(modT[:, :, b], psM[:, 0:NMOD, b], bac[:, :], ALU.add).then_inc(s_mc, 1)
                dve.wait_ge(s_mc, at(B))
                for part in (1, 4, 7):
                    m = modT[:, part * KC:(part + 1) * KC, :]
                    nc.vector.tensor_scalar(m, m, 1.0, None, ALU.add).then_inc(s_mc, 1)
                for n in range(3 * B):
                    dve.wait_ge(s_g, at(n + 1))
                    nc.vector.tensor_copy(gate[:, n // B, n % B, :], psG[n % 2][:, 0:C]).then_inc(s_gc, 1)

            @block.tensor
            def _(pe):
                pe.wait_ge(s_d, at(3))
                for n in range(NMOD):
                    for k in range(KC):
                        mm = nc.tensor.matmul(psM[:, n, :], wa[:, k, n * P:(n + 1) * P], sl[:, k, :],
                                              start=(k == 0), stop=(k == KC - 1))
                mm.then_inc(s_m, 1)
                pe.wait_ge(s_slb, at(KC * B))
                for n in range(3 * B):
                    g, b = n // B, n % B
                    cols = slice((3 * g + 2) * C, (3 * g + 3) * C)
                    if n >= 2:
                        pe.wait_ge(s_gc, at(n - 1))
                    nc.tensor.matmul(psG[n % 2][:, 0:C], ones[0:1, :], bar[:, cols], start=True, stop=False)
                    for k in range(KC):
                        mm = nc.tensor.matmul(psG[n % 2][:, 0:C], slb[:, k, b, :], wa[:, k, cols],
                                              start=False, stop=(k == KC - 1))
                    mm.then_inc(s_g, 1)

        def norm_buffers(s):
            t = {}
            t["st"] = sbuf(s, "st", [P, NT, 6])
            t["mv"] = sbuf(s, "mv", [P, NT, 2])
            t["ve"] = sbuf(s, "ve", [P, NT])
            t["rs"] = sbuf(s, "rs", [P, NT])
            t["xn"] = sbuf(s, "xn", [P, NT, C])
            t["hT"] = sbuf(s, "hT", [P, KC, L])
            t["psX"] = [psum(s, f"psX{k}", [P, L]) for k in range(KC)]
            for n in ("stats", "aggr", "var", "rstd", "xnorm", "turned", "hready"):
                t[n] = sem(s, "s_" + n)
            return t

        def norm_vector(dve, t, b, added=None, adds=NT):
            for w in range(NT):
                if added is not None:
                    dve.wait_ge(added, at(adds * b + w + 1))
                    dve.sem_inc(s_held, 1)
                nc.vector.bn_stats(t["st"][:, w, :], xs[:, b, w, :]).then_inc(t["stats"], 1)
            for w in range(NT):
                dve.wait_ge(t["stats"], at(NT * b + w + 1))
                dve.sem_inc(s_held, 1)
                nc.vector.bn_aggr(t["mv"][:, w, :], t["st"][:, w, :]).then_inc(t["aggr"], 1)
            dve.wait_ge(t["rstd"], at(b + 1))
            dve.wait_ge(t["turned"], at(KC * NT * b))
            for w in range(NT):
                nc.vector.tensor_scalar(t["xn"][:, w, :], xs[:, b, w, :], t["mv"][:, w, 0:1],
                                        t["rs"][:, w:w + 1], ALU.subtract, ALU.mult).then_inc(t["xnorm"], 1)

        def norm_pool(pool, t, b):
            pool.wait_ge(t["aggr"], at(NT * (b + 1)))
            pool.wait_ge(t["xnorm"], at(NT * b))
            pool.sem_inc(s_held, 1)
            nc.gpsimd.tensor_scalar(t["ve"][:, :], t["mv"][:, :, 1], EPS, None, ALU.add).then_inc(t["var"], 1)
            pool.wait_ge(t["var"], at(b + 1))
            nc.gpsimd.tensor_tensor(t["rs"][:, :], t["ve"][:, :], mhalf[:, :], ALU.pow).then_inc(t["rstd"], 1)

        def norm_tensor(pe, t, b):
            pe.wait_ge(t["hready"], at(KC * b))
            for w in range(NT):
                pe.wait_ge(t["xnorm"], at(NT * b + w + 1))
                for k in range(KC):
                    nc.tensor.transpose(t["psX"][k][:, w * P:(w + 1) * P], t["xn"][:, w, k * P:(k + 1) * P],
                                        ident[:, :]).then_inc(t["turned"], 1)

        def norm_scalar(act, t, b, which, used, uses):
            act.wait_ge(t["turned"], at(KC * NT * (b + 1)))
            act.wait_ge(used, at(uses * b))
            for k in range(KC):
                nc.scalar.activation(t["hT"][:, k, :], t["psX"][k][:, :], ACT.Identity,
                                     bias=modT[:, (3 * which) * KC + k, bass.ds(b, 1)],
                                     scale=modT[:, (3 * which + 1) * KC + k, bass.ds(b, 1)]).then_inc(t["hready"], 1)

        def split_buffers(s):
            t = {"psP": [psum(s, f"psP{k}", [P, L]) for k in range(2)],
                 "T": [sbuf(s, f"T{k}", [P, L]) for k in range(2)],
                 "R": [sbuf(s, f"R{k}", [P, L]) for k in range(2)],
                 "Pt": [sbuf(s, f"Pt{k}", [P, PARTS, L], BF16) for k in range(2)]}
            for n in ("prod", "biased", "part1", "rest", "part2", "part3"):
                t[n] = sem(s, "s_" + n)
            t["parted"] = [sem(s, f"s_parted{k}") for k in range(2)]
            return t

        def split_tensor(pe, t, b, J, j, n, lhs, rhs):
            pe.wait_ge(t["biased"], at(J * b if j < 2 else J * b + j - 1))
            for k in range(KC):
                mm = nc.tensor.matmul(t["psP"][j % 2][:, 0:n], lhs(k), rhs(k), start=(k == 0), stop=(k == KC - 1))
            mm.then_inc(t["prod"], 1)

        def split_scalar(act, t, b, J, j, n, bias, scale):
            act.wait_ge(t["prod"], at(J * b + j + 1))
            act.wait_ge(t["rest"], at(J * b if j < 2 else J * b + j - 1))
            nc.scalar.activation(t["T"][j % 2][:, 0:n], t["psP"][j % 2][:, 0:n], ACT.Identity,
                                 bias=bias, scale=scale).then_inc(t["biased"], 1)

        def split_vector(dve, t, b, J, j, n):
            T, R, Pt = t["T"][j % 2], t["R"][j % 2], t["Pt"][j % 2]
            g = J * b + j
            dve.wait_ge(t["biased"], at(g + 1))
            dve.wait_ge(t["parted"][j % 2], at(16 * PARTS * (J // 2 * b + j // 2)))
            nc.vector.tensor_copy(Pt[:, 0, 0:n], T[:, 0:n]).then_inc(t["part1"], 1)
            dve.wait_ge(t["part1"], at(g + 1))
            dve.wait_ge(t["part3"], at(J * b if j < 2 else g - 1))
            nc.vector.tensor_tensor(R[:, 0:n], T[:, 0:n], Pt[:, 0, 0:n], ALU.subtract).then_inc(t["rest"], 1)
            dve.wait_ge(t["rest"], at(g + 1))
            nc.vector.tensor_copy(Pt[:, 1, 0:n], R[:, 0:n]).then_inc(t["part2"], 1)

        def split_pool(pool, t, b, J, j, n):
            R, Pt = t["R"][j % 2], t["Pt"][j % 2]
            pool.wait_ge(t["part2"], at(J * b + j + 1))
            nc.gpsimd.tensor_tensor(Pt[:, 2, 0:n], R[:, 0:n], Pt[:, 1, 0:n], ALU.subtract).then_inc(t["part3"], 1)

        def split_sync(sp, t, b, J, j, n, dram, chunk, c0):
            sp.wait_ge(t["part3"], at(J * b + j + 1))
            sp.sem_inc(s_held, 1)
            for a in range(PARTS):
                sp.dma_start(dram[a, bass.ds(b * C + chunk * P, P), c0:c0 + n],
                             t["Pt"][j % 2][:, a, 0:n]).then_inc(t["parted"][j % 2], 16)

        def add_buffers(s):
            t = {"psV": [psum(s, f"psV{k}", [P, 512]) for k in range(2)],
                 "tmp": [sbuf(s, f"tmp{k}", [P, C]) for k in range(2)]}
            for n in ("summed", "gated", "added"):
                t[n] = sem(s, "s_" + n)
            return t

        def add_tensor(pe, t, b, J, j, bias, lhs, rhs, chunks):
            pe.wait_ge(t["gated"], at(J * b if j < 2 else J * b + j - 1))
            ps = t["psV"][j % 2][:, 0:C]
            nc.tensor.matmul(ps, ones[0:1, :], bias, start=True, stop=False)
            for k in range(chunks):
                mm = nc.tensor.matmul(ps, lhs(k), rhs(k), start=False, stop=(k == chunks - 1))
            mm.then_inc(t["summed"], 1)

        def add_vector(dve, t, b, J, j, w, which):
            dve.wait_ge(t["summed"], at(J * b + j + 1))
            dve.wait_ge(t["added"], at(J * b if j < 2 else J * b + j - 1))
            nc.vector.tensor_tensor(t["tmp"][j % 2][:, :], t["psV"][j % 2][:, 0:C],
                                    gate[:, which, bass.ds(b, 1), :], ALU.mult).then_inc(t["gated"], 1)
            dve.wait_ge(t["gated"], at(J * b + j + 1))
            xt = xs[:, b, w, :]
            nc.vector.tensor_tensor(xt, xt, t["tmp"][j % 2][:, :], ALU.add).then_inc(t["added"], 1)

        def divide(dve, b, s_oT, s_norm, oT, oU, oL, oR):
            dve.wait_ge(s_oT, at(32 * (b + 1)))
            nc.vector.reciprocal(oR[:, :, :], oL[:, :, :]).then_inc(s_norm, 1)
            dve.wait_ge(s_norm, at(2 * b + 1))
            nc.vector.tensor_tensor(oT[:, :, :], oU[:, :, :], oR[:, :, :], ALU.mult).then_inc(s_norm, 1)

        def head_major(ap):
            return ap.rearrange("p (h d) -> p h d", d=HD)

        def column(v):
            return v.rearrange("(n p) -> p n", p=P)

        def row(v):
            return v.rearrange("(o n) -> o n", o=1)

        with ExitStack() as s:
            t = norm_buffers(s)
            f = split_buffers(s)
            wqkv = sbuf(s, "wqkv", [P, KC, 3 * C])
            bqk = sbuf(s, "bqk", [P, 2 * KC])
            bqks = sbuf(s, "bqks", [P, 2 * KC])
            bv = sbuf(s, "bv", [1, C])
            vh = sbuf(s, "vh", [P, HEADS, NT, HD])
            psV = [psum(s, f"psV{k}", [P, 512]) for k in range(2)]
            s_w, s_bs, s_v, s_vc, s_vd = (sem(s, n) for n in ("s_w", "s_bs", "s_v", "s_vc", "s_vd"))
            J = 2 * KC
            block = s.enter_context(nc.Block())

            @block.sync
            def _(sp):
                set_to_one(sp)
                sp.dma_start(wqkv[:, :, :], w_qkv.rearrange("(k p) n -> p k n", p=P)).then_inc(s_w, 16)
                sp.dma_start(bqk[:, :], column(b_qkv[0:2 * C]), allow_slow_non_contiguous=True).then_inc(s_w, 16)
                sp.dma_start(bv[:, :], row(b_qkv[2 * C:3 * C])).then_inc(s_w, 16)
                with sp.Fori(0, B) as b:
                    for j in range(J):
                        split_sync(sp, f, b, J, j, L, qs_d if j < KC else ks_d, j % KC, 0)
                    sp.wait_ge(s_vc, at(NT * (b + 1)))
                    sp.dma_start(vs_d[bass.ds(b * HEADS, HEADS), :, :].rearrange("h p n -> p h n"),
                                 vh[:, :, :, :].rearrange("p h w d -> p h (w d)")).then_inc(s_vd, 16)
                for k in range(2):
                    sp.wait_ge(f["parted"][k], at(16 * PARTS * B * J // 2))
                sp.wait_ge(s_vd, at(16 * B))

            @block.gpsimd
            def _(pool):
                with pool.Fori(0, B) as b:
                    norm_pool(pool, t, b)
                    for j in range(J):
                        split_pool(pool, f, b, J, j, L)

            @block.vector
            def _(dve):
                dve.wait_ge(s_w, at(48))
                nc.vector.tensor_scalar(bqks[:, 0:KC], bqk[:, 0:KC], QSCALE, None, ALU.mult).then_inc(s_bs, 1)
                nc.vector.tensor_copy(bqks[:, KC:2 * KC], bqk[:, KC:2 * KC]).then_inc(s_bs, 1)
                with dve.Fori(0, B) as b:
                    norm_vector(dve, t, b)
                    for j in range(J):
                        split_vector(dve, f, b, J, j, L)

            @block.scalar
            def _(act):
                act.wait_ge(s_bs, at(2))
                with act.Fori(0, B) as b:
                    norm_scalar(act, t, b, 0, s_v, NT)
                    for j in range(J):
                        split_scalar(act, f, b, J, j, L, bqks[:, j:j + 1], QSCALE if j < KC else 1.0)
                    act.wait_ge(s_vd, at(16 * b))
                    for w in range(NT):
                        act.wait_ge(s_v, at(NT * b + w + 1))
                        nc.scalar.copy(vh[:, :, w, :], head_major(psV[w % 2][:, 0:C])).then_inc(s_vc, 1)

            @block.tensor
            def _(pe):
                pe.wait_ge(s_w, at(48))
                with pe.Fori(0, B) as b:
                    norm_tensor(pe, t, b)
                    pe.wait_ge(t["hready"], at(KC * (b + 1)))
                    for j in range(J):
                        split_tensor(pe, f, b, J, j, L, lambda k: wqkv[:, k, j * P:(j + 1) * P],
                                     lambda k: t["hT"][:, k, :])
                    for w in range(NT):
                        pe.wait_ge(s_vc, at(NT * b if w < 2 else NT * b + w - 1))
                        nc.tensor.matmul(psV[w % 2][:, 0:C], ones[0:1, :], bv[:, :], start=True, stop=False)
                        for k in range(KC):
                            mm = nc.tensor.matmul(psV[w % 2][:, 0:C], t["hT"][:, k, w * P:(w + 1) * P],
                                                  wqkv[:, k, 2 * C:3 * C], start=False, stop=(k == KC - 1))
                        mm.then_inc(s_v, 1)

        with ExitStack() as s:
            f = split_buffers(s)
            wkv = sbuf(s, "wkv", [P, KC, 2 * C])
            bk = sbuf(s, "bk", [P, KC])
            bv = sbuf(s, "bv", [1, C])
            cs = sbuf(s, "cs", [P, NK, C])
            cT = sbuf(s, "cT", [P, KC, NK * P])
            vh = sbuf(s, "vh", [P, HEADS, NK, HD])
            psX = [psum(s, f"psX{k}", [P, 512]) for k in range(KC)]
            psV = [psum(s, f"psV{k}", [P, 512]) for k in range(2)]
            s_w, s_z, s_v, s_vc, s_vd = (sem(s, n) for n in ("s_w", "s_z", "s_v", "s_vc", "s_vd"))
            s_c, s_turned, s_ct = (sem(s, n) for n in ("s_c", "s_turned", "s_ct"))
            GT = 512 // P
            NG = -(-NK // GT)
            J = KC * NG
            gw = [min(GT * P, LC - g * GT * P) for g in range(NG)]
            rows = [min(P, LC - kt * P) for kt in range(NK)]
            block = s.enter_context(nc.Block())

            @block.sync
            def _(sp):
                set_to_one(sp)
                sp.dma_start(wkv[:, :, :], w_kv.rearrange("(k p) n -> p k n", p=P)).then_inc(s_w, 16)
                sp.dma_start(bk[:, :], column(b_kv[0:C]), allow_slow_non_contiguous=True).then_inc(s_w, 16)
                sp.dma_start(bv[:, :], row(b_kv[C:2 * C])).then_inc(s_w, 16)
                with sp.Fori(0, B) as b:
                    sp.wait_ge(s_turned, at(KC * NG * b))
                    cb = ctx[bass.ds(b, 1), :, :].rearrange("o r c -> (o r) c")
                    sp.dma_start(cs[:, 0:NK - 1, :],
                                 cb[0:(NK - 1) * P, :].rearrange("(t p) c -> p t c", p=P)).then_inc(s_c, 16)
                    sp.dma_start(cs[0:KLAST, NK - 1, :], cb[(NK - 1) * P:LC, :]).then_inc(s_c, 16)
                    for j in range(J):
                        split_sync(sp, f, b, J, j, gw[j // KC], kc_d, j % KC, (j // KC) * GT * P)
                    sp.wait_ge(s_vc, at(NK * (b + 1)))
                    sp.dma_start(vc_d[bass.ds(b * HEADS, HEADS), :, :].rearrange("h p n -> p h n"),
                                 vh[:, :, :, :].rearrange("p h w d -> p h (w d)")).then_inc(s_vd, 16)
                for k in range(2):
                    sp.wait_ge(f["parted"][k], at(16 * PARTS * B * J // 2))
                sp.wait_ge(s_vd, at(16 * B))

            @block.gpsimd
            def _(pool):
                nc.gpsimd.memset(vh[KLAST // 32 * 32:P, :, NK - 1, :], 0.0).then_inc(s_z, 1)
                pool.wait_ge(s_z, at(1))
                with pool.Fori(0, B) as b:
                    for j in range(J):
                        split_pool(pool, f, b, J, j, gw[j // KC])

            @block.vector
            def _(dve):
                with dve.Fori(0, B) as b:
                    dve.wait_ge(s_v, at(NK * b))
                    for g in range(NG):
                        for k in range(KC):
                            dve.wait_ge(s_turned, at(KC * NG * b + KC * g + k + 1))
                            nc.vector.tensor_copy(cT[:, k, g * GT * P:g * GT * P + gw[g]],
                                                  psX[k][:, 0:gw[g]]).then_inc(s_ct, 1)
                    for j in range(J):
                        split_vector(dve, f, b, J, j, gw[j // KC])

            @block.scalar
            def _(act):
                act.wait_ge(s_w, at(48))
                act.wait_ge(s_z, at(1))
                with act.Fori(0, B) as b:
                    for j in range(J):
                        split_scalar(act, f, b, J, j, gw[j // KC], bk[:, j % KC:j % KC + 1], 1.0)
                    act.wait_ge(s_vd, at(16 * b))
                    for kt in range(NK):
                        act.wait_ge(s_v, at(NK * b + kt + 1))
                        nc.scalar.copy(vh[0:rows[kt], :, kt, :],
                                       head_major(psV[kt % 2][0:rows[kt], 0:C])).then_inc(s_vc, 1)

            @block.tensor
            def _(pe):
                pe.wait_ge(s_w, at(48))
                with pe.Fori(0, B) as b:
                    pe.wait_ge(s_c, at(32 * (b + 1)))
                    for g in range(NG):
                        for k in range(KC):
                            pe.wait_ge(s_ct, at(J * b if g == 0 else J * b + KC * (g - 1) + k + 1))
                            for kt in range(g * GT, min(NK, (g + 1) * GT)):
                                r = rows[kt]
                                tr = nc.tensor.transpose(psX[k][:, (kt - g * GT) * P:(kt - g * GT) * P + r],
                                                         cs[0:r, kt, k * P:(k + 1) * P], ident[0:r, 0:r])
                            tr.then_inc(s_turned, 1)
                    for j in range(J):
                        g = j // KC
                        pe.wait_ge(s_ct, at(J * b + KC * (g + 1)))
                        split_tensor(pe, f, b, J, j, gw[g], lambda k: wkv[:, k, (j % KC) * P:(j % KC + 1) * P],
                                     lambda k: cT[:, k, g * GT * P:g * GT * P + gw[g]])
                    for kt in range(NK):
                        r = rows[kt]
                        pe.wait_ge(s_vc, at(NK * b if kt < 2 else NK * b + kt - 1))
                        nc.tensor.matmul(psV[kt % 2][0:r, 0:C], ones[0:1, 0:r], bv[:, :], start=True, stop=False)
                        for k in range(KC):
                            mm = nc.tensor.matmul(psV[kt % 2][0:r, 0:C], cT[:, k, kt * P:kt * P + r],
                                                  wkv[:, k, C:2 * C], start=False, stop=(k == KC - 1))
                        mm.then_inc(s_v, 1)

        KPART = [0, 1, 2, 0, 1, 0]
        QPART = [0, 0, 0, 1, 1, 2]

        def parts_of_minus(pool, s_chain, n0, m, nm, r1, mp):
            for n in range(5):
                pool.wait_ge(s_chain, at(n0 + n))
                if n == 0:
                    pool.sem_inc(s_held, 1)
                    ins = nc.gpsimd.tensor_scalar(nm, m, -1.0, None, ALU.mult)
                elif n == 1:
                    pool.sem_inc(s_held, 1)
                    ins = nc.gpsimd.tensor_copy(mp[0], nm)
                elif n == 2:
                    ins = nc.gpsimd.tensor_tensor(r1, nm, mp[0], ALU.subtract)
                elif n == 3:
                    pool.sem_inc(s_held, 1)
                    ins = nc.gpsimd.tensor_copy(mp[1], r1)
                else:
                    ins = nc.gpsimd.tensor_tensor(mp[2], r1, mp[1], ALU.subtract)
                ins.then_inc(s_chain, 1)

        def set_ones(dve, s_set, Ks, VOs, beside_v):
            for K in Ks:
                nc.vector.memset(K[KROWS:P, :], 1.0).then_inc(s_set, 1)
            for VO in VOs:
                nc.vector.memset(VO, 0.0).then_inc(s_set, 1)
            dve.wait_ge(s_set, at(len(Ks) + len(VOs)))
            for v in beside_v:
                nc.vector.memset(v, 1.0).then_inc(s_set, 1)

        with ExitStack() as s:
            G = 4
            NG = U // G
            LOADS = 2 * COMBO + 1
            Q = [sbuf(s, f"Q{y}", [P, G * L], BF16) for y in range(2)]
            K = [sbuf(s, f"K{y}", [P, G * L], BF16) for y in range(2)]
            V = [sbuf(s, f"V{y}", [P, G, NT * HD]) for y in range(2)]
            VO = [sbuf(s, f"VO{y}", [P, G * NT, 4 * HD]) for y in range(2)]
            W = sbuf(s, "W", [P, 2, L])
            OL = [sbuf(s, f"OL{y}", [4 * HD, L]) for y in range(2)]
            mx = [sbuf(s, f"mx{y}", [P, G * NT]) for y in range(2)]
            nm = sbuf(s, "nm", [P, G * NT])
            r1 = sbuf(s, "r1", [P, G * NT])
            mp = [sbuf(s, f"mp{y}", [P, G * NT, PARTS], BF16) for y in range(2)]
            psS = [psum(s, f"psS{y}", [P, L]) for y in range(2)]
            psT = psum(s, "psT", [P, G * L], BF16)
            psB = [psum(s, f"psB{y}", [P, L]) for y in range(2)]
            psO = [psum(s, f"psO{y}", [P, L]) for y in range(2)]
            s_ld = [sem(s, f"s_ld{y}") for y in range(2)]
            s_st = [sem(s, f"s_st{r}") for r in range(G // 2)]
            (s_set, s_vo, s_sc, s_mx, s_chain, s_mt, s_qb, s_b, s_e, s_pv, s_ol) = (
                sem(s, n) for n in ("s_set", "s_vo", "s_sc", "s_mx", "s_chain", "s_mt", "s_qb", "s_b", "s_e",
                                    "s_pv", "s_ol"))
            block = s.enter_context(nc.Block())

            def groups(eng, body):
                with eng.Fori(0, NG // 2 - 1) as i:
                    body(2 * i, 0, True)
                    body(2 * i + 1, 1, True)
                body(NG - 2, 0, True)
                body(NG - 1, 1, False)

            @block.sync
            def _(sp):
                set_to_one(sp)

                def load(g, y):
                    for c in range(COMBO):
                        sp.dma_start(Q[y][c * HD:(c + 1) * HD, :].rearrange("d (u l) -> d u l", l=L),
                                     qs_d[QPART[c], bass.ds(g * (G * HD), G * HD), :]
                                     .rearrange("(u d) l -> d u l", d=HD)).then_inc(s_ld[y], 16)
                        sp.dma_start(K[y][c * HD:(c + 1) * HD, :].rearrange("d (u l) -> d u l", l=L),
                                     ks_d[KPART[c], bass.ds(g * (G * HD), G * HD), :]
                                     .rearrange("(u d) l -> d u l", d=HD)).then_inc(s_ld[y], 16)
                    sp.dma_start(V[y][:, :, :], vs_d[bass.ds(g * G, G), :, :].rearrange("u p n -> p u n")
                                 ).then_inc(s_ld[y], 16)

                def body(g, y, more):
                    for r in range(G // 2):
                        n = g * 2 + r
                        sp.wait_ge(s_ol, at(n + 1))
                        sp.sem_inc(s_held, 1)
                        for z in range(2):
                            sp.dma_start(os_d[z, bass.ds(n * 2 * HD, 2 * HD), :],
                                         OL[r][z * 2 * HD:(z + 1) * 2 * HD, :]).then_inc(s_st[r], 16)

                load(0, 0)
                load(1, 1)
                with sp.Fori(0, NG // 2 - 1) as i:
                    body(2 * i, 0, True)
                    load(2 * i + 2, 0)
                    body(2 * i + 1, 1, True)
                    load(2 * i + 3, 1)
                body(NG - 2, 0, True)
                body(NG - 1, 1, False)
                for r in range(G // 2):
                    sp.wait_ge(s_st[r], at(32 * NG))

            @block.gpsimd
            def _(pool):
                def front(g, i, y):
                    pool.wait_ge(s_ld[y], at(16 * LOADS * (i + 1)))
                    pool.sem_inc(s_held, 1)
                    for r in range(2):
                        vo = VO[y][:, :, :].rearrange("p (u w) n -> p u w n", w=NT)[:, r:G:2, :, r * HD:(r + 1) * HD]
                        v = V[y][:, r:G:2, :].rearrange("p u (w d) -> p u w d", d=HD)
                        nc.gpsimd.tensor_copy(vo, v).then_inc(s_vo, 1)
                    pool.wait_ge(s_mx, at(G * (g + 1)))
                    parts_of_minus(pool, s_chain, 5 * g, mx[y][:, :], nm[:, :], r1[:, :],
                                   [mp[y][:, :, a] for a in range(PARTS)])

                pool.wait_ge(s_set, at(8))
                front(0, 0, 0)
                with pool.Fori(0, NG // 2 - 1) as i:
                    front(2 * i + 1, i, 1)
                    front(2 * i + 2, i + 1, 0)
                front(NG - 1, NG // 2 - 1, 1)

            @block.vector
            def _(dve):
                beside_v = [(VO[y][:, :, :].rearrange("p (u w) n -> p u w n", w=NT)[:, r:G:2, :, :], 2 + r)
                            for y in range(2) for r in range(2)]
                set_ones(dve, s_set, K, [VO[y][:, :, :] for y in range(2)],
                         [v[:, :, :, c * HD:(c + 1) * HD] for v, c in beside_v])

                def front(g, y):
                    for j in range(G):
                        dve.wait_ge(s_sc, at(G * g + j + 1))
                        nc.vector.tensor_reduce(mx[y][:, j * NT:(j + 1) * NT],
                                                psS[j % 2][:, :].rearrange("p (w k) -> p w k", k=P),
                                                AX_X, ALU.max).then_inc(s_mx, 1)

                front(0, 0)
                with dve.Fori(0, NG // 2 - 1) as i:
                    front(2 * i + 1, 1)
                    dve.wait_ge(s_chain, at(5 * (2 * i + 1)))
                    front(2 * i + 2, 0)
                    dve.wait_ge(s_chain, at(5 * (2 * i + 2)))
                front(NG - 1, 1)

            @block.scalar
            def _(act):
                def body(g, y, more):
                    act.wait_ge(s_mt, at(g + 1))
                    nc.scalar.copy(Q[y][KROWS:BROWS, :], psT[0:PARTS, :]).then_inc(s_qb, 1)
                    for j in range(G):
                        n = g * G + j
                        act.wait_ge(s_pv, at(G * g if j < 2 else n - 1))
                        act.wait_ge(s_b, at(n + 1))
                        nc.scalar.activation(W[:, j % 2, :], psB[j % 2][:, :], ACT.Exp).then_inc(s_e, 1)
                        if j % 2:
                            r = j // 2
                            act.wait_ge(s_pv, at(n + 1))
                            act.wait_ge(s_st[r], at(32 * g))
                            nc.scalar.copy(OL[r][:, :], psO[r][0:4 * HD, :]).then_inc(s_ol, 1)

                groups(act, body)

            @block.tensor
            def _(pe):
                def scores(g, i, y, j):
                    if j == 0:
                        pe.wait_ge(s_ld[y], at(16 * LOADS * (i + 1)))
                    pe.wait_ge(s_mx, at(G * g if j < 2 else G * g + j - 1))
                    for w in range(NT):
                        c = slice(j * L + w * P, j * L + (w + 1) * P)
                        mm = nc.tensor.matmul(psS[j % 2][:, w * P:(w + 1) * P], Q[y][0:KROWS, c], K[y][0:KROWS, c],
                                              start=True, stop=True)
                    mm.then_inc(s_sc, 1)

                def maxima(g, y):
                    pe.wait_ge(s_chain, at(5 * (g + 1)))
                    for w in range(G * NT):
                        tr = nc.tensor.transpose(psT[0:PARTS, w * P:(w + 1) * P], mp[y][:, w, :], identb[:, :])
                    tr.then_inc(s_mt, 1)

                def shifted(g, y, j):
                    if j == 0:
                        pe.wait_ge(s_qb, at(g + 1))
                    n = g * G + j
                    pe.wait_ge(s_e, at(G * g if j < 2 else n - 1))
                    for w in range(NT):
                        c = slice(j * L + w * P, j * L + (w + 1) * P)
                        mm = nc.tensor.matmul(psB[j % 2][:, w * P:(w + 1) * P], K[y][0:BROWS, c], Q[y][0:BROWS, c],
                                              start=True, stop=True)
                    mm.then_inc(s_b, 1)

                def product(g, y, j):
                    n = g * G + j
                    if j == 0:
                        pe.wait_ge(s_vo, at(2 * (g + 1)))
                    if j % 2 == 0:
                        pe.wait_ge(s_ol, at(2 * g))
                    pe.wait_ge(s_e, at(n + 1))
                    for w in range(NT):
                        mm = nc.tensor.matmul(psO[j // 2][0:4 * HD, w * P:(w + 1) * P], VO[y][:, j * NT + w, :],
                                              W[:, j % 2, w * P:(w + 1) * P],
                                              start=(j % 2 == 0 and w == 0), stop=(j % 2 == 1 and w == NT - 1),
                                              skip_group_check=True)
                    mm.then_inc(s_pv, 1)

                def body(g, i, y, more):
                    for j in range(G):
                        if more:
                            scores(g + 1, i, 1 - y, j)
                        if j == 0:
                            continue
                        if j == 1:
                            maxima(g, y)
                        shifted(g, y, j - 1)
                        if j >= 2:
                            product(g, y, j - 2)
                    shifted(g, y, G - 1)
                    product(g, y, G - 2)
                    product(g, y, G - 1)

                pe.wait_ge(s_set, at(8))
                for j in range(G):
                    scores(0, 0, 0, j)
                with pe.Fori(0, NG // 2 - 1) as i:
                    body(2 * i, i, 0, True)
                    body(2 * i + 1, i + 1, 1, True)
                body(NG - 2, NG // 2 - 1, 0, True)
                body(NG - 1, None, 1, False)

        def cross_attention():
            NS = 4
            LOADS = 2 * COMBO + 1
            NW = 3
            NCH = 20
            RUN = -(-LC // NCH)
            LCE = LC + LC % 2
            CROWS = KROWS + 1 + PARTS
            OWN = NT - 1
            FT = 6
            RT = 5
            rows = [min(P, LC - kt * P) for kt in range(NK)]
            with ExitStack() as s:
                Q = [sbuf(s, f"Q{k}", [P, L], BF16) for k in range(NS)]
                K = [sbuf(s, f"K{k}", [P, LC], BF16) for k in range(NS)]
                V = [sbuf(s, f"V{k}", [P, NK, HD]) for k in range(NS)]
                VO = [sbuf(s, f"VO{k}", [P, NK, 4 * HD]) for k in range(NS)]
                W = sbuf(s, "W", [P, NW, L])
                OL = [sbuf(s, f"OL{y}", [4 * HD, L]) for y in range(2)]
                cands = [sbuf(s, f"cand{y}", [P, NCH, 8]) for y in range(2)]
                cand2 = sbuf(s, "cand2", [P, NCH, 8])
                reach = sbuf(s, "reach", [P, NCH, 8])
                reach8 = sbuf(s, "reach8", [P, NCH])
                top8 = [sbuf(s, f"top8_{r}", [P, NT, 8]) for r in range(2)]
                next8 = [sbuf(s, f"next8_{r}", [P, NT, 8]) for r in range(2)]
                cnt = [sbuf(s, f"cnt{r}", [P, NT, 2]) for r in range(2)]
                most = sbuf(s, "most", [1, 1], mybir.dt.int32)
                redo8 = sbuf(s, "redo8", [P, 8])
                nm = sbuf(s, "nm", [P, NT])
                r1 = sbuf(s, "r1", [P, NT])
                mp = [sbuf(s, f"mp{r}", [P, NT, 1 + PARTS], BF16) for r in range(2)]
                S = [[sbuf(s, f"S{r}_{w}", [P, LCE]) for w in range(NT)] for r in range(2)]
                M = sbuf(s, "M", [P, LC])
                N = [[sbuf(s, f"N{r}_{w}", [P, LCE], BF16) for w in range(NT)] for r in range(2)]
                psS = psum(s, "psS", [P, 4 * 512])
                psT = psum(s, "psT", [P, 1024], BF16)
                psB = [psum(s, f"psB{k}", [P, 512]) for k in range(2)]
                psO = psum(s, "psO", [P, 512])
                s_ld = [sem(s, f"s_ld{k}") for k in range(NS)]
                s_st = [sem(s, f"s_st{y}") for y in range(2)]
                (s_set, s_vo, s_sc, s_ev, s_pick, s_own, s_top, s_most, s_ok, s_redo, s_chain, s_mt, s_qb, s_b, s_e, s_pv,
                 s_ol) = (sem(s, n) for n in (
                     "s_set", "s_vo", "s_sc", "s_ev", "s_pick", "s_own", "s_top", "s_most", "s_ok", "s_redo", "s_chain", "s_mt",
                     "s_qb", "s_b", "s_e", "s_pv", "s_ol"))
                block = s.enter_context(nc.Block())

                def quarter(w):
                    return range(w * NK // NT, (w + 1) * NK // NT)

                def steps(eng, step):
                    with eng.Fori(0, U // NS - 1) as i:
                        for k in range(NS):
                            step(NS * i + k, k, i, NS)
                    for k in range(NS):
                        step(U - NS + k, k, U // NS - 1, NS - 1 - k)

                def after(k, i, n):
                    return (k + n) % NS, i + (k + n) // NS

                @block.sync
                def _(sp):
                    set_to_one(sp)

                    def load(u, k):
                        for c in range(COMBO):
                            sp.dma_start(K[k][c * HD:(c + 1) * HD, :],
                                         kc_d[KPART[c], bass.ds(u * HD, HD), :]).then_inc(s_ld[k], 16)
                        for c in range(COMBO):
                            sp.dma_start(Q[k][c * HD:(c + 1) * HD, :],
                                         qc_d[QPART[c], bass.ds(u * HD, HD), :]).then_inc(s_ld[k], 16)
                        sp.dma_start(V[k][:, :, :], vc_d[bass.ds(u, 1), :, :].rearrange("o p n -> p (o n)")
                                     .rearrange("p (t d) -> p t d", d=HD)).then_inc(s_ld[k], 16)

                    def store(n, y):
                        sp.wait_ge(s_ol, at(n + 1))
                        sp.sem_inc(s_held, 1)
                        for z in range(2):
                            sp.dma_start(oc_d[z, bass.ds(n * 2 * HD, 2 * HD), :],
                                         OL[y][z * 2 * HD:(z + 1) * 2 * HD, :]).then_inc(s_st[y], 16)

                    def step(u, k, i, left):
                        sp.wait_ge(s_pv, at(NK * (u + 1)))
                        sp.sem_inc(s_held, 1)
                        if left == NS:
                            load(u + NS, k)
                        if k % 2:
                            store(2 * i + k // 2, k // 2)

                    for k in range(NS):
                        load(k, k)
                    steps(sp, step)
                    for y in range(2):
                        sp.wait_ge(s_st[y], at(32 * PAIRS // 2))

                @block.gpsimd
                def _(pool):
                    def marks(u, r, w):
                        pool.wait_ge(s_top, at(FT * (NT * u + w) + 4))
                        pool.sem_inc(s_held, 1)
                        nc.gpsimd.tensor_scalar(N[r][w][:, :], S[r][w][:, :], next8[r][:, w, 7:8], None,
                                                ALU.is_lt).then_inc(s_pick, 1)

                    def values(u, k, i):
                        pool.wait_ge(s_ld[k], at(16 * LOADS * (i + 1)))
                        pool.sem_inc(s_held, 1)
                        nc.gpsimd.tensor_copy(VO[k][:, :, k % 2 * HD:(k % 2 + 1) * HD], V[k][:, :, :]
                                              ).then_inc(s_vo, 1)

                    def front(u, k):
                        r = k % 2
                        for w in range(OWN - 1):
                            marks(u, r, w)
                        pool.wait_ge(s_top, at(FT * NT * (u + 1)))
                        pool.sem_inc(s_held, 1)
                        nc.gpsimd.tensor_tensor(mp[r][:, :, 0], cnt[r][:, :, 0], cnt[r][:, :, 1], ALU.add
                                                ).then_inc(s_chain, 1)
                        parts_of_minus(pool, s_chain, 6 * u + 1, top8[r][:, :, 0], nm[:, :], r1[:, :],
                                       [mp[r][:, :, 1 + a] for a in range(PARTS)])
                        marks(u, r, OWN - 1)

                    pool.wait_ge(s_set, at(4 * NS + 2 * NT))
                    for k in range(2):
                        values(k, k, 0)
                        front(k, k)
                    with pool.Fori(0, U // NS - 1) as i:
                        for k in range(NS):
                            k2, i2 = after(k, i, 2)
                            values(NS * i + k + 2, k2, i2)
                            pool.wait_ge(s_b, at(NK * (NS * i + k + 1)))
                            pool.sem_inc(s_held, 1)
                            front(NS * i + k + 2, k2)
                    for k in range(NS - 2):
                        values(U - NS + k + 2, k + 2, U // NS - 1)
                        pool.wait_ge(s_b, at(NK * (U - NS + k + 1)))
                        front(U - NS + k + 2, k + 2)

                @block.vector
                def _(dve):
                    set_ones(dve, s_set, K, [VO[k][:, :, :] for k in range(NS)],
                             [VO[k][:, :, (2 + k % 2) * HD:(3 + k % 2) * HD] for k in range(NS)])
                    for k in range(NS):
                        nc.vector.memset(K[k][KROWS:KROWS + 1, :], 0.0).then_inc(s_set, 1)
                    for r in range(2):
                        for w in range(NT):
                            nc.vector.memset(S[r][w][:, LC - 1:LCE], LOWEST).then_inc(s_set, 1)

                    def front(u, r, w, first):
                        n = NT * u + w
                        cand = cands[w % 2]
                        if w or not first:
                            dve.wait_ge(s_top, at(FT * (n - 1)))
                            dve.sem_inc(s_held, 1)
                        dve.wait_ge(s_ev, at(n + 1))
                        dve.sem_inc(s_held, 1)
                        for c in range(NCH):
                            run = nc.vector.max(cand[:, c, :], S[r][w][:, c * RUN:min(LC, (c + 1) * RUN)])
                        run.then_inc(s_top, 1)
                        a, b = top8[r][:, w, :], next8[r][:, w, :]
                        flat, flat2 = (t[:, :, :].rearrange("p c e -> p (c e)") for t in (cand, cand2))
                        dve.wait_ge(s_top, at(FT * n + 1))
                        dve.sem_inc(s_held, 1)
                        nc.vector.max(a, flat).then_inc(s_top, 1)
                        dve.wait_ge(s_top, at(FT * n + 2))
                        dve.sem_inc(s_held, 1)
                        nc.vector.match_replace(flat2, a, flat, LOWEST).then_inc(s_top, 1)
                        dve.wait_ge(s_top, at(FT * n + 3))
                        dve.sem_inc(s_held, 1)
                        nc.vector.max(b, flat2).then_inc(s_top, 1)
                        if w == OWN and not first:
                            dve.wait_ge(s_b, at(NK * (u - 1)))
                            dve.sem_inc(s_held, 1)
                        dve.wait_ge(s_top, at(FT * n + 4))
                        dve.sem_inc(s_held, 1)
                        nc.vector.tensor_scalar(reach[:, :, :], cand[:, :, :], b[:, 7:8], 0.0, ALU.is_ge, ALU.add,
                                                accum_out=cnt[r][:, w, 0:1]).then_inc(s_top, 1)
                        nc.vector.tensor_scalar(reach8[:, :], cand[:, :, 7], b[:, 7:8], 0.0, ALU.is_ge, ALU.add,
                                                accum_out=cnt[r][:, w, 1:2]).then_inc(s_top, 1)
                        if w == OWN:
                            nc.vector.tensor_scalar(N[r][w][:, :], S[r][w][:, :], b[:, 7:8], None,
                                                    ALU.is_lt).then_inc(s_own, 1)

                    def marks_anew(u, r):
                        for w in range(NT):
                            for n in range(RT):
                                if w or n:
                                    dve.wait_ge(s_redo, at(RT * (NT * u + w) + n))
                                    dve.sem_inc(s_held, 1)
                                src = S[r][w][:, 0:LC] if n < 2 else M[:, :]
                                if n == 4:
                                    ins = nc.vector.tensor_scalar(N[r][w][:, 0:LC], M[:, :], LOWEST, None, ALU.is_gt)
                                elif n % 2 == 0:
                                    ins = nc.vector.max(redo8[:, :], src)
                                else:
                                    ins = nc.vector.match_replace(M[:, :], redo8[:, :], src, LOWEST)
                                ins.then_inc(s_redo, 1)

                    def check(u, k):
                        dve.wait_ge(s_qb, at(u + 1))
                        nc.vector.tensor_reduce(most[:, :], Q[k][KROWS:KROWS + 1, :], AX_X, ALU.max
                                                ).then_inc(s_most, 1)
                        dve.wait_ge(s_pick, at(OWN * (u + 1)))
                        dve.wait_ge(s_own, at(u + 1))
                        dve.wait_ge(s_most, at(u + 1))
                        dve.sem_inc(s_held, 1)
                        largest = dve.value_load(most[0:1, 0:1])
                        with dve.If(largest != TOPK):
                            marks_anew(u, k % 2)
                        with dve.Else():
                            dve.sem_inc(s_redo, RT * NT)
                        dve.wait_ge(s_redo, at(RT * NT * (u + 1)))
                        dve.sem_inc(s_ok, 1)

                    def step(u, k, i, left):
                        for w in range(2):
                            if left:
                                front(u + 1, (k + 1) % 2, w, False)
                        check(u, k)
                        for w in range(2, NT):
                            if left:
                                front(u + 1, (k + 1) % 2, w, False)

                    for w in range(NT):
                        front(0, 0, w, True)
                    steps(dve, step)

                @block.scalar
                def _(act):
                    def copy_scores(u, r, w):
                        act.wait_ge(s_sc, at(NT * u + w + 1))
                        nc.scalar.copy(S[r][w][:, 0:LC], psS[:, 0:LC]).then_inc(s_ev, 1)

                    def exps(u, tiles):
                        for kt in tiles:
                            act.wait_ge(s_pv, at(NK * u if kt < NW else NK * u + kt - NW + 1))
                            act.wait_ge(s_b, at(NK * u + kt + 1))
                            nc.scalar.activation(W[0:rows[kt], kt % NW, :], psB[kt % 2][0:rows[kt], :],
                                                 ACT.Exp).then_inc(s_e, 1)

                    def rows_into_q(u, k):
                        act.wait_ge(s_mt, at(u + 1))
                        nc.scalar.copy(Q[k][KROWS:CROWS, :], psT[0:1 + PARTS, 0:L]).then_inc(s_qb, 1)

                    def step(u, k, i, left):
                        for w in range(NT):
                            exps(u, quarter(w))
                            if left >= 2:
                                if w == 0:
                                    act.wait_ge(s_ok, at(u + 1))
                                copy_scores(u + 2, k % 2, w)
                            if w == 1 and left:
                                rows_into_q(u + 1, (k + 1) % NS)
                        if k % 2:
                            y = k // 2
                            act.wait_ge(s_pv, at(NK * (u + 1)))
                            act.wait_ge(s_st[y], at(32 * i))
                            nc.scalar.copy(OL[y][:, :], psO[0:4 * HD, :]).then_inc(s_ol, 1)

                    act.wait_ge(s_set, at(4 * NS + 2 * NT))
                    for u in range(2):
                        for w in range(NT):
                            copy_scores(u, u, w)
                    rows_into_q(0, 0)
                    steps(act, step)

                @block.tensor
                def _(pe):
                    def scores(u, w, k, i):
                        if w == 0:
                            pe.wait_ge(s_ld[k], at(16 * LOADS * (i + 1)))
                        pe.wait_ge(s_ev, at(NT * u + w))
                        for c in range(0, LC, 512):
                            n = min(512, LC - c)
                            mm = nc.tensor.matmul(psS[:, c:c + n], Q[k][0:KROWS, w * P:(w + 1) * P],
                                                  K[k][0:KROWS, c:c + n], start=True, stop=True)
                        mm.then_inc(s_sc, 1)

                    def maxima(u, r):
                        pe.wait_ge(s_chain, at(6 * (u + 1)))
                        for w in range(NT):
                            tr = nc.tensor.transpose(psT[0:1 + PARTS, w * P:(w + 1) * P], mp[r][:, w, :],
                                                     identb[:, :])
                        tr.then_inc(s_mt, 1)

                    def shifted(u, k, kt):
                        r, m = k % 2, rows[kt]
                        pe.wait_ge(s_e, at(NK * u if kt < 2 else NK * u + kt - 1))
                        nc.tensor.matmul(psB[kt % 2][0:m, :], K[k][0:CROWS, kt * P:kt * P + m], Q[k][0:CROWS, :],
                                         start=True, stop=True)
                        for w in range(NT):
                            mm = nc.tensor.matmul(psB[kt % 2][0:m, w * P:(w + 1) * P], N[r][w][:, kt * P:kt * P + m],
                                                  negbig[:, :], start=False, stop=True,
                                                  skip_group_check=True)
                        mm.then_inc(s_b, 1)

                    def product(u, k, kt):
                        r, m = k % 2, rows[kt]
                        pe.wait_ge(s_e, at(NK * u + kt + 1))
                        nc.tensor.matmul(psO[0:4 * HD, :], VO[k][0:m, kt, :], W[0:m, kt % NW, :],
                                         start=(r == 0 and kt == 0), stop=(r == 1 and kt == NK - 1),
                                         skip_group_check=True).then_inc(s_pv, 1)

                    def back(u, k, i, w):
                        for kt in quarter(w):
                            shifted(u, k, kt)
                            if kt == 1:
                                pe.wait_ge(s_vo, at(u + 1))
                                if k % 2 == 0:
                                    pe.wait_ge(s_ol, at(2 * i + k // 2))
                            if kt >= 1:
                                product(u, k, kt - 1)

                    def step(u, k, i, left):
                        k2, i2 = after(k, i, 2)
                        pe.wait_ge(s_ok, at(u + 1))
                        for w in range(NT):
                            back(u, k, i, w)
                            if left >= 2:
                                scores(u + 2, w, k2, i2)
                            if w == 1 and left:
                                maxima(u + 1, (k + 1) % 2)
                        product(u, k, NK - 1)

                    pe.wait_ge(s_set, at(4 * NS + 2 * NT))
                    for u in range(2):
                        for w in range(NT):
                            scores(u, w, u, 0)
                    maxima(0, 0)
                    steps(pe, step)

        with ExitStack() as s:
            t = norm_buffers(s)
            f = split_buffers(s)
            a = add_buffers(s)
            wso = sbuf(s, "wso", [P, KC, C])
            bso = sbuf(s, "bso", [1, C])
            wq = sbuf(s, "wq", [P, KC, C])
            bq = sbuf(s, "bq", [P, KC])
            bqs = sbuf(s, "bqs", [P, KC])
            oU = sbuf(s, "oU", [P, KC, L])
            oL = sbuf(s, "oL", [P, KC, L])
            oR = sbuf(s, "oR", [P, KC, L])
            oT = sbuf(s, "oT", [P, KC, L])
            s_w, s_bs, s_oT, s_norm = (sem(s, n) for n in ("s_w", "s_bs", "s_oT", "s_norm"))
            J = KC
            block = s.enter_context(nc.Block())

            @block.sync
            def _(sp):
                set_to_one(sp)
                sp.dma_start(wso[:, :, :], w_so.rearrange("(k p) n -> p k n", p=P)).then_inc(s_w, 16)
                sp.dma_start(bso[:, :], row(b_so)).then_inc(s_w, 16)
                sp.dma_start(wq[:, :, :], w_q.rearrange("(k p) n -> p k n", p=P)).then_inc(s_w, 16)
                sp.dma_start(bq[:, :], column(b_q), allow_slow_non_contiguous=True).then_inc(s_w, 16)
                with sp.Fori(0, B) as b:
                    sp.wait_ge(s_norm, at(2 * b))
                    for z, dst in enumerate((oU, oL)):
                        sp.dma_start(dst[:, :, :], os_d[z, bass.ds(b * C, C), :].rearrange("(k p) l -> p k l", p=P)
                                     ).then_inc(s_oT, 16)
                    for j in range(J):
                        split_sync(sp, f, b, J, j, L, qc_d, j, 0)
                for k in range(2):
                    sp.wait_ge(f["parted"][k], at(16 * PARTS * B * J // 2))

            @block.gpsimd
            def _(pool):
                with pool.Fori(0, B) as b:
                    norm_pool(pool, t, b)
                    for j in range(J):
                        split_pool(pool, f, b, J, j, L)

            @block.vector
            def _(dve):
                dve.wait_ge(s_w, at(64))
                nc.vector.tensor_scalar(bqs[:, :], bq[:, :], QSCALE, None, ALU.mult).then_inc(s_bs, 1)
                with dve.Fori(0, B) as b:
                    divide(dve, b, s_oT, s_norm, oT, oU, oL, oR)
                    for w in range(NT):
                        add_vector(dve, a, b, NT, w, w, 0)
                    norm_vector(dve, t, b, a["added"])
                    for j in range(J):
                        split_vector(dve, f, b, J, j, L)

            @block.scalar
            def _(act):
                act.wait_ge(s_bs, at(1))
                with act.Fori(0, B) as b:
                    norm_scalar(act, t, b, 1, f["prod"], J)
                    for j in range(J):
                        split_scalar(act, f, b, J, j, L, bqs[:, j:j + 1], QSCALE)

            @block.tensor
            def _(pe):
                pe.wait_ge(s_w, at(64))
                with pe.Fori(0, B) as b:
                    pe.wait_ge(s_norm, at(2 * (b + 1)))
                    for w in range(NT):
                        add_tensor(pe, a, b, NT, w, bso[:, :], lambda k: oT[:, k, w * P:(w + 1) * P],
                                   lambda k: wso[:, k, :], KC)
                    norm_tensor(pe, t, b)
                    pe.wait_ge(t["hready"], at(KC * (b + 1)))
                    for j in range(J):
                        split_tensor(pe, f, b, J, j, L, lambda k: wq[:, k, j * P:(j + 1) * P],
                                     lambda k: t["hT"][:, k, :])

        cross_attention()

        with ExitStack() as s:
            t = norm_buffers(s)
            a = add_buffers(s)
            wco = sbuf(s, "wco", [P, KC, C])
            bco = sbuf(s, "bco", [1, C])
            wm1 = sbuf(s, "wm1", [P, KC, 2 * HID])
            bm1 = sbuf(s, "bm1", [P, 2 * HC])
            nbm1 = sbuf(s, "nbm1", [P, HC])
            wm2 = sbuf(s, "wm2", [P, HC, C])
            bm2 = sbuf(s, "bm2", [1, C])
            oU = sbuf(s, "oU", [P, KC, L])
            oL = sbuf(s, "oL", [P, KC, L])
            oR = sbuf(s, "oR", [P, KC, L])
            oT = sbuf(s, "oT", [P, KC, L])
            E = [sbuf(s, f"E{k}", [P, L]) for k in range(2)]
            D = sbuf(s, "D", [P, L])
            R = sbuf(s, "R", [P, L])
            SA = sbuf(s, "SA", [P, L])
            uT = sbuf(s, "uT", [P, HC, L])
            psA = [psum(s, f"psA{k}", [P, L]) for k in range(2)]
            psU = [psum(s, f"psU{k}", [P, L]) for k in range(2)]
            s_w, s_bs, s_oT, s_norm, s_u, s_ex, s_ch, s_gl, s_out = (
                sem(s, n) for n in ("s_w", "s_bs", "s_oT", "s_norm", "s_u", "s_ex", "s_ch", "s_gl", "s_out"))
            J = 2 * NT
            block = s.enter_context(nc.Block())

            @block.sync
            def _(sp):
                set_to_one(sp)
                sp.dma_start(wco[:, :, :], w_co.rearrange("(k p) n -> p k n", p=P)).then_inc(s_w, 16)
                sp.dma_start(bco[:, :], row(b_co)).then_inc(s_w, 16)
                sp.dma_start(bm2[:, :], row(b_m2)).then_inc(s_w, 16)
                sp.dma_start(bm1[:, :], column(b_m1), allow_slow_non_contiguous=True).then_inc(s_w, 16)
                sp.dma_start(wm1[:, :, :], w_m1.rearrange("(k p) n -> p k n", p=P)).then_inc(s_w, 16)
                sp.dma_start(wm2[:, :, :], w_m2.rearrange("(k p) n -> p k n", p=P)).then_inc(s_w, 16)
                with sp.Fori(0, B) as b:
                    sp.wait_ge(s_norm, at(2 * b))
                    for z, dst in enumerate((oU, oL)):
                        sp.dma_start(dst[:, :, :], oc_d[z, bass.ds(b * C, C), :].rearrange("(k p) l -> p k l", p=P)
                                     ).then_inc(s_oT, 16)
                    sp.wait_ge(a["added"], at(J * (b + 1)))
                    ob = out[bass.ds(b, 1), :, :].rearrange("o l c -> (o l) c")
                    sp.dma_start(ob[SHIFT:L - SHIFT, :].rearrange("(t p) c -> p t c", p=P),
                                 xs[:, bass.ds(b, 1), 0:NT - 1, :].rearrange("p o t c -> p (o t) c")).then_inc(s_out, 16)
                    sp.dma_start(ob[L - SHIFT:L, :],
                                 xs[0:SHIFT, bass.ds(b, 1), NT - 1, :].rearrange("p o c -> p (o c)")).then_inc(s_out, 16)
                    sp.dma_start(ob[0:SHIFT, :],
                                 xs[SHIFT:P, bass.ds(b, 1), NT - 1, :].rearrange("p o c -> p (o c)")).then_inc(s_out, 16)
                sp.wait_ge(s_out, at(48 * B))

            @block.gpsimd
            def _(pool):
                with pool.Fori(0, B) as b:
                    norm_pool(pool, t, b)

            @block.vector
            def _(dve):
                dve.wait_ge(s_w, at(96))
                nc.vector.tensor_scalar(nbm1[:, :], bm1[:, 0:HC], -1.0, None, ALU.mult).then_inc(s_bs, 1)
                with dve.Fori(0, B) as b:
                    divide(dve, b, s_oT, s_norm, oT, oU, oL, oR)
                    for w in range(NT):
                        add_vector(dve, a, b, J, w, w, 1)
                    norm_vector(dve, t, b, a["added"], J)
                    dve.wait_ge(a["summed"], at(J * b))
                    for j in range(HC):
                        n = HC * b + j
                        dve.wait_ge(s_ex, at(n + 1))
                        nc.vector.tensor_scalar(D[:, :], E[j % 2][:, :], 1.0, None, ALU.add).then_inc(s_ch, 1)
                        dve.wait_ge(s_ch, at(3 * n + 1))
                        nc.vector.reciprocal(R[:, :], D[:, :]).then_inc(s_ch, 1)
                        dve.wait_ge(s_ch, at(3 * n + 2))
                        nc.vector.scalar_tensor_tensor(out=SA[:, :], in0=psA[j % 2][:, :], scalar=bm1[:, j:j + 1],
                                                       in1=R[:, :], op0=ALU.add, op1=ALU.mult).then_inc(s_ch, 1)
                        dve.wait_ge(s_ch, at(3 * n + 3))
                        nc.vector.scalar_tensor_tensor(out=uT[:, j, :], in0=psU[j % 2][:, :],
                                                       scalar=bm1[:, HC + j:HC + j + 1], in1=SA[:, :],
                                                       op0=ALU.add, op1=ALU.mult).then_inc(s_gl, 1)
                    for w in range(NT):
                        add_vector(dve, a, b, J, NT + w, w, 2)

            @block.scalar
            def _(act):
                act.wait_ge(s_bs, at(1))
                with act.Fori(0, B) as b:
                    norm_scalar(act, t, b, 2, s_u, HC)
                    for j in range(HC):
                        n = HC * b + j
                        act.wait_ge(s_u, at(n + 1))
                        act.wait_ge(s_ch, at(3 * HC * b if j < 2 else 3 * (n - 2) + 1))
                        nc.scalar.activation(E[j % 2][:, :], psA[j % 2][:, :], ACT.Exp, bias=nbm1[:, j:j + 1],
                                             scale=-1.0).then_inc(s_ex, 1)

            @block.tensor
            def _(pe):
                pe.wait_ge(s_w, at(96))
                with pe.Fori(0, B) as b:
                    pe.wait_ge(s_norm, at(2 * (b + 1)))
                    for w in range(NT):
                        add_tensor(pe, a, b, J, w, bco[:, :], lambda k: oT[:, k, w * P:(w + 1) * P],
                                   lambda k: wco[:, k, :], KC)
                    norm_tensor(pe, t, b)
                    pe.wait_ge(t["hready"], at(KC * (b + 1)))
                    for j in range(HC):
                        pe.wait_ge(s_gl, at(HC * b if j < 2 else HC * b + j - 1))
                        for ps, c in ((psA, j * P), (psU, HID + j * P)):
                            for k in range(KC):
                                mm = nc.tensor.matmul(ps[j % 2][:, :], wm1[:, k, c:c + P], t["hT"][:, k, :],
                                                      start=(k == 0), stop=(k == KC - 1))
                        mm.then_inc(s_u, 1)
                    pe.wait_ge(s_gl, at(HC * (b + 1)))
                    for w in range(NT):
                        add_tensor(pe, a, b, J, NT + w, bm2[:, :], lambda k: uT[:, k, w * P:(w + 1) * P],
                                   lambda k: wm2[:, k, :], HC)


_INS = ['x', 'cond_1024', 'ctx_1024', 'L0_xcond_w_ada', 'L0_xcond_b_ada', 'L0_xcond_w_qkv', 'L0_xcond_b_qkv',
        'L0_xcond_w_so', 'L0_xcond_b_so', 'L0_xcond_w_q', 'L0_xcond_b_q', 'L0_xcond_w_kv', 'L0_xcond_b_kv',
        'L0_xcond_w_co', 'L0_xcond_b_co', 'L0_xcond_w_m1', 'L0_xcond_b_m1', 'L0_xcond_w_m2', 'L0_xcond_b_m2']


def kernel(**inputs):
    import numpy as _np
    import concourse.bacc as _bacc
    from concourse import mybir as _mybir
    from concourse.bass_utils import run_bass_kernel_spmd as _run

    nc = _bacc.Bacc("TRN2", target_bir_lowering=False, num_devices=1)
    arrays, args = {}, []
    for name in _INS:
        a = _np.ascontiguousarray(inputs[name])
        arrays[f"in_{name}_dram"] = a
        args.append(nc.dram_tensor(f"in_{name}_dram", a.shape, _mybir.dt.from_np(a.dtype), kind="ExternalInput").ap())
    shape = inputs['x'].shape
    args.append(nc.dram_tensor("out_0_dram", shape, _mybir.dt.from_np(_np.dtype("float32")), kind="ExternalOutput").ap())
    build(nc, *args)
    r = _run(nc, [arrays], core_ids=[0])
    return r.results[0]["out_0_dram"]
```

```python
from contextlib import ExitStack

import concourse.bass as bass
from concourse import mybir

F32 = mybir.dt.float32
BF16 = mybir.dt.bfloat16
ALU = mybir.AluOpType
ACT = mybir.ActivationFunctionType
AX_X = mybir.AxisListType.X

P = 128
HEADS = 16
HD = 16
TOPK = 16
SHIFT = 64
COMBO = 6
PARTS = 3
KROWS = COMBO * HD
BROWS = KROWS + PARTS
LOWEST = -3.4028234663852886e38
BIG = 2.0 ** 100
EPS = 1e-6


def build(nc, x, cond, ctx, w_ada, b_ada, w_qkv, b_qkv, w_so, b_so, w_q, b_q, w_kv, b_kv,
          w_co, b_co, w_m1, b_m1, w_m2, b_m2, out):
    B, L, C = x.shape
    LC = ctx.shape[1]
    HID = w_m2.shape[0]
    KC = C // P
    NT = L // P
    NK = -(-LC // P)
    KLAST = LC - (NK - 1) * P
    U = B * HEADS
    PAIRS = U // 2
    NMOD = w_ada.shape[1] // P
    QSCALE = float(HD) ** -0.5
    HC = HID // P

    with ExitStack() as top:
        used = {}

        def unique(name):
            used[name] = used.get(name, 0) + 1
            return name if used[name] == 1 else f"{name}_{used[name]}"

        def sbuf(stack, name, shape, dt=F32):
            return stack.enter_context(nc.sbuf_tensor(unique(name), shape, dt))

        def psum(stack, name, shape, dt=F32):
            return stack.enter_context(nc.psum_tensor(unique(name), shape, dt))

        fresh = []

        def sem(stack, name):
            fresh.append(stack.enter_context(nc.semaphore(unique(name))))
            return fresh[-1]

        def set_to_one(eng):
            for s in fresh:
                eng.sem_inc(s, 1)
            fresh.clear()

        s_begun = top.enter_context(nc.semaphore("s_begun"))

        def at(count):
            return count + 1

        s_held = top.enter_context(nc.semaphore("s_held"))

        qs_d = nc.dram_tensor("qs_d", [U * HD, COMBO, L], BF16)
        ks_d = nc.dram_tensor("ks_d", [U * HD, COMBO, L], BF16)
        vs_d = nc.dram_tensor("vs_d", [U, P, NT * HD], F32)
        qc_d = nc.dram_tensor("qc_d", [U * HD, COMBO, L], BF16)
        kc_d = nc.dram_tensor("kc_d", [U * HD, COMBO, LC], BF16)
        vc_d = nc.dram_tensor("vc_d", [U, P, NK * HD], F32)
        os_d = nc.dram_tensor("os_d", [2, U * HD, L], F32)
        oc_d = nc.dram_tensor("oc_d", [2, 2, U * HD, L], F32)

        xs = sbuf(top, "xs", [P, B, NT, C])
        ident = sbuf(top, "ident", [P, P])
        identb = sbuf(top, "identb", [P, P], BF16)
        negbig = sbuf(top, "negbig", [P, P], BF16)
        ones = sbuf(top, "ones", [P, P])
        modT = sbuf(top, "modT", [P, NMOD, B])
        gate = sbuf(top, "gate", [P, 3, B, C])
        mhalf = sbuf(top, "mhalf", [P, NT])

        GT = 512 // P
        NG = -(-NK // GT)

        def column(v):
            return v.rearrange("(n p) -> p n", p=P)

        def row(v):
            return v.rearrange("(o n) -> o n", o=1)

        def load_context(sp, b, cs, s_c):
            cb = ctx[bass.ds(b, 1), :, :].rearrange("o r c -> (o r) c")
            sp.dma_start(cs[:, 0:NK - 1, :],
                         cb[0:(NK - 1) * P, :].rearrange("(t p) c -> p t c", p=P)).then_inc(s_c, 16)
            sp.dma_start(cs[0:KLAST, NK - 1, :], cb[(NK - 1) * P:LC, :]).then_inc(s_c, 16)

        early = top.enter_context(ExitStack())
        wqkv = sbuf(early, "wqkv", [P, KC, 3 * C])
        wkv = sbuf(early, "wkv", [P, KC, 2 * C])
        bqk = sbuf(early, "bqk", [P, 2 * KC])
        bk = sbuf(early, "bk", [P, KC])
        bvs = sbuf(early, "bvs", [1, C])
        bvc = sbuf(early, "bvc", [1, C])
        cs = sbuf(early, "cs", [P, NK, C])
        s_we, s_c = (sem(early, n) for n in ("s_we", "s_c"))

        with ExitStack() as s:
            wa = sbuf(s, "wa", [P, KC, NMOD * P])
            bar = sbuf(s, "bar", [1, NMOD * P])
            condT = sbuf(s, "condT", [P, KC, B])
            sl = sbuf(s, "sl", [P, KC, B])
            rows = sbuf(s, "rows", [B, NMOD * P])
            sel = sbuf(s, "sel", [B, B, P])
            bac = sbuf(s, "bac", [P, NMOD])
            NR = NMOD // KC
            columns = [n for n in range(NMOD) if n // KC % 3 != 2]
            psR = [psum(s, f"psR{k}", [B, 512]) for k in range(2)]
            psM = psum(s, "psM", [P, 512 // B, B])
            psG = [psum(s, f"psG{k}", [P, 512]) for k in range(2)]
            s_x, s_w, s_sl, s_sel, s_r, s_rc = (sem(s, n) for n in ("s_x", "s_w", "s_sl", "s_sel", "s_r", "s_rc"))
            s_one, s_id, s_m, s_mc, s_g, s_gc = (sem(s, n) for n in
                                                 ("s_one", "s_id", "s_m", "s_mc", "s_g", "s_gc"))
            block = s.enter_context(nc.Block())

            @block.sync
            def _(sp):
                set_to_one(sp)
                for k in range(KC):
                    sp.dma_start(condT[:, k, :], cond[:, k * P:(k + 1) * P].rearrange("b p -> p b"),
                                 allow_slow_non_contiguous=True).then_inc(s_w, 16)
                sp.dma_start(bac[:, :], column(b_ada), allow_slow_non_contiguous=True).then_inc(s_w, 16)
                sp.dma_start(bar[:, :], b_ada.rearrange("(o n) -> o n", o=1)).then_inc(s_w, 16)
                sp.dma_start(wa[:, :, :], w_ada.rearrange("(k p) n -> p k n", p=P)).then_inc(s_w, 16)
                for b in range(B):
                    sp.dma_start(xs[:, b, 0:NT - 1, :],
                                 x[b, SHIFT:L - SHIFT, :].rearrange("(t p) c -> p t c", p=P)).then_inc(s_x, 16)
                    sp.dma_start(xs[0:SHIFT, b, NT - 1, :], x[b, L - SHIFT:L, :]).then_inc(s_x, 16)
                    sp.dma_start(xs[SHIFT:P, b, NT - 1, :], x[b, 0:SHIFT, :]).then_inc(s_x, 16)
                load_context(sp, 0, cs, s_c)
                sp.dma_start(wkv[:, :, :], w_kv.rearrange("(k p) n -> p k n", p=P)).then_inc(s_we, 16)
                sp.dma_start(bk[:, :], column(b_kv[0:C]), allow_slow_non_contiguous=True).then_inc(s_we, 16)
                sp.dma_start(bvc[:, :], row(b_kv[C:2 * C])).then_inc(s_we, 16)
                sp.dma_start(wqkv[:, :, :], w_qkv.rearrange("(k p) n -> p k n", p=P)).then_inc(s_we, 16)
                sp.dma_start(bqk[:, :], column(b_qkv[0:2 * C]), allow_slow_non_contiguous=True).then_inc(s_we, 16)
                sp.dma_start(bvs[:, :], row(b_qkv[2 * C:3 * C])).then_inc(s_we, 16)
                sp.wait_ge(s_x, at(48 * B))

            @block.gpsimd
            def _(pool):
                nc.gpsimd.memset(ident[:, :], 0.0).then_inc(s_id, 1)
                nc.gpsimd.memset(mhalf[:, :], -0.5)
                pool.wait_ge(s_id, at(1))
                nc.gpsimd.affine_select(out=ident[:, :], in_=ident[:, :], compare_op=ALU.not_equal,
                                        fill=1.0, base=0, pattern=[[-1, P]],
                                        channel_multiplier=1).then_inc(s_id, 1)
                pool.wait_ge(s_id, at(2))
                nc.gpsimd.tensor_copy(identb[:, :], ident[:, :]).then_inc(s_id, 1)
                nc.gpsimd.tensor_scalar(negbig[:, :], ident[:, :], -BIG, None, ALU.mult).then_inc(s_id, 1)

            @block.scalar
            def _(act):
                act.wait_ge(s_w, at(16 * (KC + 3)))
                nc.scalar.activation(sl[:, :, :], condT[:, :, :], ACT.Silu).then_inc(s_sl, 1)
                for n in range(NR):
                    act.wait_ge(s_r, at(n + 1))
                    nc.scalar.copy(rows[:, n * C:(n + 1) * C], psR[n % 2][:, 0:C]).then_inc(s_rc, 1)

            @block.vector
            def _(dve):
                nc.vector.memset(ones[:, :], 1.0).then_inc(s_one, 1)
                dve.wait_ge(s_one, at(1))
                dve.wait_ge(s_id, at(2))
                for b in range(B):
                    nc.vector.tensor_scalar(sel[:, b, :], ones[0:B, :], ident[0:B, b:b + 1], None, ALU.mult
                                            ).then_inc(s_sel, 1)
                dve.wait_ge(s_m, at(1))
                for g in range(3):
                    n = slice(3 * g * KC, (3 * g + 2) * KC)
                    for b in range(B):
                        nc.vector.tensor_tensor(modT[:, n, b], psM[:, n, b], bac[:, n], ALU.add).then_inc(s_mc, 1)
                dve.wait_ge(s_mc, at(3 * B))
                for part in (1, 4, 7):
                    m = modT[:, part * KC:(part + 1) * KC, :]
                    nc.vector.tensor_scalar(m, m, 1.0, None, ALU.add).then_inc(s_mc, 1)
                for n in range(3 * B):
                    dve.wait_ge(s_g, at(n + 1))
                    nc.vector.tensor_copy(gate[:, n // B, n % B, :], psG[n % 2][:, 0:C]).then_inc(s_gc, 1)

            @block.tensor
            def _(pe):
                pe.wait_ge(s_sl, at(1))
                pe.wait_ge(s_one, at(1))
                for n in range(NR):
                    if n >= 2:
                        pe.wait_ge(s_rc, at(n - 1))
                    ps, cols = psR[n % 2][:, 0:C], slice(n * C, (n + 1) * C)
                    gates = n % 3 == 2
                    if gates:
                        nc.tensor.matmul(ps, ones[0:1, 0:B], bar[:, cols], start=True, stop=False)
                    for k in range(KC):
                        mm = nc.tensor.matmul(ps, sl[:, k, :], wa[:, k, cols], start=(k == 0 and not gates),
                                              stop=(k == KC - 1))
                    mm.then_inc(s_r, 1)
                pe.wait_ge(s_rc, at(NR))
                pe.wait_ge(s_id, at(2))
                for n in columns:
                    tr = nc.tensor.transpose(psM[:, n, :], rows[:, n * P:(n + 1) * P], ident[0:B, 0:B])
                tr.then_inc(s_m, 1)
                pe.wait_ge(s_sel, at(B))
                for n in range(3 * B):
                    g, b = n // B, n % B
                    cols = slice((3 * g + 2) * C, (3 * g + 3) * C)
                    if n >= 2:
                        pe.wait_ge(s_gc, at(n - 1))
                    nc.tensor.matmul(psG[n % 2][:, 0:C], sel[:, b, :], rows[:, cols], start=True, stop=True
                                     ).then_inc(s_g, 1)

        def norm_buffers(s):
            t = {}
            t["st"] = sbuf(s, "st", [P, NT, 6])
            t["mv"] = sbuf(s, "mv", [P, NT, 2])
            t["ve"] = sbuf(s, "ve", [P, NT])
            t["rs"] = sbuf(s, "rs", [P, NT])
            t["xn"] = sbuf(s, "xn", [P, NT, C])
            t["hT"] = sbuf(s, "hT", [P, KC, L])
            t["psX"] = [psum(s, f"psX{k}", [P, L]) for k in range(KC)]
            for n in ("stats", "aggr", "var", "rstd", "xnorm", "turned", "hready"):
                t[n] = sem(s, "s_" + n)
            return t

        def norm_vector(dve, t, b, added=None, n=None):
            for w in range(NT):
                if added is not None:
                    dve.wait_ge(added, at(n + w + 1))
                    dve.sem_inc(s_held, 1)
                nc.vector.bn_stats(t["st"][:, w, :], xs[:, b, w, :]).then_inc(t["stats"], 1)
            for w in range(NT):
                dve.wait_ge(t["stats"], at(NT * b + w + 1))
                dve.sem_inc(s_held, 1)
                nc.vector.bn_aggr(t["mv"][:, w, :], t["st"][:, w, :]).then_inc(t["aggr"], 1)
            dve.wait_ge(t["rstd"], at(b + 1))
            dve.wait_ge(t["turned"], at(KC * NT * b))
            for w in range(NT):
                nc.vector.tensor_scalar(t["xn"][:, w, :], xs[:, b, w, :], t["mv"][:, w, 0:1],
                                        t["rs"][:, w:w + 1], ALU.subtract, ALU.mult).then_inc(t["xnorm"], 1)

        def norm_pool(pool, t, b):
            pool.wait_ge(t["aggr"], at(NT * (b + 1)))
            pool.wait_ge(t["xnorm"], at(NT * b))
            pool.sem_inc(s_held, 1)
            nc.gpsimd.tensor_scalar(t["ve"][:, :], t["mv"][:, :, 1], EPS, None, ALU.add).then_inc(t["var"], 1)
            pool.wait_ge(t["var"], at(b + 1))
            nc.gpsimd.tensor_tensor(t["rs"][:, :], t["ve"][:, :], mhalf[:, :], ALU.pow).then_inc(t["rstd"], 1)

        def norm_tensor(pe, t, b):
            pe.wait_ge(t["hready"], at(KC * b))
            for w in range(NT):
                pe.wait_ge(t["xnorm"], at(NT * b + w + 1))
                for k in range(KC):
                    nc.tensor.transpose(t["psX"][k][:, w * P:(w + 1) * P], t["xn"][:, w, k * P:(k + 1) * P],
                                        ident[:, :]).then_inc(t["turned"], 1)

        def norm_scalar(act, t, b, which, used, uses):
            act.wait_ge(t["turned"], at(KC * NT * (b + 1)))
            act.wait_ge(used, at(uses * b))
            for k in range(KC):
                nc.scalar.activation(t["hT"][:, k, :], t["psX"][k][:, :], ACT.Identity,
                                     bias=modT[:, (3 * which) * KC + k, bass.ds(b, 1)],
                                     scale=modT[:, (3 * which + 1) * KC + k, bass.ds(b, 1)]).then_inc(t["hready"], 1)

        def split_buffers(s):
            t = {"psP": [psum(s, f"psP{k}", [P, L]) for k in range(2)],
                 "T": [sbuf(s, f"T{k}", [P, L]) for k in range(2)],
                 "R": [sbuf(s, f"R{k}", [P, L]) for k in range(2)],
                 "Pt": [sbuf(s, f"Pt{k}", [P, PARTS, L], BF16) for k in range(2)]}
            for n in ("prod", "biased", "part1", "rest", "part2", "part3"):
                t[n] = sem(s, "s_" + n)
            t["parted"] = [sem(s, f"s_parted{k}") for k in range(2)]
            return t

        def split_tensor(pe, t, b, J, j, n, lhs, rhs):
            pe.wait_ge(t["biased"], at(J * b if j < 2 else J * b + j - 1))
            for k in range(KC):
                mm = nc.tensor.matmul(t["psP"][j % 2][:, 0:n], lhs(k), rhs(k), start=(k == 0), stop=(k == KC - 1))
            mm.then_inc(t["prod"], 1)

        def split_scalar(act, t, b, J, j, n, bias, scale):
            act.wait_ge(t["prod"], at(J * b + j + 1))
            act.wait_ge(t["rest"], at(J * b if j < 2 else J * b + j - 1))
            nc.scalar.activation(t["T"][j % 2][:, 0:n], t["psP"][j % 2][:, 0:n], ACT.Identity,
                                 bias=bias, scale=scale).then_inc(t["biased"], 1)

        def split_vector(dve, t, b, J, j, n, up):
            T, R, Pt = t["T"][j % 2], t["R"][j % 2], t["Pt"][j % 2]
            first = 0 if up else PARTS - 1
            g = J * b + j
            dve.wait_ge(t["biased"], at(g + 1))
            dve.wait_ge(t["parted"][j % 2], at(16 * PARTS * (J // 2 * b + j // 2)))
            nc.vector.tensor_copy(Pt[:, first, 0:n], T[:, 0:n]).then_inc(t["part1"], 1)
            dve.wait_ge(t["part1"], at(g + 1))
            dve.wait_ge(t["part3"], at(J * b if j < 2 else g - 1))
            nc.vector.tensor_tensor(R[:, 0:n], T[:, 0:n], Pt[:, first, 0:n], ALU.subtract).then_inc(t["rest"], 1)
            dve.wait_ge(t["rest"], at(g + 1))
            nc.vector.tensor_copy(Pt[:, 1, 0:n], R[:, 0:n]).then_inc(t["part2"], 1)

        def split_pool(pool, t, b, J, j, n, up):
            R, Pt = t["R"][j % 2], t["Pt"][j % 2]
            last = PARTS - 1 if up else 0
            pool.wait_ge(t["part2"], at(J * b + j + 1))
            nc.gpsimd.tensor_tensor(Pt[:, last, 0:n], R[:, 0:n], Pt[:, 1, 0:n], ALU.subtract).then_inc(t["part3"], 1)

        def split_sync(sp, t, b, J, j, n, dram, chunk, c0, up):
            sp.wait_ge(t["part3"], at(J * b + j + 1))
            sp.sem_inc(s_held, 1)
            for c, m in ((0, 3), (3, 2), (5, 1)):
                a = 0 if up else PARTS - m
                sp.dma_start(dram[bass.ds(b * C + chunk * P, P), c:c + m, c0:c0 + n],
                             t["Pt"][j % 2][:, a:a + m, 0:n]).then_inc(t["parted"][j % 2], 16)

        def add_buffers(s):
            t = {"psV": [psum(s, f"psV{k}", [P, 512]) for k in range(2)],
                 "tmp": [sbuf(s, f"tmp{k}", [P, C]) for k in range(2)]}
            for n in ("summed", "gated", "added"):
                t[n] = sem(s, "s_" + n)
            return t

        def add_tensor(pe, t, n, y, bias, lhs, rhs, chunks, first=False):
            if not first:
                pe.wait_ge(t["gated"], at(n - 1))
            ps = t["psV"][y][:, 0:C]
            nc.tensor.matmul(ps, ones[0:1, :], bias, start=True, stop=False)
            for k in range(chunks):
                mm = nc.tensor.matmul(ps, lhs(k), rhs(k), start=False, stop=(k == chunks - 1))
            mm.then_inc(t["summed"], 1)

        def add_vector(dve, t, n, y, b, w, which, first=False):
            dve.wait_ge(t["summed"], at(n + 1))
            if not first:
                dve.wait_ge(t["added"], at(n - 1))
            nc.vector.tensor_tensor(t["tmp"][y][:, :], t["psV"][y][:, 0:C],
                                    gate[:, which, bass.ds(b, 1), :], ALU.mult).then_inc(t["gated"], 1)
            dve.wait_ge(t["gated"], at(n + 1))
            xt = xs[:, b, w, :]
            nc.vector.tensor_tensor(xt, xt, t["tmp"][y][:, :], ALU.add).then_inc(t["added"], 1)

        def divide_buffers(s):
            t = {n: sbuf(s, n, [P, KC, L]) for n in ("oU", "oL", "oR", "oT")}
            for n in ("fetched", "inverted", "divided"):
                t[n] = sem(s, "s_" + n)
            return t

        def divide_sync(sp, t, b, dram):
            sp.wait_ge(t["divided"], at(b))
            for z, dst in enumerate((t["oU"], t["oL"])):
                sp.dma_start(dst[:, :, :], dram[z, bass.ds(b * C, C), :].rearrange("(k p) l -> p k l", p=P)
                             ).then_inc(t["fetched"], 16)

        def divide_vector(dve, t, b, k):
            if k == 0:
                dve.wait_ge(t["fetched"], at(32 * (b + 1)))
            nc.vector.reciprocal(t["oR"][:, k, :], t["oL"][:, k, :]).then_inc(t["inverted"], 1)
            if k == KC - 1:
                dve.wait_ge(t["inverted"], at(KC * (b + 1)))
                nc.vector.tensor_tensor(t["oT"][:, :, :], t["oU"][:, :, :], t["oR"][:, :, :], ALU.mult
                                        ).then_inc(t["divided"], 1)

        def head_major(ap):
            return ap.rearrange("p (h d) -> p h d", d=HD)

        with ExitStack() as s:
            t = norm_buffers(s)
            f = split_buffers(s)
            bqks = sbuf(s, "bqks", [P, 2 * KC])
            cT = sbuf(s, "cT", [P, KC, NK * P])
            vhs = sbuf(s, "vhs", [P, HEADS, NT, HD])
            vhc = sbuf(s, "vhc", [P, HEADS, NK, HD])
            psX = t["psX"]
            psV = [psum(s, f"psV{k}", [P, 512]) for k in range(2)]
            s_bs, s_z, s_v, s_vc, s_vcd, s_vsd = (
                sem(s, n) for n in ("s_bs", "s_z", "s_v", "s_vc", "s_vcd", "s_vsd"))
            s_turned, s_ct = (sem(s, n) for n in ("s_cturned", "s_ct"))
            JC = KC * NG
            J = JC + 2 * KC
            NV = NK + NT
            gw = [min(GT * P, LC - g * GT * P) for g in range(NG)]
            rows = [min(P, LC - kt * P) for kt in range(NK)]
            width = [gw[j // KC] if j < JC else L for j in range(J)]
            assert NT == 2 * KC and NK <= JC * GT // KC

            def beside(j):
                return range(j * NK // JC, (j + 1) * NK // JC) if j < JC else range(NK + j - JC, NK + j - JC + 1)

            isq = [JC <= j < JC + KC for j in range(J)]
            block = s.enter_context(nc.Block())

            def batches(eng, body):
                with eng.Fori(0, B - 1) as b:
                    body(b, True)
                body(B - 1, False)

            @block.sync
            def _(sp):
                def body(b, more):
                    if more:
                        sp.wait_ge(s_turned, at(JC * (b + 1)))
                        sp.sem_inc(s_held, 1)
                        load_context(sp, b + 1, cs, s_c)
                    for j in range(JC):
                        split_sync(sp, f, b, J, j, width[j], kc_d, j % KC, (j // KC) * GT * P, False)
                    sp.wait_ge(s_vc, at(NV * b + NK))
                    sp.sem_inc(s_held, 1)
                    sp.dma_start(vc_d[bass.ds(b * HEADS, HEADS), :, :].rearrange("h p n -> p h n"),
                                 vhc[:, :, :, :].rearrange("p h w d -> p h (w d)")).then_inc(s_vcd, 16)
                    for j in range(JC, J):
                        split_sync(sp, f, b, J, j, L, qs_d if isq[j] else ks_d, j % KC, 0, isq[j])
                    sp.wait_ge(s_vc, at(NV * (b + 1)))
                    sp.sem_inc(s_held, 1)
                    sp.dma_start(vs_d[bass.ds(b * HEADS, HEADS), :, :].rearrange("h p n -> p h n"),
                                 vhs[:, :, :, :].rearrange("p h w d -> p h (w d)")).then_inc(s_vsd, 16)

                set_to_one(sp)
                sp.sem_inc(s_begun, 1)
                batches(sp, body)
                for k in range(2):
                    sp.wait_ge(f["parted"][k], at(16 * PARTS * B * J // 2))
                sp.wait_ge(s_vcd, at(16 * B))
                sp.wait_ge(s_vsd, at(16 * B))

            @block.gpsimd
            def _(pool):
                pool.wait_ge(s_begun, 1)
                nc.gpsimd.memset(vhc[KLAST // 32 * 32:P, :, NK - 1, :], 0.0).then_inc(s_z, 1)
                pool.wait_ge(s_z, at(1))
                with pool.Fori(0, B) as b:
                    norm_pool(pool, t, b)
                    for j in range(J):
                        split_pool(pool, f, b, J, j, width[j], isq[j])

            @block.vector
            def _(dve):
                dve.wait_ge(s_begun, 1)
                def copies(b, start):
                    if not start:
                        dve.wait_ge(s_v, at(NV * (b - 1) + NK))
                    for g in range(NG):
                        for k in range(KC):
                            dve.wait_ge(s_turned, at(JC * b + KC * g + k + 1))
                            nc.vector.tensor_copy(cT[:, k, g * GT * P:g * GT * P + gw[g]],
                                                  psX[k][:, 0:gw[g]]).then_inc(s_ct, 1)

                def body(b, more):
                    norm_vector(dve, t, b)
                    for j in range(JC):
                        split_vector(dve, f, b, J, j, width[j], False)
                    if more:
                        copies(b + 1, False)
                    for j in range(JC, J):
                        split_vector(dve, f, b, J, j, L, isq[j])

                dve.wait_ge(s_we, at(96))
                nc.vector.tensor_scalar(bqks[:, 0:KC], bqk[:, 0:KC], QSCALE, None, ALU.mult).then_inc(s_bs, 1)
                nc.vector.tensor_copy(bqks[:, KC:2 * KC], bqk[:, KC:2 * KC]).then_inc(s_bs, 1)
                copies(0, True)
                batches(dve, body)

            @block.scalar
            def _(act):
                act.wait_ge(s_begun, 1)
                act.wait_ge(s_we, at(96))
                act.wait_ge(s_bs, at(2))
                act.wait_ge(s_z, at(1))
                with act.Fori(0, B) as b:
                    for j in range(JC):
                        split_scalar(act, f, b, J, j, width[j], bk[:, j % KC:j % KC + 1], 1.0)
                        if j == 0:
                            act.wait_ge(s_vcd, at(16 * b))
                        for kt in beside(j):
                            act.wait_ge(s_v, at(NV * b + kt + 1))
                            nc.scalar.copy(vhc[0:rows[kt], :, kt, :],
                                           head_major(psV[kt % 2][0:rows[kt], 0:C])).then_inc(s_vc, 1)
                        if j == JC - 3:
                            norm_scalar(act, t, b, 0, s_v, NV)
                    for j in range(JC, J):
                        i = j - JC
                        split_scalar(act, f, b, J, j, L, bqks[:, i:i + 1], QSCALE if isq[j] else 1.0)
                        if j == JC:
                            act.wait_ge(s_vsd, at(16 * b))
                        for m in beside(j):
                            act.wait_ge(s_v, at(NV * b + m + 1))
                            nc.scalar.copy(vhs[:, :, m - NK, :], head_major(psV[m % 2][:, 0:C])).then_inc(s_vc, 1)

            @block.tensor
            def _(pe):
                pe.wait_ge(s_begun, 1)
                def context_transposes(b, start):
                    pe.wait_ge(s_c, at(32 * (b + 1)))
                    if not start:
                        pe.wait_ge(t["hready"], at(KC * b))
                    for g in range(NG):
                        for k in range(KC):
                            pe.wait_ge(s_ct, at(JC * b if g == 0 else JC * b + KC * (g - 1) + k + 1))
                            for kt in range(g * GT, min(NK, (g + 1) * GT)):
                                r = rows[kt]
                                tr = nc.tensor.transpose(psX[k][:, (kt - g * GT) * P:(kt - g * GT) * P + r],
                                                         cs[0:r, kt, k * P:(k + 1) * P], ident[0:r, 0:r])
                            tr.then_inc(s_turned, 1)

                def values(b, m, r, bias, lhs, rhs):
                    pe.wait_ge(s_vc, at(NV * b if m < 2 else NV * b + m - 1))
                    nc.tensor.matmul(psV[m % 2][0:r, 0:C], ones[0:1, 0:r], bias, start=True, stop=False)
                    for k in range(KC):
                        mm = nc.tensor.matmul(psV[m % 2][0:r, 0:C], lhs(k), rhs(k), start=False, stop=(k == KC - 1))
                    mm.then_inc(s_v, 1)

                def body(b, more):
                    for j in range(JC):
                        g = j // KC
                        pe.wait_ge(s_ct, at(JC * b + KC * (g + 1)))
                        split_tensor(pe, f, b, J, j, gw[g], lambda k: wkv[:, k, (j % KC) * P:(j % KC + 1) * P],
                                     lambda k: cT[:, k, g * GT * P:g * GT * P + gw[g]])
                        for kt in beside(j):
                            values(b, kt, rows[kt], bvc[:, :], lambda k: cT[:, k, kt * P:kt * P + rows[kt]],
                                   lambda k: wkv[:, k, C:2 * C])
                        if j == JC - 3:
                            norm_tensor(pe, t, b)
                    if more:
                        context_transposes(b + 1, False)
                    pe.wait_ge(t["hready"], at(KC * (b + 1)))
                    for j in range(JC, J):
                        i = j - JC
                        split_tensor(pe, f, b, J, j, L, lambda k: wqkv[:, k, i * P:(i + 1) * P],
                                     lambda k: t["hT"][:, k, :])
                        values(b, NK + i, P, bvs[:, :], lambda k: t["hT"][:, k, i * P:(i + 1) * P],
                               lambda k: wqkv[:, k, 2 * C:3 * C])

                pe.wait_ge(s_we, at(96))
                context_transposes(0, True)
                batches(pe, body)
        early.close()

        o = divide_buffers(top)


        def parts_of_minus(pool, s_chain, n0, m, nm, r1, mp):
            for n in range(5):
                pool.wait_ge(s_chain, at(n0 + n))
                if n == 0:
                    pool.sem_inc(s_held, 1)
                    ins = nc.gpsimd.tensor_scalar(nm, m, -1.0, None, ALU.mult)
                elif n == 1:
                    pool.sem_inc(s_held, 1)
                    ins = nc.gpsimd.tensor_copy(mp[0], nm)
                elif n == 2:
                    ins = nc.gpsimd.tensor_tensor(r1, nm, mp[0], ALU.subtract)
                elif n == 3:
                    pool.sem_inc(s_held, 1)
                    ins = nc.gpsimd.tensor_copy(mp[1], r1)
                else:
                    ins = nc.gpsimd.tensor_tensor(mp[2], r1, mp[1], ALU.subtract)
                ins.then_inc(s_chain, 1)

        def set_ones(dve, s_set, Ks, VOs, beside_v):
            for K in Ks:
                nc.vector.memset(K[KROWS:P, :], 1.0).then_inc(s_set, 1)
            for VO in VOs:
                nc.vector.memset(VO, 0.0).then_inc(s_set, 1)
            dve.wait_ge(s_set, at(len(Ks) + len(VOs)))
            for v in beside_v:
                nc.vector.memset(v, 1.0).then_inc(s_set, 1)

        with ExitStack() as s:
            G = 4
            NG = U // G
            LOADS = 3
            NS = 4
            Q = [sbuf(s, f"Q{k}", [P, G * L], BF16) for k in range(NS)]
            K = [sbuf(s, f"K{k}", [P, G * L], BF16) for k in range(NS)]
            V = [sbuf(s, f"V{k}", [P, G, NT * HD]) for k in range(NS)]
            VO = [sbuf(s, f"VO{k}", [P, G * NT, 4 * HD]) for k in range(NS)]
            W = sbuf(s, "W", [P, 2, L])
            OL = [sbuf(s, f"OL{y}", [4 * HD, L]) for y in range(2)]
            mx = [sbuf(s, f"mx{y}", [P, G * NT]) for y in range(2)]
            nm = sbuf(s, "nm", [P, G * NT])
            r1 = sbuf(s, "r1", [P, G * NT])
            mp = [sbuf(s, f"mp{y}", [P, G * NT, PARTS], BF16) for y in range(2)]
            psS = [psum(s, f"psS{y}", [P, L]) for y in range(2)]
            psT = psum(s, "psT", [P, G * L], BF16)
            psB = [psum(s, f"psB{y}", [P, L]) for y in range(2)]
            psO = [psum(s, f"psO{y}", [P, L]) for y in range(2)]
            s_ld = [sem(s, f"s_ld{k}") for k in range(NS)]
            s_st = [sem(s, f"s_st{r}") for r in range(G // 2)]
            (s_set, s_vo, s_sc, s_mx, s_chain, s_mt, s_qb, s_b, s_e, s_pv, s_ol) = (
                sem(s, n) for n in ("s_set", "s_vo", "s_sc", "s_mx", "s_chain", "s_mt", "s_qb", "s_b", "s_e",
                                    "s_pv", "s_ol"))
            block = s.enter_context(nc.Block())

            def groups(eng, body):
                with eng.Fori(0, NG // NS - 1) as i:
                    for k in range(NS):
                        body(NS * i + k, k, i, NS)
                for k in range(NS):
                    body(NG - NS + k, k, NG // NS - 1, NS - 1 - k)

            @block.sync
            def _(sp):
                set_to_one(sp)

                def load(g, k):
                    rows = bass.ds(g * (G * HD), G * HD)
                    for dst, src in ((K[k], ks_d), (Q[k], qs_d)):
                        sp.dma_start(dst[0:KROWS, :].rearrange("r (u l) -> r u l", l=L),
                                     src[rows, :, :].rearrange("(u d) c l -> (d c) u l", d=HD)).then_inc(s_ld[k], 16)
                    sp.dma_start(V[k][:, :, :], vs_d[bass.ds(g * G, G), :, :].rearrange("u p n -> p u n")
                                 ).then_inc(s_ld[k], 16)

                def body(g, k, i, left):
                    for r in range(G // 2):
                        n = g * 2 + r
                        sp.wait_ge(s_ol, at(n + 1))
                        sp.sem_inc(s_held, 1)
                        for z in range(2):
                            sp.dma_start(os_d[z, bass.ds(n * 2 * HD, 2 * HD), :],
                                         OL[r][z * 2 * HD:(z + 1) * 2 * HD, :]).then_inc(s_st[r], 16)
                    if left == NS:
                        load(g + NS, k)
                    if left == NS - 1:
                        for r in range(G // 2):
                            sp.wait_ge(s_st[r], at(32 * (HEADS // G)))
                        divide_sync(sp, o, 0, os_d)

                for k in range(NS):
                    load(k, k)
                groups(sp, body)
                for r in range(G // 2):
                    sp.wait_ge(s_st[r], at(32 * NG))

            @block.gpsimd
            def _(pool):
                def front(g, k, i, left):
                    y = k % 2
                    pool.wait_ge(s_ld[k], at(16 * LOADS * (i + 1)))
                    pool.sem_inc(s_held, 1)
                    for r in range(2):
                        vo = VO[k][:, :, :].rearrange("p (u w) n -> p u w n", w=NT)[:, r:G:2, :, r * HD:(r + 1) * HD]
                        v = V[k][:, r:G:2, :].rearrange("p u (w d) -> p u w d", d=HD)
                        nc.gpsimd.tensor_copy(vo, v).then_inc(s_vo, 1)
                    pool.wait_ge(s_mx, at(G * (g + 1)))
                    parts_of_minus(pool, s_chain, 5 * g, mx[y][:, :], nm[:, :], r1[:, :],
                                   [mp[y][:, :, a] for a in range(PARTS)])

                pool.wait_ge(s_set, at(4 * NS))
                groups(pool, front)

            @block.vector
            def _(dve):
                beside_v = [(VO[k][:, :, :].rearrange("p (u w) n -> p u w n", w=NT)[:, r:G:2, :, :], 2 + r)
                            for k in range(NS) for r in range(2)]
                set_ones(dve, s_set, K, [VO[k][:, :, :] for k in range(NS)],
                         [v[:, :, :, c * HD:(c + 1) * HD] for v, c in beside_v])

                def maxima_into_q(g, k):
                    dve.wait_ge(s_mt, at(g + 1))
                    nc.vector.tensor_copy(Q[k][KROWS:BROWS, :], psT[0:PARTS, :]).then_inc(s_qb, 1)

                def front(g, y):
                    for j in range(G):
                        dve.wait_ge(s_sc, at(G * g + j + 1))
                        nc.vector.tensor_reduce(mx[y][:, j * NT:(j + 1) * NT],
                                                psS[j % 2][:, :].rearrange("p (w k) -> p w k", k=P),
                                                AX_X, ALU.max).then_inc(s_mx, 1)

                def body(g, k, i, left):
                    if left >= 2:
                        front(g + 2, k % 2)
                    if left:
                        maxima_into_q(g + 1, (k + 1) % NS)

                front(0, 0)
                front(1, 1)
                maxima_into_q(0, 0)
                groups(dve, body)
                for k in range(KC):
                    divide_vector(dve, o, 0, k)

            @block.scalar
            def _(act):
                def body(g, k, i, left):
                    for j in range(G):
                        n = g * G + j
                        act.wait_ge(s_pv, at(G * g if j < 2 else n - 1))
                        act.wait_ge(s_b, at(n + 1))
                        nc.scalar.activation(W[:, j % 2, :], psB[j % 2][:, :], ACT.Exp).then_inc(s_e, 1)
                        if j % 2:
                            r = j // 2
                            act.wait_ge(s_pv, at(n + 1))
                            act.wait_ge(s_st[r], at(32 * g))
                            nc.scalar.copy(OL[r][:, :], psO[r][0:4 * HD, :]).then_inc(s_ol, 1)

                groups(act, body)

            @block.tensor
            def _(pe):
                def scores(g, i, y, j):
                    if j == 0:
                        pe.wait_ge(s_ld[y], at(16 * LOADS * (i + 1)))
                    pe.wait_ge(s_mx, at(G * g if j < 2 else G * g + j - 1))
                    for w in range(NT):
                        c = slice(j * L + w * P, j * L + (w + 1) * P)
                        mm = nc.tensor.matmul(psS[j % 2][:, w * P:(w + 1) * P], Q[y][0:KROWS, c], K[y][0:KROWS, c],
                                              start=True, stop=True)
                    mm.then_inc(s_sc, 1)

                def maxima(g, y):
                    pe.wait_ge(s_chain, at(5 * (g + 1)))
                    for w in range(G * NT):
                        tr = nc.tensor.transpose(psT[0:PARTS, w * P:(w + 1) * P], mp[y % 2][:, w, :], identb[:, :])
                    tr.then_inc(s_mt, 1)

                def shifted(g, y, j):
                    if j == 0:
                        pe.wait_ge(s_qb, at(g + 1))
                    n = g * G + j
                    pe.wait_ge(s_e, at(G * g if j < 2 else n - 1))
                    for w in range(NT):
                        c = slice(j * L + w * P, j * L + (w + 1) * P)
                        mm = nc.tensor.matmul(psB[j % 2][:, w * P:(w + 1) * P], K[y][0:BROWS, c], Q[y][0:BROWS, c],
                                              start=True, stop=True)
                    mm.then_inc(s_b, 1)

                def product(g, y, j):
                    n = g * G + j
                    if j == 0:
                        pe.wait_ge(s_vo, at(2 * (g + 1)))
                    if j % 2 == 0:
                        pe.wait_ge(s_ol, at(2 * g))
                    pe.wait_ge(s_e, at(n + 1))
                    for w in range(NT):
                        mm = nc.tensor.matmul(psO[j // 2][0:4 * HD, w * P:(w + 1) * P], VO[y][:, j * NT + w, :],
                                              W[:, j % 2, w * P:(w + 1) * P],
                                              start=(j % 2 == 0 and w == 0), stop=(j % 2 == 1 and w == NT - 1),
                                              skip_group_check=True)
                    mm.then_inc(s_pv, 1)

                def body(g, k, i, left):
                    k2, i2 = (k + 2) % NS, i + (k + 2) // NS
                    for j in range(G):
                        shifted(g, k, j)
                        if left >= 2:
                            scores(g + 2, i2, k2, j)
                        if j >= 1:
                            product(g, k, j - 1)
                    if left:
                        maxima(g + 1, k + 1)
                    product(g, k, G - 1)

                pe.wait_ge(s_set, at(4 * NS))
                for g in range(2):
                    for j in range(G):
                        scores(g, 0, g, j)
                maxima(0, 0)
                groups(pe, body)

        def cross_attention():
            NS = 4
            LOADS = 3
            NW = 4
            assert NS * NK % NW == 0
            NCH = 16
            RUN = -(-LC // NCH)
            LCE = LC + LC % 2
            CROWS = KROWS + 1 + PARTS
            OWN = NT - 1
            FT = 5
            RT = 5
            rows = [min(P, LC - kt * P) for kt in range(NK)]
            with ExitStack() as s:
                Q = [sbuf(s, f"Q{k}", [P, L], BF16) for k in range(NS)]
                K = [sbuf(s, f"K{k}", [P, LC], BF16) for k in range(NS)]
                V = [sbuf(s, f"V{k}", [P, NK, HD]) for k in range(NS)]
                VO = [sbuf(s, f"VO{k}", [P, NK, 2 * HD]) for k in range(NS)]
                W = sbuf(s, "W", [P, NW, L])
                OL = [sbuf(s, f"OL{y}", [P, L]) for y in range(2)]
                cands = [sbuf(s, f"cand{w}", [P, NCH, 8]) for w in range(NT)]
                cand2 = sbuf(s, "cand2", [P, NCH, 8])
                reach = sbuf(s, "reach", [P, NCH, 8])
                reach8 = sbuf(s, "reach8", [P, NCH])
                top8 = [sbuf(s, f"top8_{r}", [P, NT, 8]) for r in range(2)]
                next8 = [sbuf(s, f"next8_{r}", [P, NT, 8]) for r in range(2)]
                cnt = [sbuf(s, f"cnt{r}", [P, NT, 2]) for r in range(2)]
                both = sbuf(s, "both", [P, NT])
                half = sbuf(s, "half", [P, 2])
                most = sbuf(s, "most", [1, 1], mybir.dt.int32)
                redo8 = sbuf(s, "redo8", [P, 8])
                nm = sbuf(s, "nm", [P, NT])
                r1 = sbuf(s, "r1", [P, NT])
                mp = [sbuf(s, f"mp{r}", [P, NT, 1 + PARTS], BF16) for r in range(2)]
                S = [[sbuf(s, f"S{r}_{w}", [P, LCE]) for w in range(NT)] for r in range(2)]
                M = sbuf(s, "M", [P, LC])
                N = [[sbuf(s, f"N{r}_{w}", [P, LCE], BF16) for w in range(NT)] for r in range(2)]
                psS = psum(s, "psS", [P, 4 * 512])
                psT = psum(s, "psT", [P, 1024], BF16)
                psB = [psum(s, f"psB{k}", [P, 512]) for k in range(2)]
                psO = psum(s, "psO", [P, 512])
                s_ld = [sem(s, f"s_ld{k}") for k in range(NS)]
                s_st = [sem(s, f"s_st{y}") for y in range(2)]
                (s_set, s_vo, s_sc, s_ev, s_pick, s_own, s_runs, s_top, s_most, s_ok, s_redo,
                 s_chain, s_mt, s_qb, s_b, s_e, s_pv,
                 s_ol) = (sem(s, n) for n in (
                     "s_set", "s_vo", "s_sc", "s_ev", "s_pick", "s_own", "s_runs", "s_top", "s_most",
                     "s_ok", "s_redo", "s_chain", "s_mt",
                     "s_qb", "s_b", "s_e", "s_pv", "s_ol"))
                block = s.enter_context(nc.Block())

                def quarter(w):
                    return range(w * NK // NT, (w + 1) * NK // NT)

                def steps(eng, step):
                    with eng.Fori(0, U // NS - 1) as i:
                        for k in range(NS):
                            step(NS * i + k, k, i, NS)
                    for k in range(NS):
                        step(U - NS + k, k, U // NS - 1, NS - 1 - k)

                def after(k, i, n):
                    return (k + n) % NS, i + (k + n) // NS

                @block.sync
                def _(sp):
                    set_to_one(sp)

                    def load(u, k):
                        for dst, src in ((K[k], kc_d), (Q[k], qc_d)):
                            sp.dma_start(dst[0:KROWS, :],
                                         src[bass.ds(u * HD, HD), :, :].rearrange("d c l -> (d c) l")
                                         ).then_inc(s_ld[k], 16)
                        sp.dma_start(V[k][:, :, :], vc_d[bass.ds(u, 1), :, :].rearrange("o p n -> p (o n)")
                                     .rearrange("p (t d) -> p t d", d=HD)).then_inc(s_ld[k], 16)

                    def store(n, y):
                        sp.wait_ge(s_ol, at(n + 1))
                        sp.sem_inc(s_held, 1)
                        for r in range(2):
                            sp.dma_start(oc_d[:, :, bass.ds((2 * n + r) * HD, HD), :],
                                         OL[y][r * 4 * HD:(r + 1) * 4 * HD, :]).then_inc(s_st[y], 16)

                    def step(u, k, i, left):
                        sp.wait_ge(s_pv, at(NK * (u + 1)))
                        sp.sem_inc(s_held, 1)
                        if left == NS:
                            load(u + NS, k)
                        if k % 2:
                            store(2 * i + k // 2, k // 2)
                        if left == NS - 1:
                            for y in range(2):
                                sp.wait_ge(s_st[y], at(32 * (HEADS // NS)))
                            fetch_both(sp, 0)

                    for k in range(NS):
                        load(k, k)
                    sp.dma_start(wco[:, :, :], w_co.rearrange("(k p) n -> p k n", p=P)).then_inc(s_wl, 16)
                    sp.dma_start(bco[:, :], row(b_co)).then_inc(s_wl, 16)
                    sp.dma_start(bm2[:, :], row(b_m2)).then_inc(s_wl, 16)
                    sp.dma_start(bm1[:, :], column(b_m1), allow_slow_non_contiguous=True).then_inc(s_wl, 16)
                    sp.dma_start(wm1[:, :, :], w_m1.rearrange("(k p) n -> p k n", p=P)).then_inc(s_wl, 16)
                    sp.dma_start(wm2[:, :, :], w_m2.rearrange("(k p) n -> p k n", p=P)).then_inc(s_wl, 16)
                    steps(sp, step)
                    for y in range(2):
                        sp.wait_ge(s_st[y], at(32 * PAIRS // 2))

                @block.gpsimd
                def _(pool):
                    def marks(u, r, w):
                        pool.wait_ge(s_top, at(FT * (NT * u + w) + 3))
                        pool.sem_inc(s_held, 1)
                        nc.gpsimd.tensor_scalar(N[r][w][:, :], S[r][w][:, :], next8[r][:, w, 7:8], None,
                                                ALU.is_lt).then_inc(s_pick, 1)

                    def values(u, k, i):
                        pool.wait_ge(s_ld[k], at(16 * LOADS * (i + 1)))
                        pool.sem_inc(s_held, 1)
                        nc.gpsimd.tensor_copy(VO[k][:, :, 0:HD], V[k][:, :, :]
                                              ).then_inc(s_vo, 1)

                    def front(u, k):
                        r = k % 2
                        for w in range(OWN - 1):
                            marks(u, r, w)
                        pool.wait_ge(s_top, at(FT * NT * (u + 1)))
                        pool.sem_inc(s_held, 1)
                        nc.gpsimd.tensor_tensor(both[:, :], cnt[r][:, :, 0], cnt[r][:, :, 1], ALU.add
                                                ).then_inc(s_chain, 1)
                        pool.wait_ge(s_chain, at(8 * u + 1))
                        nc.gpsimd.tensor_tensor(half[:, :], both[:, 0:2], both[:, 2:4], ALU.add).then_inc(s_chain, 1)
                        pool.wait_ge(s_chain, at(8 * u + 2))
                        nc.gpsimd.tensor_tensor(mp[r][:, 0, 0:1], half[:, 0:1], half[:, 1:2], ALU.add
                                                ).then_inc(s_chain, 1)
                        parts_of_minus(pool, s_chain, 8 * u + 3, top8[r][:, :, 0], nm[:, :], r1[:, :],
                                       [mp[r][:, :, 1 + a] for a in range(PARTS)])
                        marks(u, r, OWN - 1)

                    for r in range(2):
                        nc.gpsimd.memset(mp[r][:, :, :], 0.0)
                    pool.wait_ge(s_set, at(4 * NS + 2 * NT))
                    for k in range(2):
                        values(k, k, 0)
                        front(k, k)
                    with pool.Fori(0, U // NS - 1) as i:
                        for k in range(NS):
                            k2, i2 = after(k, i, 2)
                            values(NS * i + k + 2, k2, i2)
                            pool.wait_ge(s_b, at(NK * (NS * i + k + 1)))
                            pool.sem_inc(s_held, 1)
                            front(NS * i + k + 2, k2)
                    for k in range(NS - 2):
                        values(U - NS + k + 2, k + 2, U // NS - 1)
                        pool.wait_ge(s_b, at(NK * (U - NS + k + 1)))
                        front(U - NS + k + 2, k + 2)
                    add_parts(pool, 0)

                @block.vector
                def _(dve):
                    set_ones(dve, s_set, K, [VO[k][:, :, :] for k in range(NS)],
                             [VO[k][:, :, HD:2 * HD] for k in range(NS)])
                    for k in range(NS):
                        nc.vector.memset(K[k][KROWS:KROWS + 1, :], 0.0).then_inc(s_set, 1)
                    for r in range(2):
                        for w in range(NT):
                            nc.vector.memset(S[r][w][:, LC - 1:LCE], LOWEST).then_inc(s_set, 1)

                    def runs(u, r, w, part, start):
                        n = NT * u + w
                        if part == 0:
                            if not start:
                                dve.wait_ge(s_top, at(FT * (n - NT + 1)))
                                dve.sem_inc(s_held, 1)
                            dve.wait_ge(s_ev, at(n + 1))
                            dve.sem_inc(s_held, 1)
                        for c in range(part * NCH // NT, (part + 1) * NCH // NT):
                            run = nc.vector.max(cands[w][:, c, :], S[r][w][:, c * RUN:min(LC, (c + 1) * RUN)])
                        if part == NT - 1:
                            run.then_inc(s_runs, 1)

                    def choice(u, r, w, part):
                        n = NT * u + w
                        a, b = top8[r][:, w, :], next8[r][:, w, :]
                        flat, flat2 = (t[:, :, :].rearrange("p c e -> p (c e)") for t in (cands[w], cand2))
                        if part == 0:
                            dve.wait_ge(s_runs, at(n + 1))
                            dve.sem_inc(s_held, 1)
                            nc.vector.max(a, flat).then_inc(s_top, 1)
                        elif part == 1:
                            dve.wait_ge(s_top, at(FT * n + 1))
                            dve.sem_inc(s_held, 1)
                            nc.vector.match_replace(flat2, a, flat, LOWEST).then_inc(s_top, 1)
                        elif part == 2:
                            dve.wait_ge(s_top, at(FT * n + 2))
                            dve.sem_inc(s_held, 1)
                            nc.vector.max(b, flat2).then_inc(s_top, 1)
                        else:
                            dve.wait_ge(s_top, at(FT * n + 3))
                            dve.sem_inc(s_held, 1)
                            nc.vector.tensor_scalar(reach[:, :, :], cands[w][:, :, :], b[:, 7:8], 0.0, ALU.is_ge,
                                                    ALU.add, accum_out=cnt[r][:, w, 0:1]).then_inc(s_top, 1)
                            nc.vector.tensor_scalar(reach8[:, :], cands[w][:, :, 7], b[:, 7:8], 0.0, ALU.is_ge,
                                                    ALU.add, accum_out=cnt[r][:, w, 1:2]).then_inc(s_top, 1)
                            if w == OWN:
                                nc.vector.tensor_scalar(N[r][w][:, :], S[r][w][:, :], b[:, 7:8], None,
                                                        ALU.is_lt).then_inc(s_own, 1)

                    def marks_anew(u, r):
                        for w in range(NT):
                            for n in range(RT):
                                if w or n:
                                    dve.wait_ge(s_redo, at(RT * (NT * u + w) + n))
                                    dve.sem_inc(s_held, 1)
                                src = S[r][w][:, 0:LC] if n < 2 else M[:, :]
                                if n == 4:
                                    ins = nc.vector.tensor_scalar(N[r][w][:, 0:LC], M[:, :], LOWEST, None, ALU.is_gt)
                                elif n % 2 == 0:
                                    ins = nc.vector.max(redo8[:, :], src)
                                else:
                                    ins = nc.vector.match_replace(M[:, :], redo8[:, :], src, LOWEST)
                                ins.then_inc(s_redo, 1)

                    def count(u, k):
                        dve.wait_ge(s_qb, at(u + 1))
                        nc.vector.tensor_reduce(most[:, :], Q[k][KROWS:KROWS + 1, 0:P], AX_X, ALU.max
                                                ).then_inc(s_most, 1)

                    def check(u, k):
                        dve.wait_ge(s_most, at(u + 1))
                        dve.sem_inc(s_held, 1)
                        largest = dve.value_load(most[0:1, 0:1])
                        with dve.If(largest != TOPK * NT):
                            dve.wait_ge(s_pick, at(OWN * (u + 1)))
                            dve.wait_ge(s_own, at(u + 1))
                            dve.sem_inc(s_held, 1)
                            marks_anew(u, k % 2)
                        with dve.Else():
                            dve.sem_inc(s_redo, RT * NT)
                        dve.wait_ge(s_redo, at(RT * NT * (u + 1)))
                        dve.sem_inc(s_ok, 1)

                    def step(u, k, i, left):
                        r, r1 = k % 2, (k + 1) % 2
                        if not left:
                            for part in range(NT):
                                choice(u, r, NT - 1, part)
                            count(u, k)
                            check(u, k)
                            return
                        for w in range(NT):
                            for part in range(NT):
                                runs(u + 1, r1, w, part, False)
                                if w == 2 and part == 1:
                                    check(u, k)
                                if w == 0:
                                    choice(u, r, NT - 1, part)
                                else:
                                    choice(u + 1, r1, w - 1, part)
                            if w == 1:
                                count(u, k)

                    for w in range(NT):
                        for part in range(NT):
                            runs(0, 0, w, part, True)
                            if w:
                                choice(0, 0, w - 1, part)
                    steps(dve, step)
                    for k in range(KC):
                        divide_vector(dve, o, B, k)

                @block.scalar
                def _(act):
                    def copy_scores(u, r, w):
                        act.wait_ge(s_sc, at(NT * u + w + 1))
                        nc.scalar.copy(S[r][w][:, 0:LC], psS[:, 0:LC]).then_inc(s_ev, 1)

                    def exps(u, k, tiles):
                        for kt in tiles:
                            act.wait_ge(s_pv, at(NK * u if k == 0 and kt < NW else NK * u + kt - NW + 1))
                            act.wait_ge(s_b, at(NK * u + kt + 1))
                            nc.scalar.activation(W[0:rows[kt], (k * NK + kt) % NW, :], psB[kt % 2][0:rows[kt], :],
                                                 ACT.Exp).then_inc(s_e, 1)

                    def rows_into_q(u, k):
                        act.wait_ge(s_mt, at(u + 1))
                        nc.scalar.copy(Q[k][KROWS:CROWS, :], psT[0:1 + PARTS, 0:L]).then_inc(s_qb, 1)

                    def step(u, k, i, left):
                        for w in range(NT):
                            exps(u, k, quarter(w))
                            if left >= 2:
                                if w == 0:
                                    act.wait_ge(s_ok, at(u + 1))
                                    act.wait_ge(s_pick, at(OWN * (u + 1)))
                                copy_scores(u + 2, k % 2, w)
                            if w == 2 and left:
                                rows_into_q(u + 1, (k + 1) % NS)
                        if k % 2:
                            y = k // 2
                            act.wait_ge(s_pv, at(NK * (u + 1)))
                            act.wait_ge(s_st[y], at(32 * i))
                            nc.scalar.copy(OL[y][:, :], psO[:, :]).then_inc(s_ol, 1)

                    act.wait_ge(s_set, at(4 * NS + 2 * NT))
                    for u in range(2):
                        for w in range(NT):
                            copy_scores(u, u, w)
                    rows_into_q(0, 0)
                    steps(act, step)

                @block.tensor
                def _(pe):
                    def scores(u, w, k, i):
                        if w == 0:
                            pe.wait_ge(s_ld[k], at(16 * LOADS * (i + 1)))
                        pe.wait_ge(s_ev, at(NT * u + w))
                        for c in range(0, LC, 512):
                            n = min(512, LC - c)
                            mm = nc.tensor.matmul(psS[:, c:c + n], Q[k][0:KROWS, w * P:(w + 1) * P],
                                                  K[k][0:KROWS, c:c + n], start=True, stop=True)
                        mm.then_inc(s_sc, 1)

                    def maxima(u, r):
                        pe.wait_ge(s_chain, at(8 * (u + 1)))
                        for w in range(NT):
                            tr = nc.tensor.transpose(psT[0:1 + PARTS, w * P:(w + 1) * P], mp[r][:, w, :],
                                                     identb[:, :])
                        tr.then_inc(s_mt, 1)

                    def shifted(u, k, kt):
                        r, m = k % 2, rows[kt]
                        pe.wait_ge(s_e, at(NK * u if kt < 2 else NK * u + kt - 1))
                        nc.tensor.matmul(psB[kt % 2][0:m, :], K[k][0:CROWS, kt * P:kt * P + m], Q[k][0:CROWS, :],
                                         start=True, stop=True)
                        for w in range(NT):
                            mm = nc.tensor.matmul(psB[kt % 2][0:m, w * P:(w + 1) * P], N[r][w][:, kt * P:kt * P + m],
                                                  negbig[:, :], start=False, stop=True,
                                                  skip_group_check=True)
                        mm.then_inc(s_b, 1)

                    def product(u, k, kt):
                        r, m = k % 2, rows[kt]
                        pe.wait_ge(s_e, at(NK * u + kt + 1))
                        c = (2 * r + kt % 2) * 2 * HD
                        nc.tensor.matmul(psO[c:c + 2 * HD, :], VO[k][0:m, kt, :], W[0:m, (k * NK + kt) % NW, :],
                                         start=(kt < 2), stop=(kt >= NK - 2), skip_group_check=True,
                                         tile_position=(0, c)).then_inc(s_pv, 1)

                    def back(u, k, i, w, left):
                        k2, i2 = after(k, i, 2)
                        for kt in quarter(w):
                            shifted(u, k, kt)
                            if kt == quarter(w)[-1] and left >= 2:
                                scores(u + 2, w, k2, i2)
                            if kt == 3:
                                pe.wait_ge(s_vo, at(u + 1))
                                if k % 2 == 0:
                                    pe.wait_ge(s_ol, at(2 * i + k // 2))
                            if kt >= 3 and kt % 2:
                                product(u, k, kt - 3)
                                product(u, k, kt - 2)

                    def step(u, k, i, left):
                        pe.wait_ge(s_ok, at(u + 1))
                        pe.wait_ge(s_pick, at(OWN * (u + 1)))
                        for w in range(NT):
                            back(u, k, i, w, left)
                            if w == 2 and left:
                                maxima(u + 1, (k + 1) % 2)
                        for kt in range(NK // 2 * 2 - 2, NK):
                            product(u, k, kt)

                    pe.wait_ge(s_set, at(4 * NS + 2 * NT))
                    for u in range(2):
                        for w in range(NT):
                            scores(u, w, u, 0)
                    maxima(0, 0)
                    steps(pe, step)

        with ExitStack() as s:
            t = norm_buffers(s)
            f = split_buffers(s)
            a = add_buffers(s)
            wso = sbuf(s, "wso", [P, KC, C])
            bso = sbuf(s, "bso", [1, C])
            wq = sbuf(s, "wq", [P, KC, C])
            bq = sbuf(s, "bq", [P, KC])
            bqs = sbuf(s, "bqs", [P, KC])
            s_w, s_bs = (sem(s, n) for n in ("s_w", "s_bs"))
            J = KC
            block = s.enter_context(nc.Block())

            @block.sync
            def _(sp):
                set_to_one(sp)
                sp.sem_inc(s_begun, 1)
                sp.dma_start(wso[:, :, :], w_so.rearrange("(k p) n -> p k n", p=P)).then_inc(s_w, 16)
                sp.dma_start(bso[:, :], row(b_so)).then_inc(s_w, 16)
                sp.dma_start(wq[:, :, :], w_q.rearrange("(k p) n -> p k n", p=P)).then_inc(s_w, 16)
                sp.dma_start(bq[:, :], column(b_q), allow_slow_non_contiguous=True).then_inc(s_w, 16)
                divide_sync(sp, o, 1, os_d)
                with sp.Fori(0, B - 2) as b:
                    divide_sync(sp, o, b + 2, os_d)
                    for j in range(J):
                        split_sync(sp, f, b, J, j, L, qc_d, j, 0, True)
                for b in range(B - 2, B):
                    for j in range(J):
                        split_sync(sp, f, b, J, j, L, qc_d, j, 0, True)
                for k in range(2):
                    sp.wait_ge(f["parted"][k], at(16 * PARTS * B * J // 2))

            @block.gpsimd
            def _(pool):
                pool.wait_ge(s_begun, 2)
                norm_pool(pool, t, 0)
                with pool.Fori(0, B - 1) as b:
                    for j in range(J):
                        split_pool(pool, f, b, J, j, L, True)
                    norm_pool(pool, t, b + 1)
                for j in range(J):
                    split_pool(pool, f, B - 1, J, j, L, True)

            @block.vector
            def _(dve):
                dve.wait_ge(s_begun, 2)
                dve.wait_ge(s_w, at(64))
                nc.vector.tensor_scalar(bqs[:, :], bq[:, :], QSCALE, None, ALU.mult).then_inc(s_bs, 1)

                def residual(b, start):
                    for w in range(NT):
                        add_vector(dve, a, NT * b + w, w % 2, b, w, 0, start and w < 2)
                    norm_vector(dve, t, b, a["added"], NT * b)

                residual(0, True)
                with dve.Fori(0, B - 1) as b:
                    for k in range(KC):
                        divide_vector(dve, o, b + 1, k)
                    for j in range(J):
                        split_vector(dve, f, b, J, j, L, True)
                    residual(b + 1, False)
                for j in range(J):
                    split_vector(dve, f, B - 1, J, j, L, True)

            @block.scalar
            def _(act):
                act.wait_ge(s_begun, 2)
                act.wait_ge(s_bs, at(1))
                norm_scalar(act, t, 0, 1, f["prod"], J)
                with act.Fori(0, B - 1) as b:
                    for j in range(J):
                        split_scalar(act, f, b, J, j, L, bqs[:, j:j + 1], QSCALE)
                    norm_scalar(act, t, b + 1, 1, f["prod"], J)
                for j in range(J):
                    split_scalar(act, f, B - 1, J, j, L, bqs[:, j:j + 1], QSCALE)

            @block.tensor
            def _(pe):
                pe.wait_ge(s_begun, 2)
                pe.wait_ge(s_w, at(64))

                def output(b, start):
                    pe.wait_ge(o["divided"], at(b + 1))
                    for w in range(NT):
                        add_tensor(pe, a, NT * b + w, w % 2, bso[:, :], lambda k: o["oT"][:, k, w * P:(w + 1) * P],
                                   lambda k: wso[:, k, :], KC, start and w < 2)

                def queries(b):
                    pe.wait_ge(t["hready"], at(KC * (b + 1)))
                    for j in range(J):
                        split_tensor(pe, f, b, J, j, L, lambda k: wq[:, k, j * P:(j + 1) * P],
                                     lambda k: t["hT"][:, k, :])

                output(0, True)
                norm_tensor(pe, t, 0)
                with pe.Fori(0, B - 1) as b:
                    queries(b)
                    output(b + 1, False)
                    norm_tensor(pe, t, b + 1)
                queries(B - 1)

        wco = sbuf(top, "wco", [P, KC, C])
        bco = sbuf(top, "bco", [1, C])
        wm1 = sbuf(top, "wm1", [P, KC, 2 * HID])
        bm1 = sbuf(top, "bm1", [P, 2 * HC])
        wm2 = sbuf(top, "wm2", [P, HC, C])
        bm2 = sbuf(top, "bm2", [1, C])
        s_wl = sem(top, "s_wl")
        odd = [sbuf(top, f"odd{z}", [P, KC, L]) for z in range(2)]
        s_odd = sem(top, "s_odd")

        def fetch_both(sp, b):
            sp.wait_ge(o["divided"], at(B + b))
            sp.sem_inc(s_held, 1)
            for z in range(2):
                for a, dst in enumerate(((o["oU"], o["oL"])[z], odd[z])):
                    sp.dma_start(dst[:, :, :], oc_d[a, z, bass.ds(b * C, C), :]
                                 .rearrange("(k p) l -> p k l", p=P)).then_inc(s_odd, 16)

        def add_parts(pool, b):
            pool.wait_ge(s_odd, at(16 * 4 * (b + 1)))
            pool.sem_inc(s_held, 1)
            for even, z in ((o["oU"], 0), (o["oL"], 1)):
                nc.gpsimd.tensor_tensor(even[:, :, :], even[:, :, :], odd[z][:, :, :], ALU.add
                                        ).then_inc(o["fetched"], 16)

        cross_attention()

        with ExitStack() as s:
            t = norm_buffers(s)
            a = add_buffers(s)
            SA = [sbuf(s, f"SA{k}", [P, L]) for k in range(2)]
            uT = sbuf(s, "uT", [P, HC, L])
            psA = [psum(s, f"psA{k}", [P, L]) for k in range(2)]
            psU = [psum(s, f"psU{k}", [P, L]) for k in range(2)]
            s_u, s_sa, s_gl, s_out = (sem(s, n) for n in ("s_u", "s_sa", "s_gl", "s_out"))
            H = HC // 2
            J = 2 * NT
            block = s.enter_context(nc.Block())

            @block.sync
            def _(sp):
                set_to_one(sp)
                sp.sem_inc(s_begun, 1)
                def store(b, n):
                    sp.wait_ge(a["added"], at(n))
                    sp.sem_inc(s_held, 1)
                    ob = out[bass.ds(b, 1), :, :].rearrange("o l c -> (o l) c")
                    sp.dma_start(ob[SHIFT:L - SHIFT, :].rearrange("(t p) c -> p t c", p=P),
                                 xs[:, bass.ds(b, 1), 0:NT - 1, :].rearrange("p o t c -> p (o t) c")).then_inc(s_out, 16)
                    sp.dma_start(ob[L - SHIFT:L, :],
                                 xs[0:SHIFT, bass.ds(b, 1), NT - 1, :].rearrange("p o c -> p (o c)")).then_inc(s_out, 16)
                    sp.dma_start(ob[0:SHIFT, :],
                                 xs[SHIFT:P, bass.ds(b, 1), NT - 1, :].rearrange("p o c -> p (o c)")).then_inc(s_out, 16)

                fetch_both(sp, 1)
                with sp.Fori(0, B - 2) as b:
                    fetch_both(sp, b + 2)
                    store(b, J * (b + 1) + NT)
                store(B - 2, J * (B - 1) + NT)
                store(B - 1, J * B)
                sp.wait_ge(s_out, at(48 * B))

            @block.gpsimd
            def _(pool):
                pool.wait_ge(s_begun, 3)
                norm_pool(pool, t, 0)
                with pool.Fori(1, B) as b:
                    add_parts(pool, b)
                    norm_pool(pool, t, b)

            @block.vector
            def _(dve):
                dve.wait_ge(s_begun, 3)
                def residual(b, n, start):
                    for w in range(NT):
                        add_vector(dve, a, n + w, w % 2, b, w, 1, start and w < 2)
                    norm_vector(dve, t, b, a["added"], n)

                def glu(b, j):
                    n = HC * b + j
                    dve.wait_ge(s_sa, at(n + 1))
                    nc.vector.scalar_tensor_tensor(out=uT[:, j, :], in0=psU[j % 2][:, :],
                                                   scalar=bm1[:, HC + j:HC + j + 1], in1=SA[j % 2][:, :],
                                                   op0=ALU.add, op1=ALU.mult).then_inc(s_gl, 1)

                def body(b, more):
                    for j in range(H):
                        if more and j < KC:
                            divide_vector(dve, o, B + b + 1, j)
                        glu(b, j)
                    n = J * b + NT
                    if more:
                        residual(b + 1, n, False)
                        n = n + NT
                    for j in range(H, HC):
                        glu(b, j)
                    for w in range(NT):
                        add_vector(dve, a, n + w, w % 2, b, w, 2)

                dve.wait_ge(s_wl, at(96))
                residual(0, 0, True)
                with dve.Fori(0, B - 1) as b:
                    body(b, True)
                body(B - 1, False)

            @block.scalar
            def _(act):
                act.wait_ge(s_begun, 3)
                def gates(b):
                    for j in range(HC):
                        n = HC * b + j
                        act.wait_ge(s_u, at(n + 1))
                        act.wait_ge(s_gl, at(HC * b if j < 2 else n - 1))
                        nc.scalar.activation(SA[j % 2][:, :], psA[j % 2][:, :], ACT.Silu, bias=bm1[:, j:j + 1]
                                             ).then_inc(s_sa, 1)

                act.wait_ge(s_wl, at(96))
                norm_scalar(act, t, 0, 2, s_u, HC)
                with act.Fori(0, B - 1) as b:
                    gates(b)
                    norm_scalar(act, t, b + 1, 2, s_u, HC)
                gates(B - 1)

            @block.tensor
            def _(pe):
                pe.wait_ge(s_begun, 3)
                def output(b, n, start):
                    pe.wait_ge(o["divided"], at(B + b + 1))
                    for w in range(NT):
                        add_tensor(pe, a, n + w, w % 2, bco[:, :], lambda k: o["oT"][:, k, w * P:(w + 1) * P],
                                   lambda k: wco[:, k, :], KC, start and w < 2)

                def up(b, j):
                    pe.wait_ge(s_gl, at(HC * b if j < 2 else HC * b + j - 1))
                    for ps, c in ((psA, j * P), (psU, HID + j * P)):
                        for k in range(KC):
                            mm = nc.tensor.matmul(ps[j % 2][:, :], wm1[:, k, c:c + P], t["hT"][:, k, :],
                                                  start=(k == 0), stop=(k == KC - 1))
                    mm.then_inc(s_u, 1)

                def body(b, more):
                    pe.wait_ge(t["hready"], at(KC * (b + 1)))
                    for j in range(H):
                        up(b, j)
                    n = J * b + NT
                    if more:
                        output(b + 1, n, False)
                        n = n + NT
                    for j in range(H, HC):
                        up(b, j)
                    if more:
                        norm_tensor(pe, t, b + 1)
                    pe.wait_ge(s_gl, at(HC * (b + 1)))
                    for w in range(NT):
                        add_tensor(pe, a, n + w, w % 2, bm2[:, :], lambda k: uT[:, k, w * P:(w + 1) * P],
                                   lambda k: wm2[:, k, :], HC)

                pe.wait_ge(s_wl, at(96))
                output(0, 0, True)
                norm_tensor(pe, t, 0)
                with pe.Fori(0, B - 1) as b:
                    body(b, True)
                body(B - 1, False)


_INS = ['x', 'cond_1024', 'ctx_1024', 'L0_xcond_w_ada', 'L0_xcond_b_ada', 'L0_xcond_w_qkv', 'L0_xcond_b_qkv',
        'L0_xcond_w_so', 'L0_xcond_b_so', 'L0_xcond_w_q', 'L0_xcond_b_q', 'L0_xcond_w_kv', 'L0_xcond_b_kv',
        'L0_xcond_w_co', 'L0_xcond_b_co', 'L0_xcond_w_m1', 'L0_xcond_b_m1', 'L0_xcond_w_m2', 'L0_xcond_b_m2']


def kernel(**inputs):
    import numpy as _np
    import concourse.bacc as _bacc
    from concourse import mybir as _mybir
    from concourse.bass_utils import run_bass_kernel_spmd as _run

    nc = _bacc.Bacc("TRN2", target_bir_lowering=False, num_devices=1)
    arrays, args = {}, []
    for name in _INS:
        a = _np.ascontiguousarray(inputs[name])
        arrays[f"in_{name}_dram"] = a
        args.append(nc.dram_tensor(f"in_{name}_dram", a.shape, _mybir.dt.from_np(a.dtype), kind="ExternalInput").ap())
    shape = inputs['x'].shape
    args.append(nc.dram_tensor("out_0_dram", shape, _mybir.dt.from_np(_np.dtype("float32")), kind="ExternalOutput").ap())
    build(nc, *args)
    r = _run(nc, [arrays], core_ids=[0])
    return r.results[0]["out_0_dram"]
```
